# Optimizing a Trainium2 kernel written in Bass

```python
import numpy as np
import jax
import jax.numpy as jnp

def _softmax(x, axis=-1):
    return jax.nn.softmax(x, axis=axis)

def _gelu(x):
    return jax.nn.gelu(x, approximate=True)

def _silu(x):
    return jax.nn.silu(x)

def _sigmoid(x):
    return jax.nn.sigmoid(x)

def _layernorm(x, axis=-1, eps=1e-05):
    m = jnp.mean(x, axis=axis, keepdims=True)
    v = jnp.var(x, axis=axis, keepdims=True)
    return (x - m) / jnp.sqrt(v + eps)

def _scatter_add(tgt, idx, src, axis=0):
    return tgt.at[idx].add(src)

def _segment_sum(src, seg, n):
    return jax.ops.segment_sum(src, seg, n)
kernel_name = 'mk_decoder_preln_d4_seqx_r8_a793e3'

def setup_inputs(seed: int=0):
    np.random.seed(seed)
    _w = jnp.asarray

    def _rec_inputs():
        import jax
        import jax.numpy as jnp
        _rk = jax.random.key(seed)
        x = -0.0002928 + 1 * jax.random.normal(jax.random.fold_in(_rk, 1), (8, 128, 128), jnp.float32)
        _lenS = 128 - jax.random.randint(jax.random.fold_in(_rk, 7), (8,), 0, max(1, 128 // 4) + 1, jnp.int32)
        _lenS2 = 128 - jax.random.randint(jax.random.fold_in(_rk, 8), (8,), 0, max(1, 128 // 4) + 1, jnp.int32)
        _ctx_1024P = jax.random.normal(jax.random.fold_in(_rk, 11), (8, 16, 128), jnp.float32)
        _ctx_1024c = jax.random.dirichlet(jax.random.fold_in(_rk, 511), 0.3 * jnp.ones((16,), jnp.float32), (8, 128))
        _ctx_1024t = jnp.einsum('bsk,bkd->bsd', _ctx_1024c, _ctx_1024P)
        _ctx_1024t = _ctx_1024t * jax.lax.rsqrt(jnp.mean(jnp.square(_ctx_1024t)) + 1e-12) * 0.953939
        ctx_1024 = -1.39393e-06 + 0.999914 * (_ctx_1024t + 0.3 * jax.random.normal(jax.random.fold_in(_rk, 611), (8, 128, 128), jnp.float32))
        _validS = jnp.arange(128)[None, :] < _lenS[:, None]
        _validS2 = jnp.arange(128)[None, :] < _lenS2[:, None]
        _causal = jnp.tril(jnp.ones((128, 128), dtype=bool))
        mask_BxS2_bf0 = jnp.logical_not(jnp.ones((8, 128), dtype=bool))
        return (x, ctx_1024, mask_BxS2_bf0)
    x, ctx_1024, mask_BxS2_bf0 = _rec_inputs()

    def _L0_attn_setup():
        import jax, jax.numpy as jnp
        import numpy as np
        H = 16
        G = 16
        R = 4
        WIN = 64
        NEG = -1000000000.0
        key = jax.random.key(seed)
        ks = jax.random.split(key, 9)
        dm, D = (128, 128 // H)
        s = 0.02
        return {'x': jax.random.normal(ks[0], (1, 256, dm), dtype=jnp.float32), 'Wq': jax.random.normal(ks[1], (dm, dm), dtype=jnp.float32) * s, 'Wk': jax.random.normal(ks[2], (dm, dm), dtype=jnp.float32) * s, 'Wv': jax.random.normal(ks[3], (dm, dm), dtype=jnp.float32) * s, 'Wo': jax.random.normal(ks[4], (dm, dm), dtype=jnp.float32) * s, 'Wck': jax.random.normal(ks[5], (G * D, D), dtype=jnp.float32) * s, 'Wcv': jax.random.normal(ks[6], (G * D, D), dtype=jnp.float32) * s, 'Wg': jax.random.normal(ks[7], (D, 3), dtype=jnp.float32) * s, 'bg': jnp.zeros((3,), dtype=jnp.float32)}
    _L0_attn_all = _L0_attn_setup()
    _L0_attn_in = {k: v for k, v in _L0_attn_all.items() if k in ('Wq', 'Wk', 'Wv', 'Wo', 'Wck', 'Wcv', 'Wg', 'bg')}
    del _L0_attn_all

    def _L0_xattn_setup():
        import jax, jax.numpy as jnp
        import numpy as np
        D_MODEL = 128
        NUM_HEADS = 16
        D_K = D_MODEL // NUM_HEADS

        def _split_heads(x):
            B, S, _ = x.shape
            return x.reshape(B, S, NUM_HEADS, D_K).transpose(0, 2, 1, 3)
        key = jax.random.key(seed)
        ks = jax.random.split(key, 7)
        B, S = (2, 256)
        scale = 1.0 / np.sqrt(D_MODEL)
        return {'q': jax.random.normal(ks[0], (B, S, D_MODEL), jnp.float32), 'k': jax.random.normal(ks[1], (B, S, D_MODEL), jnp.float32), 'v': jax.random.normal(ks[2], (B, S, D_MODEL), jnp.float32), 'Wq': jax.random.normal(ks[3], (D_MODEL, D_MODEL), jnp.float32) * scale, 'Wk': jax.random.normal(ks[4], (D_MODEL, D_MODEL), jnp.float32) * scale, 'Wv': jax.random.normal(ks[5], (D_MODEL, D_MODEL), jnp.float32) * scale, 'Wo': jax.random.normal(ks[6], (D_MODEL, D_MODEL), jnp.float32) * scale}
    _L0_xattn_all = _L0_xattn_setup()
    _L0_xattn_in = {k: v for k, v in _L0_xattn_all.items() if k in ('Wq', 'Wk', 'Wv', 'Wo')}
    del _L0_xattn_all

    def _L0_ffn_setup():
        import jax, jax.numpy as jnp
        import numpy as np
        B, T, D = (2, 256, 128)
        E, K, FF = (8, 2, 512)

        def _reference_tuple_inner(x, gate_w, gate_b, w1, b1, w2, b2):
            n_experts = w1.shape[0]
            gate_logits = x @ gate_w + gate_b
            topk_vals, topk_idx = jax.lax.top_k(gate_logits, K)
            topk_w = jax.nn.softmax(topk_vals, axis=-1)
            onehot = jax.nn.one_hot(topk_idx, n_experts, dtype=x.dtype)
            comb = jnp.sum(onehot * topk_w[..., None], axis=2)
            h = jax.nn.gelu(jnp.einsum('btd,edf->ebtf', x, w1) + b1[:, None, None, :], approximate=False)
            y = jnp.einsum('ebtf,efd->ebtd', h, w2) + b2[:, None, None, :]
            output = jnp.einsum('ebtd,bte->btd', y, comb)
            expert_counts = jnp.sum(onehot, axis=(0, 1, 2)).astype(jnp.float32)
            return (output, gate_logits, topk_idx, expert_counts)
        key = jax.random.key(seed)
        ks = jax.random.split(key, 4)
        scale = 0.02
        return {'x': jax.random.normal(ks[0], (B, T, D), jnp.float32), 'gate_w': jax.random.normal(ks[1], (D, E), jnp.float32) * scale, 'gate_b': jnp.zeros((E,), jnp.float32), 'w1': jax.random.normal(ks[2], (E, D, FF), jnp.float32) * scale, 'b1': jnp.zeros((E, FF), jnp.float32), 'w2': jax.random.normal(ks[3], (E, FF, D), jnp.float32) * scale, 'b2': jnp.zeros((E, D), jnp.float32)}
    _L0_ffn_all = _L0_ffn_setup()
    _L0_ffn_in = {k: v for k, v in _L0_ffn_all.items() if k in ('gate_w', 'gate_b', 'w1', 'b1', 'w2', 'b2')}
    del _L0_ffn_all

    def _L1_attn_setup():
        import jax, jax.numpy as jnp
        import numpy as np
        DIM = 128
        HID = 192
        K = 4
        N, T = (4, 512)

        def _mk_forget_base(h, a=0.001, b=0.1, lo=-4.323, hi=-9.0):
            x = np.log(np.expm1(np.linspace(a, b, h, dtype=np.float64)))
            x = (x - x.min()) / (x.max() - x.min())
            x = x * abs(hi - lo) + hi
            return jnp.asarray(x, dtype=jnp.float32)
        key = jax.random.key(seed)
        ks = jax.random.split(key, 6)
        x = jax.random.normal(ks[0], (N, T, DIM), jnp.float32)
        Wi = jax.random.normal(ks[1], (2 * HID, DIM), jnp.float32) * DIM ** (-0.5)
        conv_w = jax.random.normal(ks[2], (HID, 1, K), jnp.float32) * K ** (-0.5)
        conv_b = jax.random.normal(ks[3], (HID,), jnp.float32) * 0.01
        Wg = jax.random.normal(ks[4], (2 * HID, HID), jnp.float32) * HID ** (-0.5)
        bg = jnp.zeros((2 * HID,), jnp.float32)
        forget_base = _mk_forget_base(HID)
        Wo = jax.random.normal(ks[5], (DIM, HID), jnp.float32) * HID ** (-0.5)
        return {'x': x, 'Wi': Wi, 'conv_w': conv_w, 'conv_b': conv_b, 'Wg': Wg, 'bg': bg, 'forget_base': forget_base, 'Wo': Wo}
    _L1_attn_all = _L1_attn_setup()
    _L1_attn_in = {k: v for k, v in _L1_attn_all.items() if k in ('Wi', 'conv_w', 'conv_b', 'Wg', 'bg', 'forget_base', 'Wo')}
    del _L1_attn_all

    def _L1_xattn_setup():
        import jax, jax.numpy as jnp
        import numpy as np
        HEADS = 16
        key = jax.random.key(seed)
        ks = jax.random.split(key, 9)
        b, s, e = (2, 256, 128)
        w_scale = 1.0 / np.sqrt(e)
        return {'q': jax.random.normal(ks[0], (b, s, e), dtype=jnp.float32), 'k': jax.random.normal(ks[1], (b, s, e), dtype=jnp.float32), 'v': jax.random.normal(ks[2], (b, s, e), dtype=jnp.float32), 'keys_pad_mask': jnp.zeros((b, s), dtype=bool), 'Wq': jax.random.normal(ks[3], (e, e), dtype=jnp.float32) * w_scale, 'bq': jax.random.normal(ks[4], (e,), dtype=jnp.float32) * 0.01, 'Wk': jax.random.normal(ks[5], (e, e), dtype=jnp.float32) * w_scale, 'bk': jax.random.normal(ks[6], (e,), dtype=jnp.float32) * 0.01, 'Wv': jax.random.normal(ks[7], (e, e), dtype=jnp.float32) * w_scale, 'bv': jax.random.normal(ks[8], (e,), dtype=jnp.float32) * 0.01}
    _L1_xattn_all = _L1_xattn_setup()
    _L1_xattn_in = {k: v for k, v in _L1_xattn_all.items() if k in ('Wq', 'bq', 'Wk', 'bk', 'Wv', 'bv')}
    del _L1_xattn_all

    def _L1_ffn_setup():
        import jax, jax.numpy as jnp
        import numpy as np
        D_MODEL = 128
        D_FF = 512
        NUM_EXPERTS = 8
        TOP_K = 2
        key = jax.random.key(seed)
        ks = jax.random.split(key, 8)
        s_in = 1.0 / np.sqrt(D_MODEL)
        s_ff = 1.0 / np.sqrt(D_FF)
        x = jax.random.normal(ks[0], (2, 256, D_MODEL), dtype=jnp.float32)
        Wg = jax.random.uniform(ks[1], (D_MODEL, NUM_EXPERTS), minval=-s_in, maxval=s_in, dtype=jnp.float32)
        bg = jax.random.uniform(ks[2], (NUM_EXPERTS,), minval=-s_in, maxval=s_in, dtype=jnp.float32)
        W1 = jax.random.uniform(ks[3], (NUM_EXPERTS, D_MODEL, D_FF), minval=-s_in, maxval=s_in, dtype=jnp.float32)
        b1 = jax.random.uniform(ks[4], (NUM_EXPERTS, D_FF), minval=-s_in, maxval=s_in, dtype=jnp.float32)
        W2 = jax.random.uniform(ks[5], (NUM_EXPERTS, D_FF, D_MODEL), minval=-s_ff, maxval=s_ff, dtype=jnp.float32)
        b2 = jax.random.uniform(ks[6], (NUM_EXPERTS, D_MODEL), minval=-s_ff, maxval=s_ff, dtype=jnp.float32)
        return {'x': x, 'Wg': Wg, 'bg': bg, 'W1': W1, 'b1': b1, 'W2': W2, 'b2': b2}
    _L1_ffn_all = _L1_ffn_setup()
    _L1_ffn_in = {k: v for k, v in _L1_ffn_all.items() if k in ('Wg', 'bg', 'W1', 'b1', 'W2', 'b2')}
    del _L1_ffn_all

    def _L2_attn_setup():
        import math
        import jax, jax.numpy as jnp
        import numpy as np
        HIDDEN = 128
        NUM_HEADS = 16
        NUM_QUERIES = 2
        NUM_Q_HEADS = NUM_HEADS * NUM_QUERIES
        HEAD_DIM = 64
        Q_DIM = NUM_Q_HEADS * HEAD_DIM
        KV_DIM = NUM_HEADS * HEAD_DIM
        BATCH, SEQ = (4, 128)

        def _alibi_slopes(num_heads: int) -> np.ndarray:
            closest_pow2 = 2 ** int(math.floor(math.log2(num_heads)))
            base = 2.0 ** (-2.0 ** (-(math.log2(closest_pow2) - 3)))
            powers = np.arange(1, closest_pow2 + 1, dtype=np.float32)
            slopes = base ** powers
            if closest_pow2 != num_heads:
                extra_base = 2.0 ** (-2.0 ** (-(math.log2(2 * closest_pow2) - 3)))
                extra_powers = np.arange(1, 2 * (num_heads - closest_pow2) + 1, 2, dtype=np.float32)
                slopes = np.concatenate([slopes, extra_base ** extra_powers])
            return slopes[:num_heads].astype(np.float32)
        ALIBI_SLOPES = jnp.asarray(_alibi_slopes(NUM_Q_HEADS))
        key = jax.random.key(seed)
        k1, k2, k3 = jax.random.split(key, 3)
        inputs = jax.random.normal(k1, (BATCH, SEQ, HIDDEN), dtype=jnp.float32)
        W_qkv = jax.random.normal(k2, (HIDDEN, Q_DIM + 2 * KV_DIM), dtype=jnp.float32) * (1.0 / math.sqrt(HIDDEN))
        W_out = jax.random.normal(k3, (Q_DIM, HIDDEN), dtype=jnp.float32) * (1.0 / math.sqrt(Q_DIM))
        return {'inputs': inputs, 'W_qkv': W_qkv, 'W_out': W_out}
    _L2_attn_all = _L2_attn_setup()
    _L2_attn_in = {k: v for k, v in _L2_attn_all.items() if k in ('W_qkv', 'W_out')}
    del _L2_attn_all

    def _L2_xattn_setup():
        import jax, jax.numpy as jnp
        import numpy as np
        H = 16

        def _forward(queries, keys, values, Wq, bq, Wk, bk, Wv, bv, Wo, bo):
            N, L, _ = queries.shape
            q = (queries @ Wq + bq).reshape(N, L, H, -1)
            k = (keys @ Wk + bk).reshape(N, L, H, -1)
            v = (values @ Wv + bv).reshape(N, L, H, -1)
            qp = jax.nn.elu(q) + 1.0
            kp = jax.nn.elu(k) + 1.0
            D = qp.shape[-1]
            K = v.shape[-1]

            def step(sums, inp):
                q_t, k_t, v_t = inp
                sums = sums + jnp.einsum('bhd,bhk->bhdk', k_t, v_t)
                out_t = jnp.einsum('bhdk,bhd->bhk', sums, q_t)
                return (sums, out_t)
            init = jnp.zeros((N, H, D, K), qp.dtype)
            xs = (jnp.swapaxes(qp, 0, 1), jnp.swapaxes(kp, 0, 1), jnp.swapaxes(v, 0, 1))
            _, res = jax.lax.scan(step, init, xs)
            res = jnp.swapaxes(res, 0, 1)
            Z = jnp.cumsum(qp, axis=1)
            out = (res / Z).reshape(N, L, -1)
            return out @ Wo + bo
        key = jax.random.key(seed)
        ks = jax.random.split(key, 8)
        N, L, dm = (4, 256, 128)
        scale = 0.02
        rn = lambda k, shape: jax.random.normal(k, shape, dtype=jnp.float32)
        return {'queries': rn(ks[0], (N, L, dm)), 'keys': rn(ks[1], (N, L, dm)), 'values': rn(ks[2], (N, L, dm)), 'Wq': rn(ks[3], (dm, dm)) * scale, 'bq': jnp.zeros((dm,), jnp.float32), 'Wk': rn(ks[4], (dm, dm)) * scale, 'bk': jnp.zeros((dm,), jnp.float32), 'Wv': rn(ks[5], (dm, dm)) * scale, 'bv': jnp.zeros((dm,), jnp.float32), 'Wo': rn(ks[6], (dm, dm)) * scale, 'bo': jnp.zeros((dm,), jnp.float32)}
    _L2_xattn_all = _L2_xattn_setup()
    _L2_xattn_in = {k: v for k, v in _L2_xattn_all.items() if k in ('Wq', 'bq', 'Wk', 'bk', 'Wv', 'bv', 'Wo', 'bo')}
    del _L2_xattn_all

    def _L2_ffn_setup():
        import jax, jax.numpy as jnp
        import numpy as np
        B, S, H, I, E_ROUTED, TOP_K = (8, 256, 128, 256, 8, 2)

        def _expert(x, Wg, Wu, Wd):
            return jax.nn.silu(x @ Wg.T) * (x @ Wu.T) @ Wd.T
        key = jax.random.key(seed)
        ks = jax.random.split(key, 9)
        s = 0.02
        return {'x': jax.random.normal(ks[0], (B, S, H), dtype=jnp.float32), 'Wg_s': jax.random.normal(ks[1], (I, H), dtype=jnp.float32) * s, 'Wu_s': jax.random.normal(ks[2], (I, H), dtype=jnp.float32) * s, 'Wd_s': jax.random.normal(ks[3], (H, I), dtype=jnp.float32) * s, 'Wg': jax.random.normal(ks[4], (E_ROUTED, I, H), dtype=jnp.float32) * s, 'Wu': jax.random.normal(ks[5], (E_ROUTED, I, H), dtype=jnp.float32) * s, 'Wd': jax.random.normal(ks[6], (E_ROUTED, H, I), dtype=jnp.float32) * s, 'Wr': jax.random.normal(ks[7], (E_ROUTED, H), dtype=jnp.float32) * s, 'rb': jnp.zeros((E_ROUTED,), dtype=jnp.float32)}
    _L2_ffn_all = _L2_ffn_setup()
    _L2_ffn_in = {k: v for k, v in _L2_ffn_all.items() if k in ('Wg_s', 'Wu_s', 'Wd_s', 'Wg', 'Wu', 'Wd', 'Wr', 'rb')}
    del _L2_ffn_all

    def _L3_attn_setup():
        import jax, jax.numpy as jnp
        import numpy as np
        D_MODEL = 128
        N_HEADS = 16
        D_K = D_MODEL // N_HEADS
        MIN_F = 3
        MAX_F = 10

        def _sparsity_score(Q):
            l2 = jnp.linalg.norm(Q, axis=-1)
            logp = jax.nn.log_softmax(Q, axis=-1)
            prob = jnp.exp(logp)
            entropy = -jnp.sum(prob * jnp.log(prob + 1e-09), axis=-1)
            var = jnp.var(Q, axis=-1, ddof=1)
            return 0.5 * l2 + 0.3 * entropy + 0.2 * var
        key = jax.random.key(seed)
        ks = jax.random.split(key, 9)
        B, L = (4, 1024)
        x = jax.random.normal(ks[0], (B, L, D_MODEL), jnp.float32)

        def w(k):
            return jax.random.normal(k, (D_MODEL, D_MODEL), jnp.float32) * 0.02

        def b(k):
            return jax.random.normal(k, (D_MODEL,), jnp.float32) * 0.02
        return {'x': x, 'wq': w(ks[1]), 'bq': b(ks[2]), 'wk': w(ks[3]), 'bk': b(ks[4]), 'wv': w(ks[5]), 'bv': b(ks[6]), 'wo': w(ks[7]), 'bo': b(ks[8])}
    _L3_attn_all = _L3_attn_setup()
    _L3_attn_in = {k: v for k, v in _L3_attn_all.items() if k in ('wq', 'bq', 'wk', 'bk', 'wv', 'bv', 'wo', 'bo')}
    del _L3_attn_all

    def _L3_xattn_setup():
        import jax, jax.numpy as jnp
        import numpy as np
        D1, D2, D3 = (128, 128, 128)
        key = jax.random.key(seed)
        k1, k2, kw, kb = jax.random.split(key, 4)
        x1 = jax.random.normal(k1, (8, 256, D1), dtype=jnp.float32)
        x2 = jax.random.normal(k2, (8, 256, D2), dtype=jnp.float32)
        bound = 1.0 / np.sqrt(D1 + D2)
        W = jax.random.uniform(kw, (D3, D1 + D2), minval=-bound, maxval=bound, dtype=jnp.float32)
        b = jax.random.uniform(kb, (D3,), minval=-bound, maxval=bound, dtype=jnp.float32)
        return {'x1': x1, 'x2': x2, 'W': W, 'b': b}
    _L3_xattn_all = _L3_xattn_setup()
    _L3_xattn_in = {k: v for k, v in _L3_xattn_all.items() if k in ('W', 'b')}
    del _L3_xattn_all

    def _L3_ffn_setup():
        import jax, jax.numpy as jnp
        import numpy as np
        NUM_EXPERTS = 8
        IN_FEATURES = 128
        HIDDEN_FEATURES = 512
        GATE_DIM = 16
        EPS = 0.0001
        key = jax.random.key(seed)
        ks = jax.random.split(key, 7)
        hidden_states = jax.random.normal(ks[0], (1, 256, IN_FEATURES), dtype=jnp.float32)
        wg_red = jax.random.normal(ks[1], (GATE_DIM, IN_FEATURES), dtype=jnp.float32) * 0.02
        wg = jax.random.normal(ks[2], (NUM_EXPERTS, GATE_DIM), dtype=jnp.float32)
        w1 = jax.random.uniform(ks[3], (NUM_EXPERTS, IN_FEATURES, HIDDEN_FEATURES), dtype=jnp.float32)
        b1 = jax.random.uniform(ks[4], (NUM_EXPERTS, HIDDEN_FEATURES), dtype=jnp.float32)
        w2 = jax.random.uniform(ks[5], (NUM_EXPERTS, HIDDEN_FEATURES, IN_FEATURES), dtype=jnp.float32)
        b2 = jax.random.uniform(ks[6], (NUM_EXPERTS, IN_FEATURES), dtype=jnp.float32)
        return {'hidden_states': hidden_states, 'wg_red': wg_red, 'wg': wg, 'w1': w1, 'b1': b1, 'w2': w2, 'b2': b2}
    _L3_ffn_all = _L3_ffn_setup()
    _L3_ffn_in = {k: v for k, v in _L3_ffn_all.items() if k in ('wg_red', 'wg', 'w1', 'b1', 'w2', 'b2')}
    del _L3_ffn_all
    return {'x': x, 'ctx_1024': ctx_1024, 'mask_BxS2_bf0': mask_BxS2_bf0, 'L0_attn_Wq': _L0_attn_in['Wq'], 'L0_attn_Wk': _L0_attn_in['Wk'], 'L0_attn_Wv': _L0_attn_in['Wv'], 'L0_attn_Wo': _L0_attn_in['Wo'], 'L0_attn_Wck': _L0_attn_in['Wck'], 'L0_attn_Wcv': _L0_attn_in['Wcv'], 'L0_attn_Wg': _L0_attn_in['Wg'], 'L0_attn_bg': _L0_attn_in['bg'], 'L0_xattn_Wq': _L0_xattn_in['Wq'], 'L0_xattn_Wk': _L0_xattn_in['Wk'], 'L0_xattn_Wv': _L0_xattn_in['Wv'], 'L0_xattn_Wo': _L0_xattn_in['Wo'], 'L0_ffn_gate_w': _L0_ffn_in['gate_w'], 'L0_ffn_gate_b': _L0_ffn_in['gate_b'], 'L0_ffn_w1': _L0_ffn_in['w1'], 'L0_ffn_b1': _L0_ffn_in['b1'], 'L0_ffn_w2': _L0_ffn_in['w2'], 'L0_ffn_b2': _L0_ffn_in['b2'], 'L1_attn_Wi': _L1_attn_in['Wi'], 'L1_attn_conv_w': _L1_attn_in['conv_w'], 'L1_attn_conv_b': _L1_attn_in['conv_b'], 'L1_attn_Wg': _L1_attn_in['Wg'], 'L1_attn_bg': _L1_attn_in['bg'], 'L1_attn_forget_base': _L1_attn_in['forget_base'], 'L1_attn_Wo': _L1_attn_in['Wo'], 'L1_xattn_Wq': _L1_xattn_in['Wq'], 'L1_xattn_bq': _L1_xattn_in['bq'], 'L1_xattn_Wk': _L1_xattn_in['Wk'], 'L1_xattn_bk': _L1_xattn_in['bk'], 'L1_xattn_Wv': _L1_xattn_in['Wv'], 'L1_xattn_bv': _L1_xattn_in['bv'], 'L1_ffn_Wg': _L1_ffn_in['Wg'], 'L1_ffn_bg': _L1_ffn_in['bg'], 'L1_ffn_W1': _L1_ffn_in['W1'], 'L1_ffn_b1': _L1_ffn_in['b1'], 'L1_ffn_W2': _L1_ffn_in['W2'], 'L1_ffn_b2': _L1_ffn_in['b2'], 'L2_attn_W_qkv': _L2_attn_in['W_qkv'], 'L2_attn_W_out': _L2_attn_in['W_out'], 'L2_xattn_Wq': _L2_xattn_in['Wq'], 'L2_xattn_bq': _L2_xattn_in['bq'], 'L2_xattn_Wk': _L2_xattn_in['Wk'], 'L2_xattn_bk': _L2_xattn_in['bk'], 'L2_xattn_Wv': _L2_xattn_in['Wv'], 'L2_xattn_bv': _L2_xattn_in['bv'], 'L2_xattn_Wo': _L2_xattn_in['Wo'], 'L2_xattn_bo': _L2_xattn_in['bo'], 'L2_ffn_Wg_s': _L2_ffn_in['Wg_s'], 'L2_ffn_Wu_s': _L2_ffn_in['Wu_s'], 'L2_ffn_Wd_s': _L2_ffn_in['Wd_s'], 'L2_ffn_Wg': _L2_ffn_in['Wg'], 'L2_ffn_Wu': _L2_ffn_in['Wu'], 'L2_ffn_Wd': _L2_ffn_in['Wd'], 'L2_ffn_Wr': _L2_ffn_in['Wr'], 'L2_ffn_rb': _L2_ffn_in['rb'], 'L3_attn_wq': _L3_attn_in['wq'], 'L3_attn_bq': _L3_attn_in['bq'], 'L3_attn_wk': _L3_attn_in['wk'], 'L3_attn_bk': _L3_attn_in['bk'], 'L3_attn_wv': _L3_attn_in['wv'], 'L3_attn_bv': _L3_attn_in['bv'], 'L3_attn_wo': _L3_attn_in['wo'], 'L3_attn_bo': _L3_attn_in['bo'], 'L3_xattn_W': _L3_xattn_in['W'], 'L3_xattn_b': _L3_xattn_in['b'], 'L3_ffn_wg_red': _L3_ffn_in['wg_red'], 'L3_ffn_wg': _L3_ffn_in['wg'], 'L3_ffn_w1': _L3_ffn_in['w1'], 'L3_ffn_b1': _L3_ffn_in['b1'], 'L3_ffn_w2': _L3_ffn_in['w2'], 'L3_ffn_b2': _L3_ffn_in['b2']}

def reference(x, ctx_1024, mask_BxS2_bf0, L0_attn_Wq, L0_attn_Wk, L0_attn_Wv, L0_attn_Wo, L0_attn_Wck, L0_attn_Wcv, L0_attn_Wg, L0_attn_bg, L0_xattn_Wq, L0_xattn_Wk, L0_xattn_Wv, L0_xattn_Wo, L0_ffn_gate_w, L0_ffn_gate_b, L0_ffn_w1, L0_ffn_b1, L0_ffn_w2, L0_ffn_b2, L1_attn_Wi, L1_attn_conv_w, L1_attn_conv_b, L1_attn_Wg, L1_attn_bg, L1_attn_forget_base, L1_attn_Wo, L1_xattn_Wq, L1_xattn_bq, L1_xattn_Wk, L1_xattn_bk, L1_xattn_Wv, L1_xattn_bv, L1_ffn_Wg, L1_ffn_bg, L1_ffn_W1, L1_ffn_b1, L1_ffn_W2, L1_ffn_b2, L2_attn_W_qkv, L2_attn_W_out, L2_xattn_Wq, L2_xattn_bq, L2_xattn_Wk, L2_xattn_bk, L2_xattn_Wv, L2_xattn_bv, L2_xattn_Wo, L2_xattn_bo, L2_ffn_Wg_s, L2_ffn_Wu_s, L2_ffn_Wd_s, L2_ffn_Wg, L2_ffn_Wu, L2_ffn_Wd, L2_ffn_Wr, L2_ffn_rb, L3_attn_wq, L3_attn_bq, L3_attn_wk, L3_attn_bk, L3_attn_wv, L3_attn_bv, L3_attn_wo, L3_attn_bo, L3_xattn_W, L3_xattn_b, L3_ffn_wg_red, L3_ffn_wg, L3_ffn_w1, L3_ffn_b1, L3_ffn_w2, L3_ffn_b2):
    import jax
    import jax.numpy as jnp

    def _L0_attn_ref(x, Wq, Wk, Wv, Wo, Wck, Wcv, Wg, bg):
        import jax, jax.numpy as jnp
        import numpy as np
        H = 16
        G = 16
        R = 4
        WIN = 64
        NEG = -1000000000.0
        B, T, dm = x.shape
        D = dm // H
        scale = float(np.sqrt(D))

        def split_heads(y):
            return y.reshape(B, T, H, D).transpose(0, 2, 1, 3)
        q = split_heads(x @ Wq)
        k = split_heads(x @ Wk)
        v = split_heads(x @ Wv)
        pad = -T % G
        T_pad = T + pad
        k_pad = jnp.pad(k, ((0, 0), (0, 0), (0, pad), (0, 0)))
        v_pad = jnp.pad(v, ((0, 0), (0, 0), (0, pad), (0, 0)))
        nb = T_pad // G
        k_c = k_pad.reshape(B, H, nb, G * D) @ Wck
        v_c = v_pad.reshape(B, H, nb, G * D) @ Wcv
        pos = jnp.arange(T)
        blk_end = (jnp.arange(nb) + 1) * G
        c_ok = pos[:, None] >= blk_end[None, :]
        s_b = jnp.einsum('bhtd,bhnd->bhtn', q, k_c) / scale
        logits_c = jnp.where(c_ok, s_b, NEG)
        out_c = jnp.einsum('bhtn,bhnd->bhtd', jax.nn.softmax(logits_c, axis=-1), v_c)
        out_c = out_c * jnp.any(c_ok, axis=-1)[:, None].astype(out_c.dtype)
        r_eff = min(R, nb)
        _, top_idx = jax.lax.top_k(logits_c, r_eff)
        tok = (top_idx[..., None] * G + jnp.arange(G)).reshape(B, H, T, r_eff * G)
        tok = jnp.clip(tok, 0, T_pad - 1)
        bi = jnp.arange(B)[:, None, None, None]
        hi = jnp.arange(H)[None, :, None, None]
        k_s = k_pad[bi, hi, tok]
        v_s = v_pad[bi, hi, tok]
        allowed = tok <= pos[None, None, :, None]
        logits_s = jnp.where(allowed, jnp.einsum('bhtd,bhtnd->bhtn', q, k_s) / scale, NEG)
        out_s = jnp.einsum('bhtn,bhtnd->bhtd', jax.nn.softmax(logits_s, axis=-1), v_s)
        out_s = out_s * jnp.any(allowed, axis=-1)[..., None].astype(out_s.dtype)
        wmask = (jnp.abs(pos[:, None] - pos[None, :]) <= WIN // 2) & (pos[:, None] >= pos[None, :])
        logits_l = jnp.where(wmask, jnp.einsum('bhtd,bhsd->bhts', q, k) / scale, NEG)
        out_l = jnp.einsum('bhts,bhsd->bhtd', jax.nn.softmax(logits_l, axis=-1), v)
        gates = jax.nn.softmax(q.mean(axis=1) @ Wg + bg, axis=-1)

        def merge(o):
            return o.transpose(0, 2, 1, 3).reshape(B, T, dm)
        out = gates[..., 0:1] * merge(out_c) + gates[..., 1:2] * merge(out_s) + gates[..., 2:3] * merge(out_l)
        return out @ Wo

    def _L0_xattn_ref(q, k, v, Wq, Wk, Wv, Wo):
        import jax, jax.numpy as jnp
        import numpy as np
        D_MODEL = 128
        NUM_HEADS = 16
        D_K = D_MODEL // NUM_HEADS

        def _split_heads(x):
            B, S, _ = x.shape
            return x.reshape(B, S, NUM_HEADS, D_K).transpose(0, 2, 1, 3)
        B, S, _ = q.shape
        qh = _split_heads(q @ Wq.T)
        kh = _split_heads(k @ Wk.T)
        vh = _split_heads(v @ Wv.T)
        scores = jnp.einsum('bhqd,bhkd->bhqk', qh, kh) / np.sqrt(D_K).astype(np.float32)
        causal = jnp.tril(jnp.ones((S, S), dtype=bool))
        scores = jnp.where(causal, scores, -jnp.inf)
        attn = jax.nn.softmax(scores, axis=-1)
        out = jnp.einsum('bhqk,bhkd->bhqd', attn, vh)
        out = out.transpose(0, 2, 1, 3).reshape(B, S, D_MODEL)
        return out @ Wo.T

    def _L0_ffn_ref(x, gate_w, gate_b, w1, b1, w2, b2):
        import jax, jax.numpy as jnp
        import numpy as np
        B, T, D = (2, 256, 128)
        E, K, FF = (8, 2, 512)

        def _reference_tuple_inner(x, gate_w, gate_b, w1, b1, w2, b2):
            n_experts = w1.shape[0]
            gate_logits = x @ gate_w + gate_b
            topk_vals, topk_idx = jax.lax.top_k(gate_logits, K)
            topk_w = jax.nn.softmax(topk_vals, axis=-1)
            onehot = jax.nn.one_hot(topk_idx, n_experts, dtype=x.dtype)
            comb = jnp.sum(onehot * topk_w[..., None], axis=2)
            h = jax.nn.gelu(jnp.einsum('btd,edf->ebtf', x, w1) + b1[:, None, None, :], approximate=False)
            y = jnp.einsum('ebtf,efd->ebtd', h, w2) + b2[:, None, None, :]
            output = jnp.einsum('ebtd,bte->btd', y, comb)
            expert_counts = jnp.sum(onehot, axis=(0, 1, 2)).astype(jnp.float32)
            return (output, gate_logits, topk_idx, expert_counts)
        return _reference_tuple_inner(x, gate_w, gate_b, w1, b1, w2, b2)[0]

    def _L1_attn_ref(x, Wi, conv_w, conv_b, Wg, bg, forget_base, Wo):
        import jax, jax.numpy as jnp
        import numpy as np
        DIM = 128
        HID = 192
        K = 4
        N, T = (4, 512)

        def _mk_forget_base(h, a=0.001, b=0.1, lo=-4.323, hi=-9.0):
            x = np.log(np.expm1(np.linspace(a, b, h, dtype=np.float64)))
            x = (x - x.min()) / (x.max() - x.min())
            x = x * abs(hi - lo) + hi
            return jnp.asarray(x, dtype=jnp.float32)
        gi = jnp.einsum('ntc,hc->nth', x, Wi)
        gate, u = jnp.split(gi, 2, axis=-1)
        u = jax.lax.conv_general_dilated(u.transpose(0, 2, 1), conv_w, window_strides=(1,), padding=[(K - 1, 0)], dimension_numbers=('NCH', 'OIH', 'NCH'), feature_group_count=HID) + conv_b[None, :, None]
        u = u.transpose(0, 2, 1)
        fg = jnp.einsum('nth,gh->ntg', u, Wg) + bg
        forget, inp = jnp.split(fg, 2, axis=-1)
        alpha = jnp.exp(-8.0 * jax.nn.softplus(forget_base) * jax.nn.sigmoid(forget))
        beta = jnp.sqrt(1.0 - alpha ** 2 + 1e-06)
        xt = beta * jax.nn.sigmoid(inp) * u

        def step(h, ax):
            a, xx = ax
            h = a * h + xx
            return (h, h)
        _, h = jax.lax.scan(step, jnp.zeros((x.shape[0], HID), x.dtype), (alpha.transpose(1, 0, 2), xt.transpose(1, 0, 2)))
        h = h.transpose(1, 0, 2)
        return jnp.einsum('nth,ch->ntc', jax.nn.gelu(gate, approximate=False) * h, Wo)

    def _L1_xattn_ref(q, k, v, keys_pad_mask, Wq, bq, Wk, bk, Wv, bv):
        import jax, jax.numpy as jnp
        import numpy as np
        HEADS = 16
        b, s_q, e = q.shape
        s_k = k.shape[1]
        h = HEADS
        Q = (q @ Wq.T + bq).reshape(b, h, s_q, -1)
        K = (k @ Wk.T + bk).reshape(b, h, s_k, -1)
        V = (v @ Wv.T + bv).reshape(b, h, s_k, -1)
        scale = jnp.sqrt(jnp.asarray(Q.shape[-1], Q.dtype))
        QK = jnp.einsum('bhqd,bhkd->bhqk', Q, K) * scale
        QK = jnp.where(keys_pad_mask[:, None, None, :], -jnp.inf, QK)
        causal = jnp.triu(jnp.ones((s_q, s_k), dtype=bool), 1)
        QK = jnp.where(causal[None, None], -jnp.inf, QK)
        attn = jax.nn.softmax(QK, axis=-1)
        out = jnp.einsum('bhqk,bhkd->bhqd', attn, V).reshape(b, s_q, -1)
        return out

    def _L1_ffn_ref(x, Wg, bg, W1, b1, W2, b2):
        import jax, jax.numpy as jnp
        import numpy as np
        D_MODEL = 128
        D_FF = 512
        NUM_EXPERTS = 8
        TOP_K = 2
        gate_logits = jnp.einsum('bsd,de->bse', x, Wg) + bg
        gate_probs = jax.nn.softmax(gate_logits, axis=-1)
        topk_probs, topk_idx = jax.lax.top_k(gate_probs, TOP_K)
        topk_probs = topk_probs / jnp.sum(topk_probs, axis=-1, keepdims=True)
        onehot = jax.nn.one_hot(topk_idx, NUM_EXPERTS, dtype=x.dtype)
        weights = jnp.einsum('bske,bsk->bse', onehot, topk_probs)
        h = jnp.einsum('bsd,edf->bsef', x, W1) + b1
        h = jax.nn.gelu(h, approximate=False)
        y = jnp.einsum('bsef,efd->bsed', h, W2) + b2
        return jnp.einsum('bsed,bse->bsd', y, weights)

    def _L2_attn_ref(inputs, W_qkv, W_out):
        import math
        import jax, jax.numpy as jnp
        import numpy as np
        HIDDEN = 128
        NUM_HEADS = 16
        NUM_QUERIES = 2
        NUM_Q_HEADS = NUM_HEADS * NUM_QUERIES
        HEAD_DIM = 64
        Q_DIM = NUM_Q_HEADS * HEAD_DIM
        KV_DIM = NUM_HEADS * HEAD_DIM
        BATCH, SEQ = (4, 128)

        def _alibi_slopes(num_heads: int) -> np.ndarray:
            closest_pow2 = 2 ** int(math.floor(math.log2(num_heads)))
            base = 2.0 ** (-2.0 ** (-(math.log2(closest_pow2) - 3)))
            powers = np.arange(1, closest_pow2 + 1, dtype=np.float32)
            slopes = base ** powers
            if closest_pow2 != num_heads:
                extra_base = 2.0 ** (-2.0 ** (-(math.log2(2 * closest_pow2) - 3)))
                extra_powers = np.arange(1, 2 * (num_heads - closest_pow2) + 1, 2, dtype=np.float32)
                slopes = np.concatenate([slopes, extra_base ** extra_powers])
            return slopes[:num_heads].astype(np.float32)
        ALIBI_SLOPES = jnp.asarray(_alibi_slopes(NUM_Q_HEADS))
        B, S, _ = inputs.shape
        qkv = inputs @ W_qkv
        q = qkv[..., :Q_DIM].reshape(B, S, NUM_Q_HEADS, HEAD_DIM).transpose(0, 2, 1, 3)
        k = qkv[..., Q_DIM:Q_DIM + KV_DIM].reshape(B, S, NUM_HEADS, HEAD_DIM).transpose(0, 2, 1, 3)
        v = qkv[..., Q_DIM + KV_DIM:].reshape(B, S, NUM_HEADS, HEAD_DIM).transpose(0, 2, 1, 3)
        k = jnp.repeat(k, NUM_QUERIES, axis=1)
        v = jnp.repeat(v, NUM_QUERIES, axis=1)
        pos = jnp.arange(S)
        rel = (pos[None, :] - pos[:, None]).astype(jnp.float32)
        bias = ALIBI_SLOPES[:, None, None] * rel[None, :, :]
        scores = jnp.einsum('bhqd,bhkd->bhqk', q, k) / math.sqrt(HEAD_DIM)
        scores = scores + bias[None]
        causal = pos[:, None] >= pos[None, :]
        scores = jnp.where(causal[None, None], scores, -jnp.inf)
        attn = jax.nn.softmax(scores, axis=-1)
        out = jnp.einsum('bhqk,bhkd->bhqd', attn, v)
        out = out.transpose(0, 2, 1, 3).reshape(B, S, Q_DIM)
        return out @ W_out

    def _L2_xattn_ref(queries, keys, values, Wq, bq, Wk, bk, Wv, bv, Wo, bo):
        import jax, jax.numpy as jnp
        import numpy as np
        H = 16

        def _forward(queries, keys, values, Wq, bq, Wk, bk, Wv, bv, Wo, bo):
            N, L, _ = queries.shape
            q = (queries @ Wq + bq).reshape(N, L, H, -1)
            k = (keys @ Wk + bk).reshape(N, L, H, -1)
            v = (values @ Wv + bv).reshape(N, L, H, -1)
            qp = jax.nn.elu(q) + 1.0
            kp = jax.nn.elu(k) + 1.0
            D = qp.shape[-1]
            K = v.shape[-1]

            def step(sums, inp):
                q_t, k_t, v_t = inp
                sums = sums + jnp.einsum('bhd,bhk->bhdk', k_t, v_t)
                out_t = jnp.einsum('bhdk,bhd->bhk', sums, q_t)
                return (sums, out_t)
            init = jnp.zeros((N, H, D, K), qp.dtype)
            xs = (jnp.swapaxes(qp, 0, 1), jnp.swapaxes(kp, 0, 1), jnp.swapaxes(v, 0, 1))
            _, res = jax.lax.scan(step, init, xs)
            res = jnp.swapaxes(res, 0, 1)
            Z = jnp.cumsum(qp, axis=1)
            out = (res / Z).reshape(N, L, -1)
            return out @ Wo + bo
        return _forward(queries, keys, values, Wq, bq, Wk, bk, Wv, bv, Wo, bo)

    def _L2_ffn_ref(x, Wg_s, Wu_s, Wd_s, Wg, Wu, Wd, Wr, rb):
        import jax, jax.numpy as jnp
        import numpy as np
        B, S, H, I, E_ROUTED, TOP_K = (8, 256, 128, 256, 8, 2)

        def _expert(x, Wg, Wu, Wd):
            return jax.nn.silu(x @ Wg.T) * (x @ Wu.T) @ Wd.T
        shared = _expert(x, Wg_s, Wu_s, Wd_s)
        logits = jnp.einsum('bsh,eh->bse', x, Wr) + rb
        probs = jax.nn.sigmoid(logits)
        scores, idx = jax.lax.top_k(probs, TOP_K)
        cw = (jax.nn.one_hot(idx, E_ROUTED, dtype=x.dtype) * scores[..., None]).sum(-2)
        out = shared
        for e in range(E_ROUTED):
            out = out + cw[..., e:e + 1] * _expert(x, Wg[e], Wu[e], Wd[e])
        return out

    def _L3_attn_ref(x, wq, bq, wk, bk, wv, bv, wo, bo):
        import jax, jax.numpy as jnp
        import numpy as np
        D_MODEL = 128
        N_HEADS = 16
        D_K = D_MODEL // N_HEADS
        MIN_F = 3
        MAX_F = 10

        def _sparsity_score(Q):
            l2 = jnp.linalg.norm(Q, axis=-1)
            logp = jax.nn.log_softmax(Q, axis=-1)
            prob = jnp.exp(logp)
            entropy = -jnp.sum(prob * jnp.log(prob + 1e-09), axis=-1)
            var = jnp.var(Q, axis=-1, ddof=1)
            return 0.5 * l2 + 0.3 * entropy + 0.2 * var
        B, L, D = x.shape
        H, dk = (N_HEADS, D_K)
        Q = (x @ wq.T + bq).reshape(B, L, H, dk).transpose(0, 2, 1, 3)
        K = (x @ wk.T + bk).reshape(B, L, H, dk).transpose(0, 2, 1, 3)
        V = (x @ wv.T + bv).reshape(B, L, H, dk).transpose(0, 2, 1, 3)
        q_scores = _sparsity_score(Q)
        q_std = jnp.std(q_scores, axis=2, keepdims=True, ddof=1)
        q_mean = jnp.mean(q_scores, axis=2, keepdims=True)
        factor = jnp.clip(jnp.round(q_std / (q_mean + 1e-06) * MAX_F).astype(jnp.int32), MIN_F, MAX_F)
        u = factor[:, 0, 0]
        _, top_idx = jax.lax.top_k(q_scores, MAX_F)
        mask = jnp.arange(MAX_F)[None, None, :] < u[:, None, None]
        Q_sparse = jnp.take_along_axis(Q, top_idx[..., None], axis=2)
        scores = jnp.einsum('bhud,bhld->bhul', Q_sparse, K) / np.sqrt(dk).astype(np.float32)
        attn = jax.nn.softmax(scores, axis=-1)
        out = jnp.einsum('bhul,bhld->bhud', attn, V)
        out = out * mask[..., None].astype(out.dtype)
        bi = jnp.arange(B)[:, None, None]
        hi = jnp.arange(H)[None, :, None]
        full = jnp.zeros((B, H, L, dk), out.dtype).at[bi, hi, top_idx].set(out)
        merged = full.transpose(0, 2, 1, 3).reshape(B, L, D)
        return merged @ wo.T + bo

    def _L3_xattn_ref(x1, x2, W, b):
        import jax, jax.numpy as jnp
        import numpy as np
        D1, D2, D3 = (128, 128, 128)
        d1 = x1.shape[-1]
        W1 = W[:, :d1]
        W2 = W[:, d1:]
        part1 = jnp.einsum('bld,ed->ble', x1, W1)
        part2 = jnp.einsum('bld,ed->be', x2, W2) / x2.shape[1]
        return part1 + part2[:, None, :] + b

    def _L3_ffn_ref(hidden_states, wg_red, wg, w1, b1, w2, b2):
        import jax, jax.numpy as jnp
        import numpy as np
        NUM_EXPERTS = 8
        IN_FEATURES = 128
        HIDDEN_FEATURES = 512
        GATE_DIM = 16
        EPS = 0.0001
        b, t, c = hidden_states.shape
        x = hidden_states.reshape(-1, c)
        xr = x @ wg_red.T
        wg_unit = wg / jnp.maximum(jnp.linalg.norm(wg, axis=1, keepdims=True), EPS)
        logits = xr @ wg_unit.T
        gates = jax.nn.softmax(logits, axis=1)
        indices_s = jnp.argmax(gates, axis=1)
        scores = jnp.max(gates, axis=1)
        E = wg.shape[0]
        out = jnp.zeros_like(x)
        for e in range(E):
            mask = (indices_s == e).astype(x.dtype)[:, None]
            h = jax.nn.gelu(x @ w1[e] + b1[e], approximate=False)
            out = out + mask * (h @ w2[e] + b2[e])
        out = out * scores[:, None]
        return out.reshape(b, t, c)
    x = x + _L0_attn_ref(_layernorm(x, axis=-1), L0_attn_Wq, L0_attn_Wk, L0_attn_Wv, L0_attn_Wo, L0_attn_Wck, L0_attn_Wcv, L0_attn_Wg, L0_attn_bg)
    x = x + _L0_xattn_ref(_layernorm(x, axis=-1), ctx_1024, ctx_1024, L0_xattn_Wq, L0_xattn_Wk, L0_xattn_Wv, L0_xattn_Wo)
    x = x + _L0_ffn_ref(_layernorm(x, axis=-1), L0_ffn_gate_w, L0_ffn_gate_b, L0_ffn_w1, L0_ffn_b1, L0_ffn_w2, L0_ffn_b2)
    x = x + _L1_attn_ref(_layernorm(x, axis=-1), L1_attn_Wi, L1_attn_conv_w, L1_attn_conv_b, L1_attn_Wg, L1_attn_bg, L1_attn_forget_base, L1_attn_Wo)
    x = x + _L1_xattn_ref(_layernorm(x, axis=-1), ctx_1024, ctx_1024, mask_BxS2_bf0, L1_xattn_Wq, L1_xattn_bq, L1_xattn_Wk, L1_xattn_bk, L1_xattn_Wv, L1_xattn_bv)
    x = x + _L1_ffn_ref(_layernorm(x, axis=-1), L1_ffn_Wg, L1_ffn_bg, L1_ffn_W1, L1_ffn_b1, L1_ffn_W2, L1_ffn_b2)
    x = x + _L2_attn_ref(_layernorm(x, axis=-1), L2_attn_W_qkv, L2_attn_W_out)
    x = x + _L2_xattn_ref(_layernorm(x, axis=-1), ctx_1024, ctx_1024, L2_xattn_Wq, L2_xattn_bq, L2_xattn_Wk, L2_xattn_bk, L2_xattn_Wv, L2_xattn_bv, L2_xattn_Wo, L2_xattn_bo)
    x = x + _L2_ffn_ref(_layernorm(x, axis=-1), L2_ffn_Wg_s, L2_ffn_Wu_s, L2_ffn_Wd_s, L2_ffn_Wg, L2_ffn_Wu, L2_ffn_Wd, L2_ffn_Wr, L2_ffn_rb)
    x = x + _L3_attn_ref(_layernorm(x, axis=-1), L3_attn_wq, L3_attn_bq, L3_attn_wk, L3_attn_bk, L3_attn_wv, L3_attn_bv, L3_attn_wo, L3_attn_bo)
    x = x + _L3_xattn_ref(_layernorm(x, axis=-1), ctx_1024, L3_xattn_W, L3_xattn_b)
    x = x + _L3_ffn_ref(_layernorm(x, axis=-1), L3_ffn_wg_red, L3_ffn_wg, L3_ffn_w1, L3_ffn_b1, L3_ffn_w2, L3_ffn_b2)
    return x

_drawn_inputs = setup_inputs


def setup_inputs(seed=0):
    import zlib

    import numpy as np

    out = dict(_drawn_inputs(seed))
    spreads = {'L0_attn_bg': (0.0, 0.8),
     'L0_ffn_gate_b': (0.0, 0.1),
     'L0_ffn_b1': (0.0, 0.508),
     'L0_ffn_b2': (0.0, 0.1),
     'L1_attn_bg': (0.0, 0.386),
     'L2_xattn_bq': (0.0, 0.657),
     'L2_xattn_bk': (0.0, 0.8),
     'L2_xattn_bv': (0.0, 0.1),
     'L2_xattn_bo': (0.0, 0.394),
     'L2_ffn_rb': (0.0, 0.8)}
    factors = {'L0_attn_Wq': 8.0,
     'L0_attn_Wk': 8.0,
     'L0_attn_Wv': 5.493,
     'L0_attn_Wo': 5.696,
     'L0_attn_Wck': 8.0,
     'L0_attn_Wcv': 8.0,
     'L0_attn_Wg': 8.0,
     'L1_attn_conv_b': 4.322,
     'L1_xattn_bq': 6.434,
     'L1_xattn_bk': 7.316,
     'L1_xattn_bv': 8.0,
     'L1_ffn_bg': 7.091,
     'L1_ffn_b1': 7.185,
     'L1_ffn_b2': 8.0,
     'L2_xattn_Wq': 5.899,
     'L2_xattn_Wk': 8.0,
     'L2_ffn_Wg_s': 8.0,
     'L2_ffn_Wu_s': 8.0,
     'L2_ffn_Wd_s': 8.0,
     'L2_ffn_Wg': 8.0,
     'L2_ffn_Wu': 8.0,
     'L2_ffn_Wd': 8.0,
     'L2_ffn_Wr': 8.0,
     'L3_attn_wq': 41.925,
     'L3_attn_bq': 64.0,
     'L3_attn_wk': 46.977,
     'L3_attn_bk': 64.0,
     'L3_attn_wv': 45.638,
     'L3_attn_bv': 64.0,
     'L3_attn_wo': 46.897,
     'L3_attn_bo': 62.616,
     'L3_xattn_b': 28.082,
     'L3_ffn_b1': 8.0,
     'L3_ffn_b2': 64.0,
     'L3_xattn_W': 4.021}
    for name, (base, spread) in spreads.items():
        noise = np.random.default_rng([zlib.crc32(name.encode()), seed]).standard_normal(out[name].shape)
        drawn = base * np.exp(spread * noise) if base else spread * noise
        out[name] = jnp.asarray(drawn.astype(out[name].dtype))
    for name, factor in factors.items():
        out[name] = (out[name] * factor).astype(out[name].dtype)
    return out
```

```python
from contextlib import ExitStack

import numpy as np

import concourse.bass as bass
from concourse import mybir

F32 = mybir.dt.float32
U8 = mybir.dt.uint8
U32 = mybir.dt.uint32
ALU = mybir.AluOpType
ACT = mybir.ActivationFunctionType
AX = mybir.AxisListType
ds = bass.ds

P = 128
NB = 8
T = NB * P
H = 16
HD = 8
NE = 8
BANK = 512
BIG = 1.0e30
NEG = -1.0e9
EPS = 1.0e-5
G0 = 16
NBLK = P // G0
TOP_BLOCKS = 4
WIN = 32
HID = 192
HC = HID // 2
KC = 4
QH, KVH, DH = 32, 16, 64
NPAIR = KVH // 2
FF = 512
FI = 256
MIN_F, MAX_F = 3, 10
ENGINES = ("sync", "gpsimd", "scalar", "tensor", "vector")


class Flow:

    def __init__(self, nc, ctx):
        self.nc, self.ctx = nc, ctx
        self.sems = {e: ctx.enter_context(nc.semaphore(f"done_{e}")) for e in ENGINES}
        self.segments = []
        self.base = {}

    def semaphore(self, name):
        self.sems[name] = self.ctx.enter_context(self.nc.semaphore(name))
        return name

    def segment(self, name, trips=1):
        if self.segments:
            last = self.segments[-1]
            for s, k in last["count"].items():
                self.base[s] = self.base.get(s, 0) + k * last["trips"]
        self.segments.append(dict(name=name, trips=trips, base=dict(self.base), count={},
                                  queue={e: [] for e in ENGINES}))

    def put(self, engine, make, after, sem=None, step=1):
        seg = self.segments[-1]
        waits = []

        def add(a):
            if a is None:
                return
            if isinstance(a, list):
                for x in a:
                    add(x)
            else:
                waits.append(a)
        add(list(after))
        mark = None
        if sem is not False:
            name = sem or engine
            seg["count"][name] = seg["count"].get(name, 0) + step
            mark = (len(self.segments) - 1, name, seg["count"][name])
            signal = (name, step)
        else:
            signal = None
        seg["queue"][engine].append((make, waits, signal))
        return mark

    def run(self, engine, eng):
        for at, seg in enumerate(self.segments):
            queue = seg["queue"][engine]
            if not queue:
                continue
            if seg["trips"] == 1:
                self.issue(engine, eng, at, seg, queue, 0)
            else:
                with eng.Fori(0, seg["trips"]) as i:
                    self.issue(engine, eng, at, seg, queue, i)

    def issue(self, engine, eng, at, seg, queue, i):
        looped = seg["trips"] > 1
        seen = {}

        def wait(name, value, per_trip):
            eng.wait_ge(self.sems[name], i * per_trip + value if looped and per_trip else value)

        if engine != "sync":
            for other in ENGINES[1:]:
                start, per_trip = seg["base"].get(other, 0), seg["count"].get(other, 0)
                if start or (looped and per_trip):
                    wait(other, start, per_trip)
        for make, waits, signal in queue:
            need = {}
            for where, name, k in waits:
                if where == at:
                    need[(name, True)] = max(need.get((name, True), 0), k)
                elif name not in ENGINES[1:] or engine == "sync":
                    s = self.segments[where]
                    total = s["base"].get(name, 0) + (s["trips"] - 1) * s["count"][name] + k
                    need[(name, False)] = max(need.get((name, False), 0), total)
            for (name, here), k in need.items():
                if seen.get((name, here), 0) >= k:
                    continue
                seen[(name, here)] = k
                if here:
                    wait(name, seg["base"].get(name, 0) + k, seg["count"][name])
                else:
                    eng.wait_ge(self.sems[name], k)
            ins = make(eng, i)
            if signal:
                ins.then_inc(self.sems[signal[0]], signal[1])


class Ring:

    def __init__(self, buffers):
        self.buffers, self.at, self.busy = buffers, 0, [[] for _ in buffers]

    def take(self):
        n = self.at % len(self.buffers)
        self.at += 1
        freed, self.busy[n] = self.busy[n], []
        return n, self.buffers[n], freed

    def give(self, n, *marks):
        self.busy[n] += list(marks)


def build_program(nc, d, out, last_layer=12):
    ctx = ExitStack()
    with ctx:
        fl = Flow(nc, ctx)

        def sb(name, shape, dt=F32):
            return ctx.enter_context(nc.sbuf_tensor(name, shape, dt))

        def V(make, *after):
            return fl.put("vector", make, after)

        def A(make, *after):
            return fl.put("scalar", make, after)

        def G(make, *after):
            return fl.put("gpsimd", make, after)

        def M(make, *after, signal=True):
            return fl.put("tensor", make, others(after), sem=None if signal else False)

        def others(after):
            return [others(a) if isinstance(a, (list, tuple)) and not is_mark(a) else a for a in after
                    if not (is_mark(a) and a[1] == "tensor")]

        def is_mark(a):
            return isinstance(a, tuple) and len(a) == 3 and isinstance(a[1], str)

        def D(sem, dst, src, *after):
            return fl.put("sync", lambda e, i: e.dma_start(dst, src), after, sem=sem, step=16)

        def bc(ap, axis, n):
            ap = ap.unsqueeze(axis)
            shape = list(ap.shape)
            shape[axis] = n
            return ap.broadcast_to(shape)

        x = sb("x", [P, T])
        xnT = sb("xnT", [P, T])
        ctxT = sb("ctxT", [P, T])
        bufA = sb("bufA", [P, 2 * NE * FF])
        bufB = sb("bufB", [P, 2 * NE * FF])
        arena = sb("arena", [P, 19500])
        banks = [ctx.enter_context(nc.psum_tensor(f"bank{n}", [P, BANK], F32)) for n in range(8)]
        used = [0]

        def fresh():
            used[0] = 0

        def carve(*shape, parts=P):
            n = int(np.prod(shape))
            v = arena[0:parts, used[0]:used[0] + n]
            used[0] += n
            assert used[0] <= 19500, used[0]
            if len(shape) == 2:
                v = v.rearrange("p (a b) -> p a b", b=shape[1])
            elif len(shape) == 3:
                v = v.rearrange("p (a b c) -> p a b c", b=shape[1], c=shape[2])
            return v

        def loaded(names, sem):
            fl.semaphore(sem)
            tiles, mark = {}, None
            for n in names:
                shape = list(d[n].shape)
                tiles[n] = sb(f"w_{n}", shape)
                mark = D(sem, tiles[n][tuple(slice(None) for _ in shape)], d[n])
            return tiles, mark

        fl.segment("constants")
        fl.semaphore("in_x")
        m_x = D("in_x", x[:, :], d["x"])
        fl.semaphore("in_ctx")
        W = {}
        ready = {}
        for group, names in (
            ("L0_attn", ("L0_attn_Wq", "L0_attn_Wk", "L0_attn_Wv", "L0_attn_Wo", "L0_attn_WckR", "L0_attn_WcvR",
                         "L0_attn_WgR", "L0_attn_bg")),
            ("L0_xattn", ("L0_xattn_WqT", "L0_xattn_WkT", "L0_xattn_WvT", "L0_xattn_WoT")),
            ("L0_ffn", ("L0_ffn_gate_w", "L0_ffn_gate_b", "L0_ffn_b1T", "L0_ffn_b2")),
            ("L1_attn", ("L1_attn_WiT", "L1_attn_conv_w", "L1_attn_conv_b", "L1_attn_WgT", "L1_attn_bg",
                         "L1_attn_forget_base", "L1_attn_WoT")),
            ("L1_xattn", ("L1_xattn_WqT", "L1_xattn_WkT", "L1_xattn_WvT", "L1_xattn_bq8", "L1_xattn_bk8",
                          "L1_xattn_bv8")),
            ("L1_ffn", ("L1_ffn_Wg", "L1_ffn_bg", "L1_ffn_b1T", "L1_ffn_b2")),
            ("L2_attn", ("slopes",)),
            ("L2_xattn", ("L2_xattn_Wq", "L2_xattn_bq", "L2_xattn_Wk", "L2_xattn_bk", "L2_xattn_Wv",
                          "L2_xattn_bv", "L2_xattn_Wo", "L2_xattn_bo")),
            ("L2_ffn", ("L2_ffn_WrT", "L2_ffn_rb")),
            ("L3_attn", ("L3_attn_wqT", "L3_attn_bq", "L3_attn_bqrow", "L3_attn_wkT", "L3_attn_bk",
                         "L3_attn_wvT", "L3_attn_bv", "L3_attn_woT", "L3_attn_bo")),
            ("L3_xattn", ("L3_xattn_W1T", "L3_xattn_W2T", "L3_xattn_b")),
            ("L3_ffn", ("L3_ffn_wg_redT", "L3_ffn_wg", "L3_ffn_b1T", "L3_ffn_b2")),
        ):
            tiles, ready[group] = loaded(names, f"in_{group}")
            W.update(tiles)
            if group == "L0_attn":
                m_ctx = D("in_ctx", ctxT[:, :], d["ctxT"])
            if group == "L0_ffn":
                fl.semaphore("in_A")
                fl.semaphore("in_B")
                half = NE * FF
                D("in_A", bufA[:, 0:half], d["L0_ffn_w1"])
                m_A = D("in_A", bufA[:, half:2 * half], d["L0_ffn_w2"])
                D("in_B", bufB[:, 0:half], d["L1_ffn_W1"])
                m_B = D("in_B", bufB[:, half:2 * half], d["L1_ffn_W2"])
        pad_u8 = sb("pad_u8", [P, T], U8)
        fl.semaphore("in_pad")
        m_pad = D("in_pad", pad_u8[:, :], d["mask"].partition_broadcast(P))

        ident = sb("ident", [P, P])
        mask16 = sb("mask16", [P, H])
        mask4 = sb("mask4", [P, 4])
        causal = sb("causal", [P, P])
        window = sb("window", [P, P])
        tri = sb("tri", [P, P])
        blk01 = sb("blk01", [P, NBLK])
        blkneg = sb("blkneg", [P, NBLK])
        anyblk = sb("anyblk", [P, 1])
        below = sb("below", [P, 8, 8])
        nm7 = sb("nm7", [P, 8])

        def select(t, pattern, base, mult, op, fill, *after):
            return G(lambda e, i: e.affine_select(out=t, in_=t, compare_op=op, fill=fill, base=base,
                                                  pattern=pattern, channel_multiplier=mult), *after)

        def filled(t, v):
            return G(lambda e, i: e.memset(t, v))

        select(ident[:, :], [[-1, P]], 0, 1, ALU.not_equal, 1.0, filled(ident[:, :], 0.0))
        m = filled(mask16[:, :], 1.0)
        m = select(mask16[:, :], [[-HD, H]], 0, 1, ALU.is_ge, 0.0, m)
        m16 = select(mask16[:, :], [[HD, H]], HD - 1, -1, ALU.is_ge, 0.0, m)
        V(lambda e, i: e.tensor_reduce(mask4[:, :], mask16[:, :].rearrange("p (g j) -> p j g", j=4),
                                       AX.X, ALU.add), m16)
        select(causal[:, :], [[-1, P]], 0, 1, ALU.is_ge, -BIG, filled(causal[:, :], 0.0))
        m = select(window[:, :], [[-1, P]], 0, 1, ALU.is_ge, -BIG, filled(window[:, :], 0.0))
        select(window[:, :], [[1, P]], WIN, -1, ALU.is_ge, -BIG, m)
        select(tri[:, :], [[1, P]], 0, -1, ALU.is_ge, 0.0, filled(tri[:, :], 1.0))
        select(blk01[:, :], [[-G0, NBLK]], -G0, 1, ALU.is_ge, 0.0, filled(blk01[:, :], 1.0))
        select(blkneg[:, :], [[-G0, NBLK]], -G0, 1, ALU.is_ge, NEG, filled(blkneg[:, :], 0.0))
        select(anyblk[:, :], [[0, 1]], -G0, 1, ALU.is_ge, 0.0, filled(anyblk[:, :], 1.0))
        select(below[:, :, :], [[1, 8], [-1, 8]], 0, 0, ALU.is_gt, 0.0, filled(below[:, :, :], 1.0))
        G(lambda e, i: e.iota(nm7[:, :], pattern=[[1, 8]], base=-7, channel_multiplier=0,
                              allow_small_or_imprecise_dtypes=True))

        def b_(ap):
            return lambda b: ap[:, ds(b * P, P)]

        stat = [sb(f"stat{n}", [P, NB]) for n in range(3)]

        def normalise(name, *after, loads=()):
            last = end_marks(fl)
            fl.segment(name)
            marks = [D(sem, dst, d[src], last) for sem, dst, src in loads]
            fresh()
            x3 = x[:, :].rearrange("p (b f) -> p b f", f=P)
            xc, sq = carve(NB, P), carve(NB, P)
            mean, var, rstd = (s[:, :] for s in stat)
            m = V(lambda e, i: e.tensor_reduce(mean, x3, AX.X, ALU.add), *after)
            m = V(lambda e, i: e.tensor_scalar(mean, mean, 1.0 / P, None, ALU.mult), m)
            mc = V(lambda e, i: e.tensor_tensor(xc, x3, bc(mean, 2, P), ALU.subtract), m)
            m = V(lambda e, i: e.tensor_tensor(sq, xc, xc, ALU.mult), mc)
            m = V(lambda e, i: e.tensor_reduce(var, sq, AX.X, ALU.add), m)
            m = V(lambda e, i: e.tensor_scalar(var, var, 1.0 / P, EPS, ALU.mult, ALU.add), m)
            m = A(lambda e, i: e.activation(rstd, var, ACT.Sqrt), m)
            m = V(lambda e, i: e.reciprocal(rstd, rstd), m)
            for k in range(2):
                h = slice(4 * k, 4 * k + 4)
                mn = V(lambda e, i, h=h: e.tensor_tensor(xc[:, h, :], xc[:, h, :], bc(rstd[:, h], 2, P), ALU.mult), m)
                for b in range(4 * k, 4 * k + 4):
                    mt = M(lambda e, i, b=b: e.transpose(banks[b // 4][:, (b % 4) * P:(b % 4 + 1) * P],
                                                         xc[:, b, :], ident[:, :]), mn)
                evacuate(xnT[:, k * BANK:(k + 1) * BANK], banks[k][:, :], k, mt)
            fl.segment(name + ": work")
            fresh()
            return marks

        def evacuate(dst, src, turn, *after):
            if turn % 2:
                return V(lambda e, i: e.tensor_copy(dst, src), *after)
            return A(lambda e, i: e.activation(dst, src, ACT.Copy), *after)

        def project(dst, w, src, ring, bias=None, *after):
            marks = []
            for k in range(2):
                n, bank, freed = ring.take()
                c = slice(k * BANK, (k + 1) * BANK)
                m = M(lambda e, i, bank=bank, c=c: e.matmul(bank[:, :], w, src[:, c], start=True, stop=True),
                      freed, *after)
                if bias is None:
                    m = evacuate(dst[:, c], bank[:, :], k, m)
                else:
                    m = V(lambda e, i, bank=bank, c=c: e.tensor_scalar(dst[:, c], bank[:, :], bias, None, ALU.add), m)
                ring.give(n, m)
                marks.append(m)
            return marks

        def project_tokens(dst4, w, src, ring, bias=None, *after):
            marks = []
            for k in range(2):
                n, bank, freed = ring.take()
                for j in range(4):
                    c = (4 * k + j) * P
                    m = M(lambda e, i, bank=bank, j=j, c=c: e.matmul(bank[:, j * P:(j + 1) * P], src[:, c:c + P], w,
                                                                      start=True, stop=True), freed, *after)
                dst, view = dst4(k, bank)
                if bias is None:
                    m = evacuate(dst, view, k, m)
                else:
                    m = V(lambda e, i, dst=dst, view=view: e.tensor_tensor(dst, view, bias, ALU.add), m)
                ring.give(n, m)
                marks.append(m)
            return marks

        def heads_with_ones():
            v = carve(NB * H, HD + 1)
            m = G(lambda e, i: e.memset(v[:, :, HD:HD + 1], 1.0))

            def dst4(k, bank):
                return (v[:, 4 * H * k:4 * H * (k + 1), 0:HD], bank[:, :].rearrange("p (a c) -> p a c", c=HD))
            return v, dst4, m

        def ranked(v, rows, keep, ge, tmp, r1, r2, *after):
            big = [P, rows, 8, 8]
            m = V(lambda e, i: e.tensor_tensor(tmp, v.unsqueeze(2).broadcast_to(big),
                                               v.unsqueeze(3).broadcast_to(big), ALU.is_ge), *after)
            m = V(lambda e, i: e.tensor_tensor(tmp, tmp, below[:, :, :].unsqueeze(1).broadcast_to(big), ALU.mult), m)
            m1 = V(lambda e, i: e.tensor_reduce(r1, tmp, AX.X, ALU.add), m)
            m2 = V(lambda e, i: e.tensor_reduce(r2, tmp.rearrange("p r n m -> p r m n"), AX.X, ALU.add), m)
            m = V(lambda e, i: e.tensor_tensor(r1, r1, r2, ALU.subtract), m1, m2)
            m = V(lambda e, i: e.tensor_tensor(r1, r1, bc(nm7[:, :], 1, rows), ALU.subtract), m)
            return V(lambda e, i: e.tensor_scalar(keep, r1, ge - 0.5, None, ALU.is_lt), m)

        def staircase(n, *stages):
            state = [None] * n
            for step in range(n + len(stages) - 1):
                for s, stage in enumerate(stages):
                    k = step - s
                    if 0 <= k < n:
                        state[k] = stage(k, state[k])

        def softmax_ready(tile, heads, scale, mx, *after):
            m = V(lambda e, i: e.tensor_reduce(mx, tile, AX.X, ALU.max), *after)
            m = V(lambda e, i: e.tensor_tensor(tile, tile, bc(mx, 2, P), ALU.subtract), m)
            return A(lambda e, i: e.activation(tile, tile, ACT.Exp, scale=scale), m)

        def turned(ring_t, ring_p, tile, turn, *after):
            n, bank, freed = ring_t.take()
            for j in range(4):
                m = M(lambda e, i, j=j: e.transpose(bank[:, j * P:(j + 1) * P], tile[:, j * P:(j + 1) * P], ident[:, :]),
                      freed, *after)
            q, dst, freed = ring_p.take()
            c = evacuate(dst, bank[:, :], turn, m, freed)
            ring_t.give(n, c)
            return q, dst, m, c

        def add_projected(b, o, area, oT, w, *after, bias=None):
            m = M(lambda e, i: e.transpose(area[:, 0:P], o, ident[:, :]), *after)
            m = A(lambda e, i: e.activation(oT, area[:, 0:P], ACT.Copy), m)
            m = M(lambda e, i: e.matmul(area[:, P:2 * P], oT, w, start=True, stop=True), m)
            m = V(lambda e, i: e.tensor_tensor(b_(x)(b(i)), b_(x)(b(i)), area[:, P:2 * P], ALU.add), m)
            if bias is not None:
                m = V(lambda e, i: e.tensor_tensor(b_(x)(b(i)), b_(x)(b(i)), bias, ALU.add), m)
            return m

        def attention(name, qT, kT, v, mask, wo, bias=None, keep=None):
            fl.segment(name, NB // 2)
            scale = 1.0 / float(np.sqrt(HD))
            qb = [carve(P) for _ in range(2)]
            kM = [carve(4, P) for _ in range(2)]
            o, oT, rs = ([carve(n) for _ in range(2)] for n in (P, P, H))
            ring_s, ring_t = Ring(banks[0:3]), Ring(banks[3:6])
            ring_a, ring_p = Ring([carve(BANK) for _ in range(3)]), Ring([carve(BANK) for _ in range(3)])
            mxs = [carve(4) for _ in range(8)]
            bat = [lambda i: i * 2, lambda i: i * 2 + 1]
            staged = []
            for u in range(2):
                m1 = G(lambda e, i, u=u: e.tensor_copy(qb[u], b_(qT)(bat[u](i))))
                m2 = V(lambda e, i, u=u: e.tensor_tensor(kM[u], b_(kT)(bat[u](i)).unsqueeze(1).broadcast_to([P, 4, P]),
                                                         bc(mask4[:, :], 2, P), ALU.mult))
                staged.append([m1, m2])

            def score(k, _):
                u, g = divmod(k, 4)
                q = slice(32 * g, 32 * g + 32)
                n, bank, freed = ring_s.take()
                m = M(lambda e, i: e.matmul(bank[:, :], qb[u][q, :], kM[u][q, :, :].rearrange("p j t -> p (j t)"),
                                            start=True, stop=True), freed, staged[u])
                a, tile, freed = ring_a.take()
                t3 = tile.rearrange("p (j t) -> p j t", t=P)
                s3 = bank[:, :].rearrange("p (j t) -> p j t", t=P)
                if mask is not None:
                    m = V(lambda e, i: e.tensor_tensor(t3, s3, bc(mask, 1, 4), ALU.add), m, freed)
                else:
                    m = V(lambda e, i: e.tensor_copy(t3, s3), m, freed)
                ring_s.give(n, m)
                return a, tile, softmax_ready(t3, 4, scale, mxs[k], m)

            def turn(k, s):
                a, tile, m = s
                q, pT, mt, mc = turned(ring_t, ring_p, tile, 0, m)
                ring_a.give(a, mt)
                return q, pT, mc

            def values(k, s):
                u, g = divmod(k, 4)
                q, pT, m = s
                bank = banks[6 + u]
                for j in range(4):
                    h = 4 * g + j
                    m = M(lambda e, i, h=h, j=j: e.matmul(
                        bank[:, h * 9:h * 9 + 9], pT[:, j * P:(j + 1) * P],
                        v[:, ds(bat[u](i) * H + h, 1), :].rearrange("p a c -> p (a c)"), start=True, stop=True), m)
                ring_p.give(q, m)
                if g == 3:
                    o3 = bank[:, 0:9 * H].rearrange("p (h c) -> p h c", c=9)
                    m = V(lambda e, i: e.reciprocal(rs[u].unsqueeze(2), o3[:, :, HD:HD + 1]), m)
                    if keep is not None:
                        m = V(lambda e, i: e.tensor_tensor(rs[u], rs[u], keep(bat[u](i)), ALU.mult), m)
                    m = V(lambda e, i: e.tensor_tensor(o[u].rearrange("p (h c) -> p h c", c=HD), o3[:, :, 0:HD],
                                                       bc(rs[u], 2, HD), ALU.mult), m)
                    add_projected(bat[u], o[u], bank[:, 144:144 + 2 * P], oT[u], wo, m, bias=bias)

            staircase(8, score, turn, values)

        def add_expert_bias(comb, b2, *after):
            cT = carve(T, parts=NE)
            for k in range(2):
                for j in range(4):
                    m = M(lambda e, i, k=k, j=j: e.transpose(banks[k][0:NE, j * P:(j + 1) * P], comb[:, 4 * k + j, :],
                                                             ident[:, :]), *after)
                m = evacuate(cT[:, k * BANK:(k + 1) * BANK], banks[k][0:NE, :], 0, m)
                for j in range(4):
                    c = (4 * k + j) * P
                    m = M(lambda e, i, k=k, j=j, c=c: e.matmul(banks[2 + k][:, j * P:(j + 1) * P], cT[:, c:c + P], b2,
                                                               start=True, stop=True), m)
                xs = x[:, k * BANK:(k + 1) * BANK]
                V(lambda e, i, k=k, xs=xs: e.tensor_tensor(xs, xs, banks[2 + k][:, :], ALU.add), m)

        def experts(name, comb, w1, w2, b1, buf_ready):
            fl.segment(name, NE // 2)
            NF = FF // P
            w1s, w2s = ([carve(FF) for _ in range(2)] for _ in range(2))
            b1s, cs = [carve(NF) for _ in range(2)], [carve(NB) for _ in range(2)]
            ring_h, ring_y = Ring(banks[0:4]), Ring(banks[4:8])
            ring_a = Ring([carve(NF, BANK) for _ in range(2)])
            staged = []
            for u in range(2):
                m = [G(lambda e, i, u=u: e.tensor_copy(w1s[u], w1[:, ds((i * 2 + u) * FF, FF)]), buf_ready),
                     G(lambda e, i, u=u: e.tensor_copy(b1s[u], b1[:, ds((i * 2 + u) * NF, NF)])),
                     G(lambda e, i, u=u: e.tensor_copy(w2s[u], w2[:, ds((i * 2 + u) * FF, FF)])),
                     G(lambda e, i, u=u: e.tensor_copy(cs[u].unsqueeze(2), comb[:, :, ds(i * 2 + u, 1)]))]
                staged.append(m)

            def up(k, _):
                u, t = divmod(k, 2)
                a, h, freed_h = ring_a.take()
                marks = []
                for f in range(NF):
                    n, bank, freed = ring_h.take()
                    m = M(lambda e, i, bank=bank, f=f: e.matmul(bank[:, :], w1s[u][:, f * P:(f + 1) * P],
                                                               xnT[:, t * BANK:(t + 1) * BANK], start=True, stop=True),
                          freed, staged[u][0])
                    m = A(lambda e, i, bank=bank, f=f: e.activation(h[:, f, :], bank[:, :], ACT.Gelu,
                                                                   bias=b1s[u][:, f:f + 1]), m, staged[u][1], freed_h)
                    ring_h.give(n, m)
                return a, h, m

            def down(k, s):
                u, t = divmod(k, 2)
                a, h, m = s
                n, bank, freed = ring_y.take()
                for j in range(4):
                    for f in range(NF):
                        my = M(lambda e, i, j=j, f=f: e.matmul(bank[:, j * P:(j + 1) * P], h[:, f, j * P:(j + 1) * P],
                                                               w2s[u][:, f * P:(f + 1) * P], start=f == 0,
                                                               stop=f == NF - 1), freed, m, staged[u][2],
                               signal=f == NF - 1)
                for j in range(4):
                    xs = x[:, (4 * t + j) * P:(4 * t + j + 1) * P]
                    c = cs[u][:, 4 * t + j:4 * t + j + 1]
                    mv = V(lambda e, i, j=j, xs=xs, c=c: e.scalar_tensor_tensor(
                        xs, bank[:, j * P:(j + 1) * P], c, xs, ALU.mult, ALU.add), my, staged[u][3],
                        last_x.get((t, j)))
                    last_x[(t, j)] = mv
                ring_a.give(a, my)
                ring_y.give(n, mv)

            last_x = {}
            staircase(4, up, down)

        def token_logits(w, width, src=None, *after):
            src = xnT if src is None else src
            for b in range(NB):
                m = M(lambda e, i, b=b: e.matmul(banks[7][:, b * width:(b + 1) * width], src[:, b * P:(b + 1) * P], w,
                                                 start=True, stop=True), *after)
            return banks[7][:, 0:NB * width].rearrange("p (b c) -> p b c", c=width), m

        def soft8(v, out, mx, sm, m, keep=None):
            m = V(lambda e, i: e.tensor_reduce(mx, v, AX.X, ALU.max), m)
            m = V(lambda e, i: e.tensor_tensor(out, v, bc(mx, 2, NE), ALU.subtract), m)
            m = A(lambda e, i: e.activation(out, out, ACT.Exp), m)
            if keep is not None:
                m = V(lambda e, i: e.tensor_tensor(out, out, keep, ALU.mult), m)
            m = V(lambda e, i: e.tensor_reduce(sm, out, AX.X, ALU.add), m)
            m = V(lambda e, i: e.reciprocal(sm, sm), m)
            return V(lambda e, i: e.tensor_tensor(out, out, bc(sm, 2, NE), ALU.mult), m)

        gate = dict(v=sb("gate_v", [P, NB, NE]), c=sb("gate_comb", [P, NB, NE]), r1=sb("gate_r1", [P, NB, NE]),
                    r2=sb("gate_r2", [P, NB, NE]), k=sb("gate_keep", [P, NB, NE]), mx=sb("gate_mx", [P, NB]),
                    sm=sb("gate_sm", [P, NB]), t=sb("gate_pairs", [P, NB, NE, NE]))
        gv, gc, gr1, gr2, gk = (gate[n][:, :, :] for n in ("v", "c", "r1", "r2", "k"))
        gmx, gsm, gt = gate["mx"][:, :], gate["sm"][:, :], gate["t"][:, :, :, :]
        x3 = x[:, :].rearrange("p (b f) -> p b f", f=P)

        ckT, cvT = sb("ckT", [P, NB * NBLK]), sb("cvT", [P, NB * NBLK])

        def layer0_attention():
            normalise("L0_attn", m_x)
            ring = Ring(banks)
            w = {n: W[f"L0_attn_{n}"] for n in ("Wq", "Wk", "Wv", "Wo", "WckR", "WcvR", "WgR", "bg")}
            lw = ready["L0_attn"]
            qT, kT, vT = carve(T), carve(T), carve(T)
            mq = project(qT, w["Wq"][:, :], xnT, ring, None, lw)
            mk = project(kT, w["Wk"][:, :], xnT, ring, None, lw)
            mv = project(vT, w["Wv"][:, :], xnT, ring, None, lw)
            v, dst4, ones = heads_with_ones()
            project_tokens(dst4, w["Wv"][:, :], xnT, ring, None, lw)
            comp = {}
            for n, src, ms in (("WckR", kT, mk), ("WcvR", vT, mv)):
                diag = carve(G0 * H * HD)
                wr = w[n][:, :].rearrange("p (g c) -> p g c", c=HD)
                shape = [P, G0, H, HD]
                md = V(lambda e, i, diag=diag, wr=wr: e.tensor_tensor(
                    diag.rearrange("p (g h c) -> p g h c", h=H, c=HD), wr.unsqueeze(2).broadcast_to(shape),
                    bc(mask16[:, :], 1, G0).unsqueeze(3).broadcast_to(shape), ALU.mult), lw)
                k, bank, freed = ring.take()
                for g in range(G0):
                    m = M(lambda e, i, diag=diag, src=src, bank=bank, g=g: e.matmul(
                        bank[:, 0:NB * NBLK], diag[:, g * P:(g + 1) * P],
                        src.rearrange("p (n g) -> p g n", g=G0)[:, g, :], start=g == 0, stop=g == G0 - 1),
                        freed, md, ms, signal=g == G0 - 1)
                comp[n] = (ckT, cvT)[n == "WcvR"][:, :]
                m = V(lambda e, i, dst=comp[n], bank=bank: e.tensor_copy(dst, bank[:, 0:NB * NBLK]), m)
                ring.give(k, m)

            fl.segment("L0_attn: batch", NB // 2)
            used[0] = 3 * T + NB * H * 9
            two = range(2)
            qb, o, oT, pc, pcT, vcBD, o2 = ([carve(P) for _ in two] for _ in range(7))
            kM = [carve(4, P) for _ in two]
            kcM, vcM, L, r1, r2, sel = ([carve(H, NBLK) for _ in two] for _ in range(6))
            pairs = [carve(H, NBLK * NBLK) for _ in range(1)]
            pairs = pairs[0].rearrange("p h (n m) -> p h n m", m=NBLK)
            rs, rl, mc, sc = ([carve(H) for _ in two] for _ in range(4))
            gl, gm = [carve(4) for _ in two], [carve(1) for _ in two]
            gs = [carve(1) for _ in two]
            ring_s, ring_t = Ring(banks[0:2]), Ring(banks[2:4])
            ring_a, ring_p = Ring([carve(BANK) for _ in range(4)]), Ring([carve(BANK) for _ in range(3)])
            mxs = [carve(4) for _ in range(16)]
            bat = [lambda i: i * 2, lambda i: i * 2 + 1]
            scale = 1.0 / float(np.sqrt(HD))
            staged, chosen, coarse, gates = [], [None] * 2, [None] * 2, [None] * 2
            pairs_free = [None]
            for u in two:
                m1 = G(lambda e, i, u=u: e.tensor_copy(qb[u], b_(qT)(bat[u](i))))
                m2 = V(lambda e, i, u=u: e.tensor_tensor(kM[u], b_(kT)(bat[u](i)).unsqueeze(1).broadcast_to([P, 4, P]),
                                                         bc(mask4[:, :], 2, P), ALU.mult))
                m3 = [V(lambda e, i, u=u, s=s, t=t: e.tensor_tensor(
                    t[u], s[:, ds(bat[u](i) * NBLK, NBLK)].unsqueeze(1).broadcast_to([P, H, NBLK]),
                    bc(mask16[:, :], 2, NBLK), ALU.mult)) for s, t in ((ckT, kcM), (cvT, vcM))]
                staged.append([m1, m2, m3])

            def compressed(u):
                aux = banks[6 + u]
                m1, _, m3 = staged[u]
                ms = M(lambda e, i: e.matmul(aux[:, 0:P], qb[u], kcM[u].rearrange("p h n -> p (h n)"),
                                             start=True, stop=True), m1, m3)
                mg = M(lambda e, i: e.matmul(aux[:, P:P + 3], qb[u], w["WgR"][:, :], start=True, stop=True), m1)
                mv = M(lambda e, i: e.transpose(aux[:, 2 * P:3 * P], vcM[u].rearrange("p h n -> p (h n)"),
                                                ident[:, :]), m3)
                mv = A(lambda e, i: e.activation(vcBD[u], aux[:, 2 * P:3 * P], ACT.Copy), mv)
                a3 = aux[:, 0:P].rearrange("p (h n) -> p h n", n=NBLK)
                m = V(lambda e, i: e.scalar_tensor_tensor(L[u], a3, scale, bc(blk01[:, :], 1, H), ALU.mult,
                                                          ALU.mult), ms, mv)
                g3 = gl[u][:, 0:3]
                mg = V(lambda e, i: e.scalar_tensor_tensor(g3, aux[:, P:P + 3], 1.0 / H, w["bg"][:, :], ALU.mult,
                                                           ALU.add), mg, mv)
                ml = V(lambda e, i: e.tensor_tensor(L[u], L[u], bc(blkneg[:, :], 1, H), ALU.add), m)
                m = ranked(L[u], H, sel[u], TOP_BLOCKS, pairs, r1[u], r2[u], ml, pairs_free[0])
                pairs_free[0] = m
                chosen[u] = V(lambda e, i: e.tensor_scalar(sel[u], sel[u], 1.0, BIG, ALU.subtract, ALU.mult), m)
                m = V(lambda e, i: e.tensor_reduce(mc[u], L[u], AX.X, ALU.max), ml)
                m = V(lambda e, i: e.tensor_tensor(L[u], L[u], bc(mc[u], 2, NBLK), ALU.subtract), m)
                p3 = pc[u].rearrange("p (h n) -> p h n", n=NBLK)
                me = A(lambda e, i: e.activation(p3, L[u], ACT.Exp), m)
                m = V(lambda e, i: e.tensor_reduce(sc[u], p3, AX.X, ALU.add), me)
                m = V(lambda e, i: e.reciprocal(sc[u], sc[u]), m)
                m = V(lambda e, i: e.tensor_tensor(p3, p3, bc(sc[u], 2, NBLK), ALU.mult), m)
                m = M(lambda e, i: e.transpose(aux[:, 3 * P:4 * P], pc[u], ident[:, :]), m, mg)
                m = A(lambda e, i: e.activation(pcT[u], aux[:, 3 * P:4 * P], ACT.Copy), m)
                coarse[u] = M(lambda e, i: e.matmul(aux[:, 0:P], pcT[u], vcBD[u], start=True, stop=True), m, mv, ml)
                m = V(lambda e, i: e.tensor_reduce(gm[u], g3, AX.X, ALU.max), mg)
                m = V(lambda e, i: e.tensor_scalar(g3, g3, gm[u], None, ALU.subtract), m)
                m = A(lambda e, i: e.activation(g3, g3, ACT.Exp), m)
                m = V(lambda e, i: e.tensor_reduce(gs[u], g3, AX.X, ALU.add), m)
                m = V(lambda e, i: e.reciprocal(gs[u], gs[u]), m)
                m = V(lambda e, i: e.tensor_scalar(g3, g3, gs[u], None, ALU.mult), m)
                gates[u] = V(lambda e, i: e.tensor_tensor(gl[u][:, 0:1], gl[u][:, 0:1], anyblk[:, :], ALU.mult), m)

            compressed(0)
            compressed(1)

            def score(k, _):
                u, g, local = k // 8, k % 8 // 2, k % 2
                q = slice(32 * g, 32 * g + 32)
                if not local:
                    n, bank, freed = ring_s.take()
                    m = M(lambda e, i: e.matmul(bank[:, :], qb[u][q, :], kM[u][q, :, :].rearrange("p j t -> p (j t)"),
                                                start=True, stop=True), freed, staged[u][0:2])
                    scores[0] = n, bank, m
                n, bank, m = scores[0]
                a, tile, freed = ring_a.take()
                t3 = tile.rearrange("p (j t) -> p j t", t=P)
                s3 = bank[:, :].rearrange("p (j t) -> p j t", t=P)
                mask = window if local else causal
                m = V(lambda e, i: e.tensor_tensor(t3, s3, bc(mask[:, :], 1, 4), ALU.add), m, freed)
                if local:
                    ring_s.give(n, m)
                else:
                    t4 = tile.rearrange("p (a c) -> p a c", c=G0)
                    s4 = sel[u][:, 4 * g:4 * g + 4, :].rearrange("p h n -> p (h n)")
                    m = G(lambda e, i: e.tensor_tensor(t4, t4, bc(s4, 2, G0), ALU.add), m, chosen[u])
                return a, tile, softmax_ready(t3, 4, scale, mxs[k], m)

            def turn(k, s):
                a, tile, m = s
                q, pT, mt, mcp = turned(ring_t, ring_p, tile, 0, m)
                ring_a.give(a, mt)
                return q, pT, mcp

            def values(k, s):
                u, g, local = k // 8, k % 8 // 2, k % 2
                q, pT, m = s
                bank = banks[4 + u]
                for j in range(4):
                    h = 4 * g + j
                    c = local * 144 + h * 9
                    m = M(lambda e, i, h=h, j=j, c=c: e.matmul(
                        bank[:, c:c + 9], pT[:, j * P:(j + 1) * P],
                        v[:, ds(bat[u](i) * H + h, 1), :].rearrange("p a c -> p (a c)"), start=True, stop=True), m)
                ring_p.give(q, m)
                if k % 8 == 7:
                    so = bank[:, 0:144].rearrange("p (h c) -> p h c", c=9)
                    lo = bank[:, 144:288].rearrange("p (h c) -> p h c", c=9)
                    parts = []
                    for r, src, gi, dst in ((rs[u], so, 1, o[u]), (rl[u], lo, 2, o2[u])):
                        mm = V(lambda e, i, r=r, src=src: e.reciprocal(r.unsqueeze(2), src[:, :, HD:HD + 1]), m)
                        mm = V(lambda e, i, r=r, gi=gi: e.tensor_scalar(r, r, gl[u][:, gi:gi + 1], None, ALU.mult),
                               mm, gates[u])
                        parts.append(V(lambda e, i, r=r, src=src, dst=dst: e.tensor_tensor(
                            dst.rearrange("p (h c) -> p h c", c=HD), src[:, :, 0:HD], bc(r, 2, HD), ALU.mult), mm))
                    m = V(lambda e, i: e.tensor_tensor(o[u], o[u], o2[u], ALU.add), parts)
                    m = V(lambda e, i: e.scalar_tensor_tensor(o[u], banks[6 + u][:, 0:P], gl[u][:, 0:1], o[u],
                                                              ALU.mult, ALU.add), m, coarse[u])
                    add_projected(bat[u], o[u], banks[6 + u][:, P:3 * P], oT[u], w["Wo"][:, :], m)

            scores = [None]
            staircase(16, score, turn, values)

        def layer0_cross():
            normalise("L0_xattn")
            ring = Ring(banks)
            lw = [ready["L0_xattn"], m_ctx]
            qT, kT = carve(T), carve(T)
            project(qT, W["L0_xattn_WqT"][:, :], xnT, ring, None, lw)
            project(kT, W["L0_xattn_WkT"][:, :], ctxT, ring, None, lw)
            v, dst4, _ = heads_with_ones()
            project_tokens(dst4, W["L0_xattn_WvT"][:, :], ctxT, ring, None, lw)
            attention("L0_xattn: batch", qT, kT, v, causal[:, :], W["L0_xattn_WoT"][:, :])

        def mixture(name, gw, gb, top, w1, w2, b1, b2, buf_ready):
            normalise(name)
            lw = ready[name]
            lg, m = token_logits(gw[:, :], NE, None, lw)
            m = V(lambda e, i: e.tensor_tensor(gv, lg, gb, ALU.add), m)
            if top == "logits":
                mk = ranked(gv, NB, gk, 2, gt, gr1, gr2, m)
                m = soft8(gv, gc, gmx, gsm, mk, keep=gk)
            else:
                m = soft8(gv, gc, gmx, gsm, m)
                m = ranked(gc, NB, gk, 2, gt, gr1, gr2, m)
                m = V(lambda e, i: e.tensor_tensor(gc, gc, gk, ALU.mult), m)
                m = V(lambda e, i: e.tensor_reduce(gsm, gc, AX.X, ALU.add), m)
                m = V(lambda e, i: e.reciprocal(gsm, gsm), m)
                m = V(lambda e, i: e.tensor_tensor(gc, gc, bc(gsm, 2, NE), ALU.mult), m)
            add_expert_bias(gc, b2[:, :], m)
            experts(name + ": experts", gc, w1, w2, b1[:, :], buf_ready)

        def layer1_recurrence():
            normalise("L1_attn")
            lw = ready["L1_attn"]
            wi, cw, cb, wg, bg, fb, wo = (W[f"L1_attn_{n}"] for n in (
                "WiT", "conv_w", "conv_b", "WgT", "bg", "forget_base", "WoT"))
            two = range(2)
            C = HC
            gate_, u2, al, be = (carve(2, T, parts=C) for _ in range(4))
            up = carve(2 * NB, P + KC - 1, parts=C)
            sp = [carve(2, parts=C) for _ in range(5)]
            ring = Ring(banks)
            fbv = fb[:, :]
            z, s, s2, acc, num = sp
            m = V(lambda e, i: e.tensor_scalar(z, fbv, -1.0, None, ALU.mult), lw)
            m = V(lambda e, i: e.tensor_tensor(z, z, fbv, ALU.min), m)
            m = A(lambda e, i: e.activation(z, z, ACT.Exp), m)
            m = V(lambda e, i: e.tensor_scalar(s, z, 2.0, None, ALU.add), m)
            m = V(lambda e, i: e.reciprocal(s, s), m)
            m = V(lambda e, i: e.tensor_tensor(s, s, z, ALU.mult), m)
            m = V(lambda e, i: e.tensor_tensor(s2, s, s, ALU.mult), m)
            m = V(lambda e, i: e.tensor_scalar(acc, s2, 1.0 / 17, 1.0 / 15, ALU.mult, ALU.add), m)
            for k in (13, 11, 9, 7, 5, 3, 1):
                m = V(lambda e, i: e.tensor_tensor(acc, acc, s2, ALU.mult), m)
                m = V(lambda e, i, k=k: e.tensor_scalar(acc, acc, 1.0 / k, None, ALU.add), m)
            m = V(lambda e, i: e.tensor_tensor(acc, acc, s, ALU.mult), m)
            m = V(lambda e, i: e.tensor_scalar(num, fbv, 0.0, None, ALU.max), m)
            m = V(lambda e, i: e.scalar_tensor_tensor(acc, acc, 2.0, num, ALU.mult, ALU.add), m)
            m_sp = V(lambda e, i: e.tensor_scalar(acc, acc, -8.0, None, ALU.mult), m)
            m0 = G(lambda e, i: e.memset(up[:, :, 0:KC - 1], 0.0))
            conv = []
            for c in two:
                mu = []
                for k in two:
                    n, bank, freed = ring.take()
                    m = M(lambda e, i, bank=bank, c=c, k=k: e.matmul(
                        bank[0:C, :], wi[:, HID + c * C:HID + (c + 1) * C], xnT[:, k * BANK:(k + 1) * BANK],
                        start=True, stop=True), freed, lw)
                    m = A(lambda e, i, bank=bank, c=c, k=k: e.activation(
                        up[:, c * NB + 4 * k:c * NB + 4 * k + 4, KC - 1:KC - 1 + P],
                        bank[0:C, :].rearrange("p (b t) -> p b t", t=P), ACT.Copy), m)
                    ring.give(n, m)
                    mu.append(m)
                u3 = u2[:, c, :].rearrange("p (b t) -> p b t", t=P)
                uc = up[:, c * NB:(c + 1) * NB, :]
                m = V(lambda e, i, c=c, u3=u3, uc=uc: e.tensor_scalar(
                    u3, uc[:, :, 0:P], cw[:, c * KC:c * KC + 1], cb[:, c:c + 1], ALU.mult, ALU.add), mu, m0)
                for k in range(1, KC):
                    m = V(lambda e, i, c=c, k=k, u3=u3, uc=uc: e.scalar_tensor_tensor(
                        u3, uc[:, :, k:k + P], cw[:, c * KC + k:c * KC + k + 1], u3, ALU.mult, ALU.add), m)
                conv.append(m)
            for c in two:
                for k in two:
                    n, bank, freed = ring.take()
                    m = M(lambda e, i, bank=bank, c=c, k=k: e.matmul(
                        bank[0:C, :], wi[:, c * C:(c + 1) * C], xnT[:, k * BANK:(k + 1) * BANK],
                        start=True, stop=True), freed)
                    m = A(lambda e, i, bank=bank, c=c, k=k: e.activation(
                        gate_[:, c, k * BANK:(k + 1) * BANK], bank[0:C, :], ACT.Gelu), m)
                    ring.give(n, m)
            sig = []
            for g in range(4):
                dst = (al, be)[g // 2][:, g % 2, :]
                for k in two:
                    n, bank, freed = ring.take()
                    for c in two:
                        m = M(lambda e, i, bank=bank, c=c, k=k, g=g: e.matmul(
                            bank[0:C, :], wg[:, c * 2 * HID + g * C:c * 2 * HID + (g + 1) * C],
                            u2[:, c, k * BANK:(k + 1) * BANK], start=c == 0, stop=c == 1), freed, conv)
                    m = A(lambda e, i, bank=bank, k=k, g=g, dst=dst: e.activation(
                        dst[:, k * BANK:(k + 1) * BANK], bank[0:C, :], ACT.Sigmoid, bias=bg[:, g:g + 1]), m)
                    ring.give(n, m)
                    sig.append(m)
            m_in = V(lambda e, i: e.tensor_tensor(be, be, u2, ALU.mult), sig)
            ma = [A(lambda e, i, c=c: e.activation(al[:, c, :], al[:, c, :], ACT.Exp, scale=acc[:, c:c + 1]),
                    sig, m_sp) for c in two]
            beta = carve(2, T, parts=C)
            m = V(lambda e, i: e.tensor_tensor(beta, al, al, ALU.mult), ma)
            m = V(lambda e, i: e.tensor_scalar(beta, beta, -1.0, 1.0, ALU.mult, ALU.add), m)
            m = V(lambda e, i: e.tensor_scalar(beta, beta, 1.0e-6, None, ALU.add), m)
            m = A(lambda e, i: e.activation(beta, beta, ACT.Sqrt), m)
            m_xt = V(lambda e, i: e.tensor_tensor(be, be, beta, ALU.mult), m, m_in)
            m_z = V(lambda e, i: e.memset(al.rearrange("p c (b t) -> p (c b) t", t=P)[:, :, 0:1], 0.0), ma, m_xt)
            hs = u2
            for c in two:
                m = V(lambda e, i, c=c: e.tensor_tensor_scan(hs[:, c, :], al[:, c, :], be[:, c, :], 0.0, ALU.mult,
                                                             ALU.add), m_z, m_xt)
                m_y = V(lambda e, i, c=c: e.tensor_tensor(hs[:, c, :], hs[:, c, :], gate_[:, c, :], ALU.mult), m)
            for k in two:
                n, bank, freed = ring.take()
                for j in range(4):
                    for c in two:
                        t0 = (4 * k + j) * P
                        m = M(lambda e, i, bank=bank, c=c, j=j, t0=t0: e.matmul(
                            bank[:, j * P:(j + 1) * P], hs[:, c, t0:t0 + P], wo[:, c * P:(c + 1) * P],
                            start=c == 0, stop=c == 1), freed, m_y)
                xs = x[:, k * BANK:(k + 1) * BANK]
                V(lambda e, i, xs=xs, bank=bank: e.tensor_tensor(xs, xs, bank[:, :], ALU.add), m)

        def layer1_cross():
            normalise("L1_xattn")
            lw = [ready["L1_xattn"], m_ctx]
            NP_ = 2 * H * P
            tiles = []
            ring = Ring(banks)
            for n, (wn, bn, src) in enumerate((("WqT", "bq8", xnT), ("WkT", "bk8", ctxT), ("WvT", "bv8", ctxT))):
                w, b8 = W[f"L1_xattn_{wn}"], W[f"L1_xattn_{bn}"]
                dst = carve(NP_)
                for f2 in range(H // 2):
                    k, bank, freed = ring.take()
                    for f in (2 * f2, 2 * f2 + 1):
                        f0 = min(8 * f, P - 32)
                        for g in range(4):
                            m = M(lambda e, i, bank=bank, f=f, g=g, w=w, src=src: e.matmul(
                                bank[32 * g:32 * g + 32, (f % 2) * 256:(f % 2) * 256 + 256], w[:, 8 * f:8 * f + 32],
                                src[:, 256 * g:256 * g + 256], start=True, stop=True), freed, lw)
                    view = dst.rearrange("p (t f) -> p f t", f=H)[:, 2 * f2:2 * f2 + 2, :]
                    bias = bc(b8[:, 2 * f2:2 * f2 + 2], 2, 256)
                    m = V(lambda e, i, bank=bank, view=view, bias=bias: e.tensor_tensor(
                        view, bank[:, :].rearrange("p (f t) -> p f t", f=2), bias, ALU.add), m)
                    ring.give(k, m)
                tiles.append(dst)
            fl.segment("L1_xattn: batch", 2)
            S2 = H * P
            scale = float(np.sqrt(HD))
            qs, ks, vs = (bufA[:, n * S2:(n + 1) * S2] for n in range(3))
            st = [G(lambda e, i: e.tensor_copy(qs, tiles[0][:, ds(i * S2, S2)])),
                  A(lambda e, i: e.activation(ks, tiles[1][:, ds(i * S2, S2)], ACT.Copy)),
                  G(lambda e, i: e.tensor_copy(vs, tiles[2][:, ds(i * S2, S2)]))]
            vh = [carve(H, HD + 1) for _ in range(4)]
            ring_s, ring_t = Ring(banks[0:2]), Ring(banks[2:5])
            ring_a = Ring([bufA[:, 3 * S2 + n * BANK:3 * S2 + (n + 1) * BANK] for n in range(3)])
            ring_p, o8 = Ring([carve(BANK) for _ in range(3)]), [carve(S2) for _ in range(2)]
            ring_o = Ring(banks[5:7])
            mask = [sb(f"l1mask{g}", [P, P])[:, :] for g in range(4)]
            rs = [sb(f"l1rs{g}", [P, H])[:, :] for g in range(4)]
            tmp = [sb(f"l1tmp{g}", [P, P])[:, :] for g in range(4)]
            mx = sb("l1mx", [P, 16 * 4])
            bat = [lambda i, g=g: i + 2 * g for g in range(4)]
            m_one = [G(lambda e, i, g=g: e.memset(vh[g][:, :, HD:HD + 1], 1.0)) for g in range(4)]
            mm = []
            for g in range(4):
                m = V(lambda e, i, g=g: e.scalar_tensor_tensor(
                    mask[g], pad_u8[:, ds(bat[g](i) * P, P)], -BIG, causal[:, :], ALU.mult, ALU.add), m_pad)
                mm.append(m)
                n, bank, freed = ring_o.take()
                for h in range(H):
                    m = M(lambda e, i, g=g, h=h, bank=bank: e.matmul(
                        bank[:, h * HD:(h + 1) * HD], vs[32 * g:32 * g + HD, h * P:(h + 1) * P],
                        ident[32 * g:32 * g + HD, 32 * g:32 * g + HD], start=True, stop=True), freed, st[2])
                m = V(lambda e, i, g=g, bank=bank: e.tensor_copy(
                    vh[g][:, :, 0:HD], bank[:, 0:P].rearrange("p (h c) -> p h c", c=HD)), m)
                ring_o.give(n, m)
                m_one[g] = [m_one[g], m]

            def score(k, _):
                g, hg = divmod(k, 4)
                n, bank, freed = ring_s.take()
                r = slice(32 * g, 32 * g + HD)
                for j in range(4):
                    c = slice((4 * hg + j) * P, (4 * hg + j + 1) * P)
                    m = M(lambda e, i, j=j, c=c: e.matmul(bank[:, j * P:(j + 1) * P], qs[r, c], ks[r, c],
                                                          start=True, stop=True), freed, st[0:2])
                a, tile, freed = ring_a.take()
                t3 = tile.rearrange("p (j t) -> p j t", t=P)
                s3 = bank[:, :].rearrange("p (j t) -> p j t", t=P)
                m = V(lambda e, i: e.tensor_tensor(t3, s3, bc(mask[g], 1, 4), ALU.add), m, freed, mm[g])
                ring_s.give(n, m)
                return a, tile, softmax_ready(t3, 4, scale, mx[:, 4 * k:4 * k + 4], m)

            def turn(k, s):
                a, tile, m = s
                q, pT, mt, mc = turned(ring_t, ring_p, tile, 0, m)
                ring_a.give(a, mt)
                return q, pT, mc

            def values(k, s):
                g, hg = divmod(k, 4)
                q, pT, m = s
                n, bank, freed = ring_o.take()
                for j in range(4):
                    h = 4 * hg + j
                    m = M(lambda e, i, j=j, h=h: e.matmul(bank[0:9, j * P:(j + 1) * P], vh[g][:, h, :],
                                                          pT[:, j * P:(j + 1) * P], start=True, stop=True),
                          m, freed, m_one[g])
                ring_p.give(q, m)
                dst = o8[g % 2][0:9, hg * BANK:(hg + 1) * BANK]
                m = A(lambda e, i: e.activation(dst, bank[0:9, :], ACT.Copy), m, o8_free[g % 2])
                ring_o.give(n, m)
                if hg == 3:
                    src = o8[g % 2][0:9, :].rearrange("p (t f) -> p f t", f=H)
                    n, bank = 0, banks[7]
                    for f in range(H):
                        m = M(lambda e, i, f=f: e.matmul(bank[:, f * 9:f * 9 + 9], src[:, f, :], ident[0:9, 0:9],
                                                         start=True, stop=True), m, b7_free)
                    o8_free[g % 2] = m
                    o3 = bank[:, 0:144].rearrange("p (f c) -> p f c", c=9)
                    m = V(lambda e, i: e.reciprocal(rs[g].unsqueeze(2), o3[:, :, HD:HD + 1]), m)
                    m = V(lambda e, i: e.tensor_tensor(tmp[g].rearrange("p (f c) -> p f c", c=HD), o3[:, :, 0:HD],
                                                       bc(rs[g], 2, HD), ALU.mult), m)
                    b7_free[:] = [m]
                    V(lambda e, i: e.tensor_tensor(b_(x)(bat[g](i)), b_(x)(bat[g](i)), tmp[g], ALU.add), m)

            o8_free, b7_free = [None, None], []
            staircase(16, score, turn, values)

        def layer2_attention():
            gu, dn = (NE + 1) * 2 * FI, (NE + 1) * 3 * FI
            marks = normalise("L2_attn", loads=[
                ("in_A", bufA[:, 0:4096], "L2_attn_Wqkv"), ("in_A", bufA[:, 4096:6144], "L2_attn_Wout"),
                ("in_B", bufB[:, 0:gu], "L2_ffn_Wgu"), ("in_B", bufB[:, gu:dn], "L2_ffn_Wd")])
            m_late["L2_ffn"] = marks[3]
            lw = [ready["L2_attn"], marks[1]]
            wq, wk, wv = bufA[:, 0:2048], bufA[:, 2048:3072], bufA[:, 3072:4096]
            wo = bufA[:, 4096:6144]
            bias = carve(QH, P)
            rel = carve(P)
            m = G(lambda e, i: e.iota(rel, pattern=[[1, P]], base=0, channel_multiplier=-1,
                                      allow_small_or_imprecise_dtypes=True))
            m = V(lambda e, i: e.tensor_tensor(bias, bc(rel, 1, QH), bc(W["slopes"][:, :], 2, P), ALU.mult), m, lw)
            V(lambda e, i: e.tensor_tensor(bias, bias, bc(causal[:, :], 1, QH), ALU.add), m)
            v = carve(KVH, DH + 1)
            G(lambda e, i: e.memset(v[:, :, DH:DH + 1], 1.0))
            fl.segment("L2_attn: batch", NB)
            xb = carve(P)
            qT, kT = carve(2 * NPAIR * P), carve(NPAIR * P)
            ring_s, ring_t, ring_o = Ring(banks[0:2]), Ring(banks[2:4]), Ring(banks[4:6])
            ring_a, ring_p = Ring([carve(BANK) for _ in range(3)]), Ring([carve(BANK) for _ in range(3)])
            oo, oT = [carve(2 * P) for _ in range(2)], [carve(2 * P) for _ in range(2)]
            rs, mxs = [carve(4) for _ in range(2)], [carve(4) for _ in range(8)]
            m_xb = A(lambda e, i: e.activation(xb, b_(xnT)(i), ACT.Copy))
            rings = [ring_s, ring_t, ring_o]
            mk, mq, mv = [], [], []
            turn_ = 0
            for n in range(2):
                r = rings[n % 3]
                k, bank, freed = r.take()
                m = M(lambda e, i, bank=bank, n=n: e.matmul(bank[:, :], xb, wv[:, n * BANK:(n + 1) * BANK],
                                                            start=True, stop=True), freed, m_xb, lw)
                m = evacuate(v[:, 8 * n:8 * n + 8, 0:DH], bank[:, :].rearrange("p (h c) -> p h c", c=DH), n, m)
                r.give(k, m)
                mv.append(m)
            for dst, w, count, marks in ((kT, wk, 2, mk), (qT, wq, 4, mq)):
                for n in range(count):
                    turn_ += 1
                    r = rings[turn_ % 3]
                    k, bank, freed = r.take()
                    for j in range(4):
                        c = (4 * n + j) * P
                        m = M(lambda e, i, bank=bank, j=j, c=c, w=w: e.matmul(
                            bank[:, j * P:(j + 1) * P], w[:, c:c + P], xb, start=True, stop=True), freed, m_xb)
                    m = evacuate(dst[:, n * BANK:(n + 1) * BANK], bank[:, :], turn_, m)
                    r.give(k, m)
                    marks.append(m)

            products = {}

            def score(k, _):
                if k % 2 == 0:
                    slots = [ring_s.take() for _ in range(2)]
                    for jj in range(2):
                        for s in range(2):
                            for r in range(2):
                                j = k + jj
                                p, c = slice(64 * r, 64 * r + 64), (2 * j + s) * P
                                n, bank, freed = slots[r]
                                at = (2 * jj + s) * P
                                products[k + r] = M(lambda e, i, p=p, c=c, j=j, at=at, bank=bank: e.matmul(
                                    bank[:, at:at + P], qT[p, c:c + P], kT[p, j * P:(j + 1) * P],
                                    start=True, stop=True), freed, mk[j // 4], mq[j // 2])
                    products["slots"] = slots
                n, bank, _ = products["slots"][k % 2]
                m = products[k]
                a, tile, freed = ring_a.take()
                bb = bias[:, 4 * k:4 * k + 4, :].rearrange("p h t -> p (h t)")
                m = V(lambda e, i: e.scalar_tensor_tensor(tile, bank[:, :], 1.0 / np.sqrt(DH).item(), bb, ALU.mult,
                                                          ALU.add), m, freed)
                ring_s.give(n, m)
                return a, tile, softmax_ready(tile.rearrange("p (j t) -> p j t", t=P), 4, 1.0, mxs[k], m)

            def turn(k, s):
                a, tile, m = s
                q, pT, mt, mc = turned(ring_t, ring_p, tile, 0, m)
                ring_a.give(a, mt)
                return q, pT, mc

            def values(k, s):
                q, pT, m = s
                n, bank, freed = ring_o.take()
                for hh in range(4):
                    m = M(lambda e, i, hh=hh: e.matmul(bank[:, hh * 65:hh * 65 + 65], pT[:, hh * P:(hh + 1) * P],
                                                       v[:, 2 * (2 * (k // 2) + hh // 2) + k % 2, :], start=True, stop=True), m, freed, mv)
                ring_p.give(q, m)
                o3 = bank[:, 0:260].rearrange("p (h c) -> p h c", c=65)
                u = k % 2
                m = V(lambda e, i: e.reciprocal(rs[u].unsqueeze(2), o3[:, :, DH:DH + 1]), m, rs_free[u])
                m = V(lambda e, i: e.tensor_tensor(oo[u].rearrange("p (h c) -> p h c", c=DH), o3[:, :, 0:DH],
                                                   bc(rs[u], 2, DH), ALU.mult), m, oo_free[u])
                rs_free[u] = m
                ring_o.give(n, m)
                return m

            def outputs(k, m):
                u = k % 2
                bank = banks[6]
                for j in range(2):
                    m = M(lambda e, i, j=j: e.transpose(bank[:, (2 * u + j) * P:(2 * u + j + 1) * P],
                                                        oo[u][:, j * P:(j + 1) * P], ident[:, :]), m, b6_free[0])
                oo_free[u] = m
                m = A(lambda e, i: e.activation(oT[u], bank[:, 2 * u * P:2 * (u + 1) * P], ACT.Copy), m, oT_free[u])
                b6_free[0] = m
                for j in range(2):
                    c = (2 * (2 * (k // 2) + j) + k % 2) * P
                    m = M(lambda e, i, j=j, c=c: e.matmul(banks[7][:, 0:P], oT[u][:, j * P:(j + 1) * P], wo[:, c:c + P],
                                                          start=k == j == 0, stop=k == NPAIR - 1 and j == 1), m)
                oT_free[u] = m
                if k == NPAIR - 1:
                    V(lambda e, i: e.tensor_tensor(b_(x)(i), b_(x)(i), banks[7][:, 0:P], ALU.add), m)

            rs_free, oo_free, b6_free, oT_free = ([None, None] for _ in range(4))
            staircase(NPAIR, score, turn, values, outputs)

        def layer2_cross():
            half = NE * FF
            marks = normalise("L2_xattn", loads=[("in_A", bufA[:, 0:half], "L3_ffn_w1"),
                                                 ("in_A", bufA[:, half:2 * half], "L3_ffn_w2")])
            m_late["L3_ffn"] = marks[1]
            w = {n: W[f"L2_xattn_{n}"] for n in ("Wq", "bq", "Wk", "bk", "Wv", "bv", "Wo", "bo")}
            lw = [ready["L2_xattn"], m_ctx]
            ring = Ring(banks)
            qT, kT, low = carve(T), carve(T), carve(T)
            v, dst4, _ = heads_with_ones()
            mv = project_tokens(dst4, w["Wv"][:, :], ctxT, ring,
                                w["bv"][:, :].rearrange("p (a c) -> p a c", c=HD), lw)
            m_low = None
            for dst, wn, bn, src in ((qT, "Wq", "bq", xnT), (kT, "Wk", "bk", ctxT)):
                m = project(dst, w[wn][:, :], src, ring, w[bn][:, 0:1], lw)
                m = V(lambda e, i, dst=dst: e.tensor_scalar(low, dst, 0.0, None, ALU.min), m, m_low)
                me = A(lambda e, i: e.activation(low, low, ACT.Exp), m)
                m_low = V(lambda e, i, dst=dst: e.scalar_tensor_tensor(dst, dst, 0.0, low, ALU.max, ALU.add), me)
            fl.segment("L2_xattn: batch", NB // 2)
            two = range(2)
            kb, qb, qtok, o, oT, zr = ([carve(P) for _ in two] for _ in range(6))
            qM = [carve(4, P) for _ in two]
            ring_s, ring_a = Ring(banks[0:4]), Ring([carve(BANK) for _ in range(4)])
            bat = [lambda i: i * 2, lambda i: i * 2 + 1]
            staged = []
            for u in two:
                m1 = G(lambda e, i, u=u: e.tensor_copy(kb[u], b_(kT)(bat[u](i))))
                m2 = V(lambda e, i, u=u: e.tensor_tensor(qM[u], b_(qT)(bat[u](i)).unsqueeze(1).broadcast_to([P, 4, P]),
                                                         bc(mask4[:, :], 2, P), ALU.mult))
                m3 = G(lambda e, i, u=u: e.tensor_copy(qb[u], b_(qT)(bat[u](i))))
                staged.append([m1, m2, m3])

            def running_sums(u):
                z = banks[6 + u]
                m = M(lambda e, i: e.transpose(z[:, 0:P], qb[u], ident[:, :]), staged[u][2])
                m = A(lambda e, i: e.activation(qtok[u], z[:, 0:P], ACT.Copy), m)
                m = M(lambda e, i: e.matmul(z[:, P:2 * P], tri[:, :], qtok[u], start=True, stop=True), m)
                return V(lambda e, i: e.reciprocal(zr[u], z[:, P:2 * P]), m)

            norms = [running_sums(u) for u in two]

            def score(k, _):
                u, g = divmod(k, 4)
                q = slice(32 * g, 32 * g + 32)
                n, bank, freed = ring_s.take()
                m = M(lambda e, i: e.matmul(bank[:, :], kb[u][q, :], qM[u][q, :, :].rearrange("p j t -> p (j t)"),
                                            start=True, stop=True), freed, staged[u][0:2])
                a, tile, freed = ring_a.take()
                m = V(lambda e, i: e.tensor_tensor(tile.rearrange("p (j t) -> p j t", t=P),
                                                   bank[:, :].rearrange("p (j t) -> p j t", t=P),
                                                   bc(tri[:, :], 1, 4), ALU.mult), m, freed)
                ring_s.give(n, m)
                return a, tile, m

            def values(k, s):
                u, g = divmod(k, 4)
                a, tile, m = s
                bank = banks[4 + u]
                for j in range(4):
                    h = 4 * g + j
                    m = M(lambda e, i, h=h, j=j: e.matmul(
                        bank[:, h * HD:(h + 1) * HD], tile[:, j * P:(j + 1) * P],
                        v[:, ds(bat[u](i) * H + h, 1), 0:HD].rearrange("p a c -> p (a c)"), start=True, stop=True), m)
                ring_a.give(a, m)
                if g == 3:
                    m = V(lambda e, i: e.tensor_tensor(o[u], bank[:, 0:P], zr[u], ALU.mult), m, norms[u])
                    add_projected(bat[u], o[u], bank[:, P:3 * P], oT[u], w["Wo"][:, :], m, bias=w["bo"][:, :])

            staircase(8, score, values)

        def layer2_experts():
            normalise("L2_ffn")
            lg, m = token_logits(W["L2_ffn_WrT"][:, :], NE, None, ready["L2_ffn"])
            m = V(lambda e, i: e.tensor_tensor(gv, lg, bc(W["L2_ffn_rb"][:, :], 1, NB), ALU.add), m)
            m = A(lambda e, i: e.activation(gv, gv, ACT.Sigmoid), m)
            m = ranked(gv, NB, gk, 2, gt, gr1, gr2, m)
            comb = carve(NE + 1, NB)
            V(lambda e, i: e.tensor_tensor(comb[:, 0:NE, :].rearrange("p e b -> p b e"), gv, gk, ALU.mult), m)
            G(lambda e, i: e.memset(comb[:, NE, :], 1.0))
            U = 3
            fl.segment("L2_ffn: experts", (NE + 1) // U)
            WU = 2 * FI
            wu, wd = bufB[:, 0:(NE + 1) * WU], bufB[:, (NE + 1) * WU:(NE + 1) * (WU + FI)]
            wus, wds, cs = [carve(WU) for _ in range(U)], [carve(FI) for _ in range(U)], [carve(NB) for _ in range(U)]
            ring_h, ring_y = Ring(banks[0:6]), Ring(banks[6:8])
            ring_a = Ring([carve(2, BANK) for _ in range(2)])
            ring_g = Ring([carve(BANK) for _ in range(2)])
            staged = []
            for u in range(U):
                staged.append([
                    G(lambda e, i, u=u: e.tensor_copy(wus[u], wu[:, ds((i * U + u) * WU, WU)]), m_late["L2_ffn"]),
                    G(lambda e, i, u=u: e.tensor_copy(wds[u], wd[:, ds((i * U + u) * FI, FI)])),
                    G(lambda e, i, u=u: e.tensor_copy(cs[u], comb[:, ds(i * U + u, 1), :].rearrange(
                        "p a b -> p (a b)")))])

            def up(k, _):
                u, t = divmod(k, 2)
                a, h, freed_h = ring_a.take()
                for f in range(2):
                    n1, bg_, freed1 = ring_h.take()
                    n2, bu_, freed2 = ring_h.take()
                    ms = []
                    for bank, c, fr in ((bg_, f * P, freed1), (bu_, FI + f * P, freed2)):
                        ms.append(M(lambda e, i, bank=bank, c=c: e.matmul(
                            bank[:, :], wus[u][:, c:c + P], xnT[:, t * BANK:(t + 1) * BANK], start=True, stop=True),
                            fr, staged[u][0]))
                    g, sg, freed = ring_g.take()
                    m = A(lambda e, i, sg=sg, bg_=bg_: e.activation(sg, bg_[:, :], ACT.Silu), ms[0], freed)
                    ring_h.give(n1, m)
                    m = V(lambda e, i, sg=sg, bu_=bu_, f=f: e.tensor_tensor(h[:, f, :], sg, bu_[:, :], ALU.mult),
                          m, ms[1], freed_h)
                    ring_h.give(n2, m)
                    ring_g.give(g, m)
                return a, h, m

            def down(k, s):
                u, t = divmod(k, 2)
                a, h, m = s
                n, bank, freed = ring_y.take()
                for j in range(4):
                    for f in range(2):
                        my = M(lambda e, i, j=j, f=f: e.matmul(bank[:, j * P:(j + 1) * P], h[:, f, j * P:(j + 1) * P],
                                                               wds[u][:, f * P:(f + 1) * P], start=f == 0, stop=f == 1),
                               freed, m, staged[u][1], signal=f == 1)
                for j in range(4):
                    xs = x[:, (4 * t + j) * P:(4 * t + j + 1) * P]
                    c = cs[u][:, 4 * t + j:4 * t + j + 1]
                    last_x[(t, j)] = mv = V(lambda e, i, j=j, xs=xs, c=c: e.scalar_tensor_tensor(
                        xs, bank[:, j * P:(j + 1) * P], c, xs, ALU.mult, ALU.add), my, staged[u][2],
                        last_x.get((t, j)))
                ring_a.give(a, my)
                ring_y.give(n, mv)

            last_x = {}
            staircase(2 * U, up, down)

        def layer3_attention():
            normalise("L3_attn")
            w = {n: W[f"L3_attn_{n}"] for n in ("wqT", "bq", "bqrow", "wkT", "bk", "wvT", "bv", "woT", "bo")}
            lw = ready["L3_attn"]
            ring = Ring(banks[0:7])
            qT, kT = carve(T), carve(T)
            project(qT, w["wqT"][:, :], xnT, ring, w["bq"][:, 0:1], lw)
            project(kT, w["wkT"][:, :], xnT, ring, w["bk"][:, 0:1], lw)
            v, dst4, _ = heads_with_ones()
            project_tokens(dst4, w["wvT"][:, :], xnT, ring, w["bv"][:, :].rearrange("p (a c) -> p a c", c=HD), lw)
            BH = NB * H
            keepT = carve(BH)
            q, t1, t2 = (carve(BH, HD) for _ in range(3))
            l2, mx, sm, en, mean, var = (carve(BH) for _ in range(6))

            def q4(k, bank):
                return q[:, 4 * H * k:4 * H * (k + 1), :], bank[:, :].rearrange("p (a c) -> p a c", c=HD)
            mq = project_tokens(q4, w["wqT"][:, :], xnT, ring, w["bqrow"][:, :].rearrange("p (a c) -> p a c", c=HD), lw)
            m = V(lambda e, i: e.tensor_tensor(t1, q, q, ALU.mult), mq)
            m = V(lambda e, i: e.tensor_reduce(l2, t1, AX.X, ALU.add), m)
            ml = A(lambda e, i: e.activation(l2, l2, ACT.Sqrt), m)
            m = V(lambda e, i: e.tensor_reduce(mean, q, AX.X, ALU.add), mq)
            m = V(lambda e, i: e.tensor_scalar(mean, mean, 1.0 / HD, None, ALU.mult), m)
            m = V(lambda e, i: e.tensor_tensor(t1, q, bc(mean, 2, HD), ALU.subtract), m)
            m = V(lambda e, i: e.tensor_tensor(t1, t1, t1, ALU.mult), m)
            m = V(lambda e, i: e.tensor_reduce(var, t1, AX.X, ALU.add), m)
            mvar = V(lambda e, i: e.tensor_scalar(var, var, 1.0 / (HD - 1), 0.2, ALU.mult, ALU.mult), m)
            m = V(lambda e, i: e.tensor_reduce(mx, q, AX.X, ALU.max), mq)
            mq2 = V(lambda e, i: e.tensor_tensor(q, q, bc(mx, 2, HD), ALU.subtract), m)
            m = A(lambda e, i: e.activation(t2, q, ACT.Exp), mq2)
            m = V(lambda e, i: e.tensor_reduce(sm, t2, AX.X, ALU.add), m)
            m = A(lambda e, i: e.activation(sm, sm, ACT.Ln), m)
            m = V(lambda e, i: e.tensor_tensor(q, q, bc(sm, 2, HD), ALU.subtract), m)
            me = A(lambda e, i: e.activation(t2, q, ACT.Exp), m)
            m = V(lambda e, i: e.tensor_scalar(t1, t2, 1.0e-9, None, ALU.add), me, mvar)
            m = A(lambda e, i: e.activation(t1, t1, ACT.Ln), m)
            m = V(lambda e, i: e.tensor_tensor(t1, t1, t2, ALU.mult), m)
            m = V(lambda e, i: e.tensor_reduce(en, t1, AX.X, ALU.add), m)
            m = V(lambda e, i: e.scalar_tensor_tensor(var, en, -0.3, var, ALU.mult, ALU.add), m, mvar)
            m = V(lambda e, i: e.scalar_tensor_tensor(var, l2, 0.5, var, ALU.mult, ALU.add), m, ml)
            m = M(lambda e, i: e.transpose(banks[7][:, 0:P], var, ident[:, :]), m)
            sc, sc2, iota, kp = (carve(P) for _ in range(4))
            c1 = [carve(1) for _ in range(4)]
            top, idf = carve(16), carve(16)
            idx = sb("top_index", [P, 16], U32)
            ms = V(lambda e, i: e.tensor_copy(sc, banks[7][:, 0:P]), m)
            mu, sd, fac, tmp = c1
            m = V(lambda e, i: e.tensor_reduce(mu, sc, AX.X, ALU.add), ms)
            m = V(lambda e, i: e.tensor_scalar(mu, mu, 1.0 / P, None, ALU.mult), m)
            m = V(lambda e, i: e.tensor_scalar(sc2, sc, mu, None, ALU.subtract), m)
            m = V(lambda e, i: e.tensor_tensor(sc2, sc2, sc2, ALU.mult), m)
            m = V(lambda e, i: e.tensor_reduce(sd, sc2, AX.X, ALU.add), m)
            m = V(lambda e, i: e.tensor_scalar(sd, sd, 1.0 / (P - 1), None, ALU.mult), m)
            m = A(lambda e, i: e.activation(sd, sd, ACT.Sqrt), m)
            m = V(lambda e, i: e.tensor_scalar(tmp, mu, 1.0e-6, None, ALU.add), m)
            m = V(lambda e, i: e.reciprocal(tmp, tmp), m)
            m = V(lambda e, i: e.scalar_tensor_tensor(fac, sd, tmp, sd, ALU.mult, ALU.bypass), m)
            m = V(lambda e, i: e.tensor_scalar(fac, fac, float(MAX_F), None, ALU.mult), m)
            m = V(lambda e, i: e.tensor_scalar(fac, fac, -100.0, 100.0, ALU.max, ALU.min), m)
            m = V(lambda e, i: e.tensor_scalar(fac, fac, 12582912.0, None, ALU.add), m)
            m = V(lambda e, i: e.tensor_scalar(fac, fac, 12582912.0, None, ALU.subtract), m)
            m = V(lambda e, i: e.tensor_scalar(fac, fac, float(MIN_F), float(MAX_F), ALU.max, ALU.min), m)
            pick, blk = carve(P), carve(P)
            mp = G(lambda e, i: e.memset(pick, 1.0))
            p3 = pick.rearrange("p (b h) -> p b h", h=H)
            mp = select(p3, [[-H, NB], [0, H]], 0, 1, ALU.is_equal, 0.0, mp)
            m = M(lambda e, i: e.matmul(banks[7][:, P:P + 1], pick, fac, start=True, stop=True), m, mp)
            mcount = V(lambda e, i: e.tensor_copy(fac, banks[7][:, P:P + 1]), m)
            m = V(lambda e, i: e.max(top[:, 0:8], sc), ms)
            m1 = V(lambda e, i: e.max_index(idx[:, 0:8], top[:, 0:8], sc), m)
            m = V(lambda e, i: e.match_replace(sc2, top[:, 0:8], sc, -3.0e38), m, m1)
            m2 = V(lambda e, i: e.max(top[:, 8:16], sc2), m)
            m2 = V(lambda e, i: e.max_index(idx[:, 8:16], top[:, 8:16], sc2), m2)
            m = V(lambda e, i: e.tensor_copy(idf, idx[:, :]), m1, m2)
            mi = G(lambda e, i: e.iota(iota, pattern=[[1, P]], base=0, channel_multiplier=0,
                                       allow_small_or_imprecise_dtypes=True))
            act = carve(16)
            for j in range(MAX_F):
                m = V(lambda e, i, j=j: e.tensor_scalar(act[:, j:j + 1], fac, float(j) + 0.5, 1000.0, ALU.is_lt,
                                                        ALU.mult), m, mcount)
            m = V(lambda e, i: e.tensor_tensor(idf[:, 0:MAX_F], idf[:, 0:MAX_F], act[:, 0:MAX_F], ALU.add), m)
            m = V(lambda e, i: e.tensor_scalar(kp, iota, idf[:, 0:1], None, ALU.is_equal), m, mi)
            for j in range(1, MAX_F):
                m = V(lambda e, i, j=j: e.scalar_tensor_tensor(kp, iota, idf[:, j:j + 1], kp, ALU.is_equal, ALU.add), m)
            m = M(lambda e, i: e.transpose(banks[7][:, 2 * P:3 * P], kp, ident[:, :]), m)
            V(lambda e, i: e.tensor_copy(keepT, banks[7][:, 2 * P:3 * P]), m)
            used[0] = 2 * T + NB * H * 9 + BH
            attention("L3_attn: batch", qT, kT, v, None, w["woT"][:, :], bias=w["bo"][:, :],
                      keep=lambda b: keepT[:, ds(b * H, H)])

        def layer3_cross():
            normalise("L3_xattn")
            lw = [ready["L3_xattn"], m_ctx]
            cs, cb = carve(NB), carve(NB, P)
            m = V(lambda e, i: e.tensor_reduce(cs, ctxT[:, :].rearrange("p (b t) -> p b t", t=P), AX.X, ALU.add), lw)
            m = V(lambda e, i: e.tensor_scalar(cs, cs, 1.0 / P, None, ALU.mult), m)
            mc = V(lambda e, i: e.tensor_copy(cb, bc(cs, 2, P)), m)
            for k in range(2):
                bank = banks[k]
                for j in range(4):
                    b = 4 * k + j
                    M(lambda e, i, b=b, j=j, bank=bank: e.matmul(bank[:, j * P:(j + 1) * P], xnT[:, b * P:(b + 1) * P],
                                                                 W["L3_xattn_W1T"][:, :], start=True, stop=False),
                      mc, lw, signal=False)
                    m = M(lambda e, i, b=b, j=j, bank=bank: e.matmul(bank[:, j * P:(j + 1) * P], cb[:, b, :],
                                                                     W["L3_xattn_W2T"][:, :], start=False, stop=True))
                xs = x[:, k * BANK:(k + 1) * BANK]
                m = V(lambda e, i, xs=xs, bank=bank: e.tensor_tensor(xs, xs, bank[:, :], ALU.add), m)
                V(lambda e, i, k=k: e.tensor_tensor(x3[:, 4 * k:4 * k + 4, :], x3[:, 4 * k:4 * k + 4, :],
                                                    bc(W["L3_xattn_b"][:, :], 1, 4), ALU.add), m)

        def layer3_experts():
            normalise("L3_ffn")
            lw = ready["L3_ffn"]
            GD = 16
            wg, wgT = W["L3_ffn_wg"], carve(NE, parts=GD)
            sq, nr = carve(GD, parts=NE), carve(1, parts=NE)
            m = V(lambda e, i: e.tensor_tensor(sq, wg[:, :], wg[:, :], ALU.mult), lw)
            m = V(lambda e, i: e.tensor_reduce(nr, sq, AX.X, ALU.add), m)
            m = A(lambda e, i: e.activation(nr, nr, ACT.Sqrt), m)
            m = V(lambda e, i: e.tensor_scalar(nr, nr, 1.0e-4, None, ALU.max), m)
            m = V(lambda e, i: e.reciprocal(nr, nr), m)
            m = V(lambda e, i: e.tensor_scalar(sq, wg[:, :], nr, None, ALU.mult), m)
            m = M(lambda e, i: e.transpose(banks[6][0:GD, 0:NE], sq, ident[0:NE, 0:NE]), m)
            mw = V(lambda e, i: e.tensor_copy(wgT, banks[6][0:GD, 0:NE]), m)
            xr = carve(T, parts=GD)
            mr = []
            for k in range(2):
                c = slice(k * BANK, (k + 1) * BANK)
                m = M(lambda e, i, k=k, c=c: e.matmul(banks[4 + k][0:GD, :], W["L3_ffn_wg_redT"][:, :], xnT[:, c],
                                                      start=True, stop=True), lw)
                mr.append(evacuate(xr[:, c], banks[4 + k][0:GD, :], k, m))
            lg, m = token_logits(wgT, NE, xr, mw, mr)
            m = V(lambda e, i: e.tensor_copy(gv, lg), m)
            m = soft8(gv, gc, gmx, gsm, m)
            m = ranked(gc, NB, gk, 1, gt, gr1, gr2, m)
            m = V(lambda e, i: e.tensor_tensor(gc, gc, gk, ALU.mult), m)
            add_expert_bias(gc, W["L3_ffn_b2"][:, :], m)
            half = NE * FF
            experts("L3_ffn: experts", gc, bufA[:, 0:half], bufA[:, half:2 * half], W["L3_ffn_b1T"][:, :], m_late["L3_ffn"])

        half = NE * FF
        m_late = {}
        layer0_attention()
        layer0_cross() if last_layer > 1 else None
        if last_layer > 2:
            gb0 = bc(W["L0_ffn_gate_b"][:, :], 1, NB)
            mixture("L0_ffn", W["L0_ffn_gate_w"], gb0, "logits", bufA[:, 0:half], bufA[:, half:2 * half],
                    W["L0_ffn_b1T"], W["L0_ffn_b2"], m_A)
        if last_layer > 3:
            layer1_recurrence()
        if last_layer > 4:
            layer1_cross()
        if last_layer > 5:
            mixture("L1_ffn", W["L1_ffn_Wg"], bc(W["L1_ffn_bg"][:, :], 1, NB), "probabilities", bufB[:, 0:half],
                    bufB[:, half:2 * half], W["L1_ffn_b1T"], W["L1_ffn_b2"], m_B)
        if last_layer > 6:
            layer2_attention()
        if last_layer > 7:
            layer2_cross()
        if last_layer > 8:
            layer2_experts()
        if last_layer > 9:
            layer3_attention()
        if last_layer > 10:
            layer3_cross()
        if last_layer > 11:
            layer3_experts()

        fl.segment("out")
        fl.semaphore("stored")
        stored = D("stored", out, x[:, :].rearrange("p (b f) -> p b f", f=P), end_marks(fl, -2))
        fl.put("sync", lambda e, i: e.nop(), [stored, list(ready.values()), m_ctx, m_pad, m_A, m_B, list(m_late.values())],
               sem=False)

        block = ctx.enter_context(nc.Block())

        @block.sync
        def _(eng):
            fl.run("sync", eng)

        @block.gpsimd
        def _(eng):
            fl.run("gpsimd", eng)

        @block.scalar
        def _(eng):
            fl.run("scalar", eng)

        @block.tensor
        def _(eng):
            fl.run("tensor", eng)

        @block.vector
        def _(eng):
            fl.run("vector", eng)


def end_marks(fl, at=-1):
    n = len(fl.segments) + at
    return [(n, e, k) for e, k in fl.segments[n]["count"].items() if e in ENGINES[1:]]


def lay_out(inputs):
    a = {k: np.asarray(v) for k, v in inputs.items()}
    out = {}

    def rep(v, n=P):
        return np.broadcast_to(v.reshape(1, -1), (n, v.size))

    out["x"] = a["x"].transpose(1, 0, 2).reshape(P, T)
    out["ctxT"] = a["ctx_1024"].transpose(2, 0, 1).reshape(P, T)
    out["mask"] = a["mask_BxS2_bf0"].reshape(T)
    for n in ("Wq", "Wk", "Wv", "Wo"):
        out[f"L0_attn_{n}"] = a[f"L0_attn_{n}"]
        out[f"L0_xattn_{n}T"] = a[f"L0_xattn_{n}"].T
    for n in ("Wck", "Wcv"):
        out[f"L0_attn_{n}R"] = np.tile(a[f"L0_attn_{n}"].reshape(G0, HD, HD).transpose(1, 0, 2).reshape(HD, -1), (H, 1))
    out["L0_attn_WgR"] = np.tile(a["L0_attn_Wg"], (H, 1))
    out["L0_attn_bg"] = rep(a["L0_attn_bg"])
    out["L0_ffn_gate_w"] = a["L0_ffn_gate_w"]
    out["L0_ffn_gate_b"] = rep(a["L0_ffn_gate_b"])
    out["L1_ffn_Wg"] = a["L1_ffn_Wg"]
    out["L1_ffn_bg"] = rep(a["L1_ffn_bg"])
    for layer, w1, w2 in (("L0", "w1", "w2"), ("L1", "W1", "W2"), ("L3", "w1", "w2")):
        out[f"{layer}_ffn_{w1}"] = a[f"{layer}_ffn_{w1}"].transpose(1, 0, 2).reshape(P, NE * FF)
        w = a[f"{layer}_ffn_{w2}"].reshape(NE, FF // P, P, P)
        out[f"{layer}_ffn_{w2}"] = w.transpose(2, 0, 1, 3).reshape(P, NE * FF)
        out[f"{layer}_ffn_b1T"] = a[f"{layer}_ffn_b1"].reshape(NE * FF // P, P).T
        out[f"{layer}_ffn_b2"] = a[f"{layer}_ffn_b2"]
    out["L1_attn_WiT"] = a["L1_attn_Wi"].T
    out["L1_attn_conv_w"] = a["L1_attn_conv_w"].reshape(2, HC, KC).transpose(1, 0, 2).reshape(HC, 2 * KC)
    out["L1_attn_conv_b"] = a["L1_attn_conv_b"].reshape(2, HC).T
    out["L1_attn_WgT"] = a["L1_attn_Wg"].T.reshape(2, HC, 2 * HID).transpose(1, 0, 2).reshape(HC, 4 * HID)
    out["L1_attn_bg"] = a["L1_attn_bg"].reshape(4, HC).T
    out["L1_attn_forget_base"] = a["L1_attn_forget_base"].reshape(2, HC).T
    out["L1_attn_WoT"] = a["L1_attn_Wo"].T.reshape(2, HC, P).transpose(1, 0, 2).reshape(HC, 2 * P)
    for n in "qkv":
        wt = a[f"L1_xattn_W{n}"].T
        out[f"L1_xattn_W{n}T"] = np.concatenate([wt, wt[:, 0:24]], axis=1)
        b8 = a[f"L1_xattn_b{n}"].reshape(H, HD).T
        out[f"L1_xattn_b{n}8"] = np.tile(b8, (P // HD, 1))
    out["slopes"] = rep(alibi_slopes().reshape(NPAIR // 2, 2, 2, 2).transpose(0, 2, 1, 3))
    w = a["L2_attn_W_qkv"]
    wq = w[:, 0:QH * DH].reshape(P, NPAIR, 2, 2, DH).transpose(0, 1, 3, 2, 4).reshape(P, QH * DH)
    out["L2_attn_Wqkv"] = np.concatenate([wq, w[:, QH * DH:]], axis=1)
    out["L2_attn_Wout"] = a["L2_attn_W_out"].reshape(QH * DH // P, P, P).transpose(1, 0, 2).reshape(P, QH * DH)
    for n in ("Wq", "Wk", "Wv", "Wo"):
        out[f"L2_xattn_{n}"] = a[f"L2_xattn_{n}"]
    for n in ("bq", "bk"):
        out[f"L2_xattn_{n}"] = a[f"L2_xattn_{n}"].reshape(P, 1)
        out[f"L3_attn_{n}"] = a[f"L3_attn_{n}"].reshape(P, 1)
    out["L2_xattn_bv"] = rep(np.tile(a["L2_xattn_bv"], 4))
    out["L2_xattn_bo"] = rep(a["L2_xattn_bo"])
    gu = np.concatenate([np.concatenate([a["L2_ffn_Wg"], a["L2_ffn_Wu"]], axis=1),
                         np.concatenate([a["L2_ffn_Wg_s"], a["L2_ffn_Wu_s"]], axis=0)[None]], axis=0)
    out["L2_ffn_Wgu"] = gu.transpose(2, 0, 1).reshape(P, (NE + 1) * 2 * FI)
    wd = np.concatenate([a["L2_ffn_Wd"], a["L2_ffn_Wd_s"][None]], axis=0).transpose(0, 2, 1)
    out["L2_ffn_Wd"] = wd.reshape(NE + 1, FI // P, P, P).transpose(2, 0, 1, 3).reshape(P, (NE + 1) * FI)
    out["L2_ffn_WrT"] = a["L2_ffn_Wr"].T
    out["L2_ffn_rb"] = rep(a["L2_ffn_rb"])
    for n in ("wq", "wk", "wv", "wo"):
        out[f"L3_attn_{n}T"] = a[f"L3_attn_{n}"].T
    out["L3_attn_bqrow"] = rep(np.tile(a["L3_attn_bq"], 4))
    out["L3_attn_bv"] = rep(np.tile(a["L3_attn_bv"], 4))
    out["L3_attn_bo"] = rep(a["L3_attn_bo"])
    out["L3_xattn_W1T"] = a["L3_xattn_W"][:, 0:P].T
    out["L3_xattn_W2T"] = a["L3_xattn_W"][:, P:].T
    out["L3_xattn_b"] = rep(a["L3_xattn_b"])
    out["L3_ffn_wg_redT"] = a["L3_ffn_wg_red"].T
    out["L3_ffn_wg"] = a["L3_ffn_wg"]
    return {k: np.ascontiguousarray(v) for k, v in out.items()}


def alibi_slopes():
    base = 2.0 ** (-(2.0 ** (-(np.log2(QH) - 3))))
    return (base ** np.arange(1, QH + 1, dtype=np.float32)).astype(np.float32)


def kernel(**inputs):
    import concourse.bacc as bacc
    from concourse.bass_utils import run_bass_kernel_spmd

    arrays = lay_out(inputs)
    nc = bacc.Bacc("TRN2", target_bir_lowering=False, num_devices=1)
    d = {n: nc.dram_tensor(f"in_{n}", list(v.shape), mybir.dt.from_np(v.dtype), kind="ExternalInput").ap()
         for n, v in arrays.items()}
    out = nc.dram_tensor("out_0", [NB, P, P], F32, kind="ExternalOutput").ap()
    build_program(nc, d, out.rearrange("b t f -> t b f"))
    r = run_bass_kernel_spmd(nc, [{f"in_{n}": v for n, v in arrays.items()}], core_ids=[0])
    return r.results[0]["out_0"]
```

```python
from contextlib import ExitStack

import numpy as np

import concourse.bass as bass
from concourse import mybir

F32 = mybir.dt.float32
U8 = mybir.dt.uint8
U32 = mybir.dt.uint32
ALU = mybir.AluOpType
ACT = mybir.ActivationFunctionType
AX = mybir.AxisListType
ds = bass.ds

P = 128
NB = 8
T = NB * P
H = 16
HD = 8
NE = 8
BANK = 512
BIG = 1.0e30
NEG = -1.0e9
EPS = 1.0e-5
G0 = 16
NBLK = P // G0
TOP_BLOCKS = 4
WIN = 32
HID = 192
HC = HID // 2
KC = 4
QH, KVH, DH = 32, 16, 64
NPAIR = KVH // 2
FF = 512
FI = 256
MIN_F, MAX_F = 3, 10
ENGINES = ("sync", "gpsimd", "scalar", "tensor", "vector")


class Flow:

    def __init__(self, nc, ctx):
        self.nc, self.ctx = nc, ctx
        self.sems = {e: ctx.enter_context(nc.semaphore(f"done_{e}")) for e in ENGINES}
        self.segments = []
        self.base = {}

    def semaphore(self, name):
        self.sems[name] = self.ctx.enter_context(self.nc.semaphore(name))
        return name

    def segment(self, name, trips=1):
        if self.segments:
            last = self.segments[-1]
            for s, k in last["count"].items():
                self.base[s] = self.base.get(s, 0) + k * last["trips"]
        self.segments.append(dict(name=name, trips=trips, base=dict(self.base), count={},
                                  queue={e: [] for e in ENGINES}))

    def put(self, engine, make, after, sem=None, step=1):
        seg = self.segments[-1]
        waits = []

        def add(a):
            if a is None:
                return
            if isinstance(a, list):
                for x in a:
                    add(x)
            else:
                waits.append(a)
        add(list(after))
        mark = None
        if sem is not False:
            name = sem or engine
            seg["count"][name] = seg["count"].get(name, 0) + step
            mark = (len(self.segments) - 1, name, seg["count"][name])
            signal = (name, step)
        else:
            signal = None
        seg["queue"][engine].append((make, waits, signal))
        return mark

    def run(self, engine, eng):
        for at, seg in enumerate(self.segments):
            queue = seg["queue"][engine]
            if not queue:
                continue
            if seg["trips"] == 1:
                self.issue(engine, eng, at, seg, queue, 0)
            else:
                with eng.Fori(0, seg["trips"]) as i:
                    self.issue(engine, eng, at, seg, queue, i)

    def issue(self, engine, eng, at, seg, queue, i):
        looped = seg["trips"] > 1
        seen = {}

        def wait(name, value, per_trip):
            eng.wait_ge(self.sems[name], i * per_trip + value if looped and per_trip else value)

        if engine != "sync":
            for other in ENGINES[1:]:
                start, per_trip = seg["base"].get(other, 0), seg["count"].get(other, 0)
                if start or (looped and per_trip):
                    wait(other, start, per_trip)
        for make, waits, signal in queue:
            need = {}
            for where, name, k in waits:
                if where == at:
                    need[(name, True)] = max(need.get((name, True), 0), k)
                elif name not in ENGINES[1:] or engine == "sync":
                    s = self.segments[where]
                    total = s["base"].get(name, 0) + (s["trips"] - 1) * s["count"][name] + k
                    need[(name, False)] = max(need.get((name, False), 0), total)
            for (name, here), k in need.items():
                if seen.get((name, here), 0) >= k:
                    continue
                seen[(name, here)] = k
                if here:
                    wait(name, seg["base"].get(name, 0) + k, seg["count"][name])
                else:
                    eng.wait_ge(self.sems[name], k)
            ins = make(eng, i)
            if signal:
                ins.then_inc(self.sems[signal[0]], signal[1])


class Ring:

    def __init__(self, buffers):
        self.buffers, self.at, self.busy = buffers, 0, [[] for _ in buffers]

    def take(self):
        n = self.at % len(self.buffers)
        self.at += 1
        freed, self.busy[n] = self.busy[n], []
        return n, self.buffers[n], freed

    def give(self, n, *marks):
        self.busy[n] += list(marks)


def build_program(nc, d, out, last_layer=12):
    ctx = ExitStack()
    with ctx:
        fl = Flow(nc, ctx)

        def sb(name, shape, dt=F32):
            return ctx.enter_context(nc.sbuf_tensor(name, shape, dt))

        def V(make, *after):
            return fl.put("vector", make, after)

        def A(make, *after):
            return fl.put("scalar", make, after)

        def G(make, *after):
            return fl.put("gpsimd", make, after)

        def M(make, *after, signal=True):
            return fl.put("tensor", make, others(after), sem=None if signal else False)

        def others(after):
            return [others(a) if isinstance(a, (list, tuple)) and not is_mark(a) else a for a in after
                    if not (is_mark(a) and a[1] == "tensor")]

        def is_mark(a):
            return isinstance(a, tuple) and len(a) == 3 and isinstance(a[1], str)

        def D(sem, dst, src, *after):
            return fl.put("sync", lambda e, i: e.dma_start(dst, src), after, sem=sem, step=16)

        def bc(ap, axis, n):
            ap = ap.unsqueeze(axis)
            shape = list(ap.shape)
            shape[axis] = n
            return ap.broadcast_to(shape)

        x = sb("x", [P, T])
        xnT = sb("xnT", [P, T])
        ctxT = sb("ctxT", [P, T])
        bufA = sb("bufA", [P, 2 * NE * FF])
        bufB = sb("bufB", [P, 2 * NE * FF])
        arena = sb("arena", [P, 19500])
        banks = [ctx.enter_context(nc.psum_tensor(f"bank{n}", [P, BANK], F32)) for n in range(8)]
        used = [0]

        def fresh():
            used[0] = 0

        def carve(*shape, parts=P):
            n = int(np.prod(shape))
            v = arena[0:parts, used[0]:used[0] + n]
            used[0] += n
            assert used[0] <= 19500, used[0]
            if len(shape) == 2:
                v = v.rearrange("p (a b) -> p a b", b=shape[1])
            elif len(shape) == 3:
                v = v.rearrange("p (a b c) -> p a b c", b=shape[1], c=shape[2])
            return v

        def loaded(names, sem):
            fl.semaphore(sem)
            tiles, mark = {}, None
            for n in names:
                shape = list(d[n].shape)
                tiles[n] = sb(f"w_{n}", shape)
                mark = D(sem, tiles[n][tuple(slice(None) for _ in shape)], d[n])
            return tiles, mark

        fl.segment("constants")
        fl.semaphore("in_x")
        m_x = D("in_x", x[:, :], d["x"])
        fl.semaphore("in_ctx")
        W = {}
        ready = {}
        for group, names in (
            ("L0_attn", ("L0_attn_Wq", "L0_attn_Wk", "L0_attn_Wv", "L0_attn_Wo", "L0_attn_WckR", "L0_attn_WcvR",
                         "L0_attn_WgR", "L0_attn_bg")),
            ("L0_xattn", ("L0_xattn_WqT", "L0_xattn_WkT", "L0_xattn_WvT", "L0_xattn_WoT")),
            ("L0_ffn", ("L0_ffn_gate_w", "L0_ffn_gate_b", "L0_ffn_b1T", "L0_ffn_b2")),
            ("L1_attn", ("L1_attn_WiT", "L1_attn_conv_w", "L1_attn_conv_b", "L1_attn_WgT", "L1_attn_bg",
                         "L1_attn_forget_base", "L1_attn_WoT")),
            ("L1_xattn", ("L1_xattn_WqT", "L1_xattn_WkT", "L1_xattn_WvT", "L1_xattn_bq8", "L1_xattn_bk8",
                          "L1_xattn_bv8")),
            ("L1_ffn", ("L1_ffn_Wg", "L1_ffn_bg", "L1_ffn_b1T", "L1_ffn_b2")),
            ("L2_attn", ("slopes",)),
            ("L2_xattn", ("L2_xattn_Wq", "L2_xattn_bq", "L2_xattn_Wk", "L2_xattn_bk", "L2_xattn_Wv",
                          "L2_xattn_bv", "L2_xattn_Wo", "L2_xattn_bo")),
            ("L2_ffn", ("L2_ffn_WrT", "L2_ffn_rb")),
            ("L3_attn", ("L3_attn_wqT", "L3_attn_bq", "L3_attn_bqrow", "L3_attn_wkT", "L3_attn_bk",
                         "L3_attn_wvT", "L3_attn_bv", "L3_attn_woT", "L3_attn_bo")),
            ("L3_xattn", ("L3_xattn_W1T", "L3_xattn_W2T", "L3_xattn_b")),
            ("L3_ffn", ("L3_ffn_wg_redT", "L3_ffn_wg", "L3_ffn_b1T", "L3_ffn_b2")),
        ):
            tiles, ready[group] = loaded(names, f"in_{group}")
            W.update(tiles)
            if group == "L0_attn":
                m_ctx = D("in_ctx", ctxT[:, :], d["ctxT"])
            if group == "L0_ffn":
                fl.semaphore("in_A")
                fl.semaphore("in_B")
                half = NE * FF
                D("in_A", bufA[:, 0:half], d["L0_ffn_w1"])
                m_A = D("in_A", bufA[:, half:2 * half], d["L0_ffn_w2"])
                D("in_B", bufB[:, 0:half], d["L1_ffn_W1"])
                m_B = D("in_B", bufB[:, half:2 * half], d["L1_ffn_W2"])
        pad_u8 = sb("pad_u8", [P, T], U8)
        fl.semaphore("in_pad")
        m_pad = D("in_pad", pad_u8[:, :], d["mask"].partition_broadcast(P))

        ident = sb("ident", [P, P])
        mask16 = sb("mask16", [P, H])
        mask4 = sb("mask4", [P, 4])
        causal = sb("causal", [P, P])
        window = sb("window", [P, P])
        tri = sb("tri", [P, P])
        blk01 = sb("blk01", [P, NBLK])
        blkneg = sb("blkneg", [P, NBLK])
        anyblk = sb("anyblk", [P, 1])
        below = sb("below", [P, 8, 8])
        nm7 = sb("nm7", [P, 8])

        def select(t, pattern, base, mult, op, fill, *after):
            return G(lambda e, i: e.affine_select(out=t, in_=t, compare_op=op, fill=fill, base=base,
                                                  pattern=pattern, channel_multiplier=mult), *after)

        def filled(t, v):
            return G(lambda e, i: e.memset(t, v))

        select(ident[:, :], [[-1, P]], 0, 1, ALU.not_equal, 1.0, filled(ident[:, :], 0.0))
        m = filled(mask16[:, :], 1.0)
        m = select(mask16[:, :], [[-HD, H]], 0, 1, ALU.is_ge, 0.0, m)
        m16 = select(mask16[:, :], [[HD, H]], HD - 1, -1, ALU.is_ge, 0.0, m)
        V(lambda e, i: e.tensor_reduce(mask4[:, :], mask16[:, :].rearrange("p (g j) -> p j g", j=4),
                                       AX.X, ALU.add), m16)
        select(causal[:, :], [[-1, P]], 0, 1, ALU.is_ge, -BIG, filled(causal[:, :], 0.0))
        m = select(window[:, :], [[-1, P]], 0, 1, ALU.is_ge, -BIG, filled(window[:, :], 0.0))
        select(window[:, :], [[1, P]], WIN, -1, ALU.is_ge, -BIG, m)
        select(tri[:, :], [[1, P]], 0, -1, ALU.is_ge, 0.0, filled(tri[:, :], 1.0))
        select(blk01[:, :], [[-G0, NBLK]], -G0, 1, ALU.is_ge, 0.0, filled(blk01[:, :], 1.0))
        select(blkneg[:, :], [[-G0, NBLK]], -G0, 1, ALU.is_ge, NEG, filled(blkneg[:, :], 0.0))
        select(anyblk[:, :], [[0, 1]], -G0, 1, ALU.is_ge, 0.0, filled(anyblk[:, :], 1.0))
        select(below[:, :, :], [[1, 8], [-1, 8]], 0, 0, ALU.is_gt, 0.0, filled(below[:, :, :], 1.0))
        G(lambda e, i: e.iota(nm7[:, :], pattern=[[1, 8]], base=-7, channel_multiplier=0,
                              allow_small_or_imprecise_dtypes=True))

        def b_(ap):
            return lambda b: ap[:, ds(b * P, P)]

        stat = [sb(f"stat{n}", [P, NB]) for n in range(3)]

        def normalise(name, *after, loads=()):
            last = end_marks(fl)
            fl.segment(name)
            marks = [D(sem, dst, d[src], last) for sem, dst, src in loads]
            fresh()
            x3 = x[:, :].rearrange("p (b f) -> p b f", f=P)
            xc, sq = carve(NB, P), carve(NB, P)
            mean, var, rstd = (s[:, :] for s in stat)
            m = V(lambda e, i: e.tensor_reduce(mean, x3, AX.X, ALU.add), *after)
            m = V(lambda e, i: e.tensor_scalar(mean, mean, 1.0 / P, None, ALU.mult), m)
            mc = V(lambda e, i: e.tensor_tensor(xc, x3, bc(mean, 2, P), ALU.subtract), m)
            m = V(lambda e, i: e.tensor_tensor(sq, xc, xc, ALU.mult), mc)
            m = V(lambda e, i: e.tensor_reduce(var, sq, AX.X, ALU.add), m)
            m = V(lambda e, i: e.tensor_scalar(var, var, 1.0 / P, EPS, ALU.mult, ALU.add), m)
            m = A(lambda e, i: e.activation(rstd, var, ACT.Sqrt), m)
            m = V(lambda e, i: e.reciprocal(rstd, rstd), m)
            for k in range(2):
                h = slice(4 * k, 4 * k + 4)
                mn = V(lambda e, i, h=h: e.tensor_tensor(xc[:, h, :], xc[:, h, :], bc(rstd[:, h], 2, P), ALU.mult), m)
                for b in range(4 * k, 4 * k + 4):
                    mt = M(lambda e, i, b=b: e.transpose(banks[b // 4][:, (b % 4) * P:(b % 4 + 1) * P],
                                                         xc[:, b, :], ident[:, :]), mn)
                evacuate(xnT[:, k * BANK:(k + 1) * BANK], banks[k][:, :], k, mt)
            fl.segment(name + ": work")
            fresh()
            return marks

        def evacuate(dst, src, turn, *after):
            if turn % 2:
                return V(lambda e, i: e.tensor_copy(dst, src), *after)
            return A(lambda e, i: e.activation(dst, src, ACT.Copy), *after)

        def project(dst, w, src, ring, bias=None, *after):
            marks = []
            for k in range(2):
                n, bank, freed = ring.take()
                c = slice(k * BANK, (k + 1) * BANK)
                m = M(lambda e, i, bank=bank, c=c: e.matmul(bank[:, :], w, src[:, c], start=True, stop=True),
                      freed, *after)
                if bias is None:
                    m = evacuate(dst[:, c], bank[:, :], k, m)
                else:
                    m = V(lambda e, i, bank=bank, c=c: e.tensor_scalar(dst[:, c], bank[:, :], bias, None, ALU.add), m)
                ring.give(n, m)
                marks.append(m)
            return marks

        def project_tokens(dst4, w, src, ring, bias=None, *after):
            marks = []
            for k in range(2):
                n, bank, freed = ring.take()
                for j in range(4):
                    c = (4 * k + j) * P
                    m = M(lambda e, i, bank=bank, j=j, c=c: e.matmul(bank[:, j * P:(j + 1) * P], src[:, c:c + P], w,
                                                                      start=True, stop=True), freed, *after)
                dst, view = dst4(k, bank)
                if bias is None:
                    m = evacuate(dst, view, k, m)
                else:
                    m = V(lambda e, i, dst=dst, view=view: e.tensor_tensor(dst, view, bias, ALU.add), m)
                ring.give(n, m)
                marks.append(m)
            return marks

        def heads_with_ones():
            v = carve(NB * H, HD + 1)
            m = G(lambda e, i: e.memset(v[:, :, HD:HD + 1], 1.0))

            def dst4(k, bank):
                return (v[:, 4 * H * k:4 * H * (k + 1), 0:HD], bank[:, :].rearrange("p (a c) -> p a c", c=HD))
            return v, dst4, m

        def ranked(v, keep, ge, pairs, r1, r2, *after):
            rows = v.shape[1]
            seen = []
            for n in range(1, 8):
                seen.append(V(lambda e, i, n=n: e.tensor_tensor(
                    pairs[:, :, n, 0:n], v[:, :, 0:n], v[:, :, n:n + 1].broadcast_to([P, rows, n]), ALU.is_ge), *after))
            for n in range(1, 8):
                m1 = V(lambda e, i, n=n: e.tensor_reduce(r1[:, :, n:n + 1], pairs[:, :, n, 0:n], AX.X, ALU.add), seen)
                m2 = V(lambda e, i, n=n: e.tensor_reduce(r2[:, :, n - 1:n], pairs[:, :, n:8, n - 1], AX.X, ALU.add),
                       seen)
            m0 = [V(lambda e, i: e.memset(r1[:, :, 0:1], 0.0), *after),
                  V(lambda e, i: e.memset(r2[:, :, 7:8], 0.0), *after)]
            m = V(lambda e, i: e.tensor_tensor(r1, r1, r2, ALU.subtract), m1, m2, m0)
            m = V(lambda e, i: e.tensor_tensor(r1, r1, bc(nm7[:, :], 1, rows), ALU.subtract), m)
            return V(lambda e, i: e.tensor_scalar(keep, r1, ge - 0.5, None, ALU.is_lt), m)

        def staircase(n, *stages, newest=False):
            state = [None] * n
            for step in range(n + max(lag for lag, _ in stages)):
                for lag, stage in (stages if newest else reversed(stages)):
                    if 0 <= step - lag < n:
                        state[step - lag] = stage(step - lag, state[step - lag])

        def softmax_ready(tile, heads, scale, mx, *after):
            m = V(lambda e, i: e.tensor_reduce(mx, tile, AX.X, ALU.max), *after)
            m = V(lambda e, i: e.tensor_tensor(tile, tile, bc(mx, 2, P), ALU.subtract), m)
            return A(lambda e, i: e.activation(tile, tile, ACT.Exp, scale=scale), m)

        def turned(ring_t, ring_p, tile, turn, *after):
            n, bank, freed = ring_t.take()
            for j in range(4):
                m = M(lambda e, i, j=j: e.transpose(bank[:, j * P:(j + 1) * P], tile[:, j * P:(j + 1) * P], ident[:, :]),
                      freed, *after)
            q, dst, freed = ring_p.take()
            c = evacuate(dst, bank[:, :], turn, m, freed)
            ring_t.give(n, c)
            return q, dst, m, c

        def turn_back(o, area, oT, *after):
            m = M(lambda e, i: e.transpose(area, o, ident[:, :]), *after)
            return A(lambda e, i: e.activation(oT, area, ACT.Copy), m)

        def add_projected(b, area, oT, w, m, bias=None):
            m = M(lambda e, i: e.matmul(area, oT, w, start=True, stop=True), m)
            m = V(lambda e, i: e.tensor_tensor(b_(x)(b(i)), b_(x)(b(i)), area, ALU.add), m)
            if bias is not None:
                m = V(lambda e, i: e.tensor_tensor(b_(x)(b(i)), b_(x)(b(i)), bias, ALU.add), m)
            return m

        def attention(name, qT, kT, v, mask, wo, bias=None, keep=None, per=4):
            fl.segment(name, NB // per)
            scale = 1.0 / float(np.sqrt(HD))
            every = range(per)
            qb, kM = [carve(P) for _ in every], [carve(4, P) for _ in every]
            o, oT, rs = ([carve(n) for _ in range(2)] for n in (P, P, H))
            ring_s, ring_t = Ring(banks[0:3]), Ring(banks[3:6])
            ring_a, ring_p = Ring([carve(BANK) for _ in range(4)]), Ring([carve(BANK) for _ in range(3)])
            mxs = [carve(4) for _ in range(8)]
            bat = [lambda i, u=u: i * per + u for u in every]
            done = {}
            staged = []
            for u in every:
                m1 = G(lambda e, i, u=u: e.tensor_copy(qb[u], b_(qT)(bat[u](i))))
                m2 = G(lambda e, i, u=u: e.tensor_tensor(kM[u], b_(kT)(bat[u](i)).unsqueeze(1).broadcast_to([P, 4, P]),
                                                         bc(mask4[:, :], 2, P), ALU.mult))
                staged.append([m1, m2])

            def score(k, _):
                u, g = divmod(k, 4)
                q = slice(32 * g, 32 * g + 32)
                n, bank, freed = ring_s.take()
                m = M(lambda e, i: e.matmul(bank[:, :], qb[u][q, :], kM[u][q, :, :].rearrange("p j t -> p (j t)"),
                                            start=True, stop=True), freed, staged[u])
                a, tile, freed = ring_a.take()
                t3 = tile.rearrange("p (j t) -> p j t", t=P)
                s3 = bank[:, :].rearrange("p (j t) -> p j t", t=P)
                mx = mxs[k % 8]
                if mask is not None:
                    m = V(lambda e, i: e.tensor_tensor(t3, s3, bc(mask, 1, 4), ALU.add), m, freed)
                    ring_s.give(n, m)
                    return a, tile, softmax_ready(t3, 4, scale, mx, m)
                m = V(lambda e, i: e.tensor_reduce(mx, s3, AX.X, ALU.max), m, freed)
                m = V(lambda e, i: e.tensor_tensor(t3, s3, bc(mx, 2, P), ALU.subtract), m)
                ring_s.give(n, m)
                return a, tile, A(lambda e, i: e.activation(t3, t3, ACT.Exp, scale=scale), m)

            def turn(k, s):
                a, tile, m = s
                q, pT, mt, mc = turned(ring_t, ring_p, tile, 0, m)
                ring_a.give(a, mt)
                return q, pT, mc

            def values(k, s):
                u, g = divmod(k, 4)
                q, pT, m = s
                bank = banks[6 + u % 2]
                for j in range(4):
                    h = 4 * g + j
                    mv = M(lambda e, i, h=h, j=j: e.matmul(
                        bank[:, h * 9:h * 9 + 9], pT[:, j * P:(j + 1) * P],
                        v[:, ds(bat[u](i) * H + h, 1), :].rearrange("p a c -> p (a c)"), start=True, stop=True),
                        m, done.get(u - 2))
                ring_p.give(q, mv)
                return mv

            def weigh(k, m):
                u, g = divmod(k, 4)
                if g < 3:
                    return None
                w = u % 2
                o3 = banks[6 + w][:, 0:9 * H].rearrange("p (h c) -> p h c", c=9)
                m = V(lambda e, i: e.reciprocal(rs[w].unsqueeze(2), o3[:, :, HD:HD + 1]), m)
                if keep is not None:
                    m = V(lambda e, i: e.tensor_tensor(rs[w], rs[w], keep(bat[u](i)), ALU.mult), m)
                return V(lambda e, i: e.tensor_tensor(o[w].rearrange("p (h c) -> p h c", c=HD), o3[:, :, 0:HD],
                                                      bc(rs[w], 2, HD), ALU.mult), m, done.get(u - 2))

            def back(k, m):
                w = k // 4 % 2
                return m and turn_back(o[w], banks[6 + w][:, 144:144 + P], oT[w], m)

            def add(k, m):
                w = k // 4 % 2
                if m:
                    done[k // 4] = add_projected(bat[k // 4], banks[6 + w][:, 144 + P:144 + 2 * P], oT[w], wo, m, bias)

            staircase(4 * per, (0, score), (2, turn), (3, values), (4, weigh), (5, back), (6, add))

        def add_expert_bias(comb, b2, *after):
            cT = carve(T, parts=NE)
            for k in range(2):
                for j in range(4):
                    m = M(lambda e, i, k=k, j=j: e.transpose(banks[k][0:NE, j * P:(j + 1) * P], comb[:, 4 * k + j, :],
                                                             ident[:, :]), *after)
                m = evacuate(cT[:, k * BANK:(k + 1) * BANK], banks[k][0:NE, :], 0, m)
                for j in range(4):
                    c = (4 * k + j) * P
                    m = M(lambda e, i, k=k, j=j, c=c: e.matmul(banks[2 + k][:, j * P:(j + 1) * P], cT[:, c:c + P], b2,
                                                               start=True, stop=True), m)
                xs = x[:, k * BANK:(k + 1) * BANK]
                V(lambda e, i, k=k, xs=xs: e.tensor_tensor(xs, xs, banks[2 + k][:, :], ALU.add), m)

        def experts(name, comb, w1, w2, b1, buf_ready):
            fl.segment(name, NE // 2)
            NF = FF // P
            w1s, w2s = ([carve(FF) for _ in range(2)] for _ in range(2))
            b1s, cs = [carve(NF) for _ in range(2)], [carve(NB) for _ in range(2)]
            ring_h, ring_y = Ring(banks[0:4]), Ring(banks[4:8])
            ring_a = Ring([carve(NF, BANK) for _ in range(2)])
            staged = []
            for u in range(2):
                m = [G(lambda e, i, u=u: e.tensor_copy(w1s[u], w1[:, ds((i * 2 + u) * FF, FF)]), buf_ready),
                     G(lambda e, i, u=u: e.tensor_copy(b1s[u], b1[:, ds((i * 2 + u) * NF, NF)])),
                     G(lambda e, i, u=u: e.tensor_copy(w2s[u], w2[:, ds((i * 2 + u) * FF, FF)])),
                     G(lambda e, i, u=u: e.tensor_copy(cs[u].unsqueeze(2), comb[:, :, ds(i * 2 + u, 1)]))]
                staged.append(m)

            def up(k, _):
                u, t = divmod(k, 2)
                a, h, freed_h = ring_a.take()
                marks = []
                for f in range(NF):
                    n, bank, freed = ring_h.take()
                    m = M(lambda e, i, bank=bank, f=f: e.matmul(bank[:, :], w1s[u][:, f * P:(f + 1) * P],
                                                               xnT[:, t * BANK:(t + 1) * BANK], start=True, stop=True),
                          freed, staged[u][0])
                    m = A(lambda e, i, bank=bank, f=f: e.activation(h[:, f, :], bank[:, :], ACT.Gelu,
                                                                   bias=b1s[u][:, f:f + 1]), m, staged[u][1], freed_h)
                    ring_h.give(n, m)
                return a, h, m

            def down(k, s):
                u, t = divmod(k, 2)
                a, h, m = s
                n, bank, freed = ring_y.take()
                for j in range(4):
                    for f in range(NF):
                        my = M(lambda e, i, j=j, f=f: e.matmul(bank[:, j * P:(j + 1) * P], h[:, f, j * P:(j + 1) * P],
                                                               w2s[u][:, f * P:(f + 1) * P], start=f == 0,
                                                               stop=f == NF - 1), freed, m, staged[u][2],
                               signal=f == NF - 1)
                for j in range(4):
                    xs = x[:, (4 * t + j) * P:(4 * t + j + 1) * P]
                    c = cs[u][:, 4 * t + j:4 * t + j + 1]
                    mv = V(lambda e, i, j=j, xs=xs, c=c: e.scalar_tensor_tensor(
                        xs, bank[:, j * P:(j + 1) * P], c, xs, ALU.mult, ALU.add), my, staged[u][3],
                        last_x.get((t, j)))
                    last_x[(t, j)] = mv
                ring_a.give(a, my)
                ring_y.give(n, mv)

            last_x = {}
            staircase(4, (0, up), (1, down), newest=True)

        def token_logits(w, width, src=None, *after):
            src = xnT if src is None else src
            for b in range(NB):
                m = M(lambda e, i, b=b: e.matmul(banks[7][:, b * width:(b + 1) * width], src[:, b * P:(b + 1) * P], w,
                                                 start=True, stop=True), *after)
            return banks[7][:, 0:NB * width].rearrange("p (b c) -> p b c", c=width), m

        def soft8(v, out, mx, sm, m, keep=None):
            m = V(lambda e, i: e.tensor_reduce(mx, v, AX.X, ALU.max), m)
            m = V(lambda e, i: e.tensor_tensor(out, v, bc(mx, 2, NE), ALU.subtract), m)
            m = A(lambda e, i: e.activation(out, out, ACT.Exp), m)
            if keep is not None:
                m = V(lambda e, i: e.tensor_tensor(out, out, keep, ALU.mult), m)
            m = V(lambda e, i: e.tensor_reduce(sm, out, AX.X, ALU.add), m)
            m = V(lambda e, i: e.reciprocal(sm, sm), m)
            return V(lambda e, i: e.tensor_tensor(out, out, bc(sm, 2, NE), ALU.mult), m)

        gate = dict(v=sb("gate_v", [P, NB, NE]), c=sb("gate_comb", [P, NB, NE]), r1=sb("gate_r1", [P, NB, NE]),
                    r2=sb("gate_r2", [P, NB, NE]), k=sb("gate_keep", [P, NB, NE]), mx=sb("gate_mx", [P, NB]),
                    sm=sb("gate_sm", [P, NB]), t=sb("gate_pairs", [P, NB, NE, NE]))
        gv, gc, gr1, gr2, gk = (gate[n][:, :, :] for n in ("v", "c", "r1", "r2", "k"))
        gmx, gsm, gt = gate["mx"][:, :], gate["sm"][:, :], gate["t"][:, :, :, :]
        x3 = x[:, :].rearrange("p (b f) -> p b f", f=P)

        ckT, cvT = sb("ckT", [P, NB * NBLK]), sb("cvT", [P, NB * NBLK])

        def layer0_attention():
            normalise("L0_attn", m_x)
            ring = Ring(banks)
            w = {n: W[f"L0_attn_{n}"] for n in ("Wq", "Wk", "Wv", "Wo", "WckR", "WcvR", "WgR", "bg")}
            lw = ready["L0_attn"]
            qT, kT, vT = carve(T), carve(T), carve(T)
            mq = project(qT, w["Wq"][:, :], xnT, ring, None, lw)
            mk = project(kT, w["Wk"][:, :], xnT, ring, None, lw)
            mv = project(vT, w["Wv"][:, :], xnT, ring, None, lw)
            v, dst4, ones = heads_with_ones()
            project_tokens(dst4, w["Wv"][:, :], xnT, ring, None, lw)
            oc, sel, gl = carve(NB, P), carve(NB * H, NBLK), carve(NB, 3)
            temporary = used[0]
            diag = [carve(G0 * P) for _ in range(2)]
            mc = []
            for n, src, ms, dg, dst in ((0, kT, mk, diag[0], ckT), (1, vT, mv, diag[1], cvT)):
                wr = w[("WckR", "WcvR")[n]][:, :].rearrange("p (g c) -> p g c", c=HD)
                shape = [P, G0, H, HD]
                md = V(lambda e, i, dg=dg, wr=wr: e.tensor_tensor(
                    dg.rearrange("p (g h c) -> p g h c", h=H, c=HD), wr.unsqueeze(2).broadcast_to(shape),
                    bc(mask16[:, :], 1, G0).unsqueeze(3).broadcast_to(shape), ALU.mult), lw)
                k, bank, freed = ring.take()
                for g in range(G0):
                    m = M(lambda e, i, dg=dg, src=src, bank=bank, g=g: e.matmul(
                        bank[:, 0:NB * NBLK], dg[:, g * P:(g + 1) * P],
                        src.rearrange("p (n g) -> p g n", g=G0)[:, g, :], start=g == 0, stop=g == G0 - 1),
                        freed, md, ms, signal=g == G0 - 1)
                m = V(lambda e, i, dst=dst, bank=bank: e.tensor_copy(dst[:, :], bank[:, 0:NB * NBLK]), m)
                ring.give(k, m)
                mc.append(m)
            used[0] = temporary
            kcM, vcM = carve(NB, P), carve(NB, P)
            by_head = [P, NB, H, NBLK]
            mM = [V(lambda e, i, s=s, t=t: e.tensor_tensor(
                t.rearrange("p b (h n) -> p b h n", n=NBLK),
                s[:, :].rearrange("p (b n) -> p b n", n=NBLK).unsqueeze(2).broadcast_to(by_head),
                bc(mask16[:, :], 1, NB).unsqueeze(3).broadcast_to(by_head), ALU.mult), mc)
                for s, t in ((ckT, kcM), (cvT, vcM))]
            vcBD = carve(NB, P)
            pc, pcT = carve(NB * H, NBLK), carve(NB, P)
            L, r1, r2 = (carve(NB * H, NBLK) for _ in range(3))
            pairs = carve(NB * H // 2, NBLK * NBLK).rearrange("p r (n m) -> p r n m", m=NBLK)
            mx, sm = carve(NB * H), carve(NB * H)
            gm, gs = carve(NB), carve(NB)
            scale = 1.0 / float(np.sqrt(HD))
            ml, mbd = [], []
            for k in range(2):
                n, bank, freed = ring.take()
                for j in range(4):
                    b = 4 * k + j
                    m = M(lambda e, i, b=b, j=j, bank=bank: e.matmul(
                        bank[:, j * P:(j + 1) * P], qT[:, b * P:(b + 1) * P], kcM[:, b, :], start=True, stop=True),
                        freed, mM, mq)
                rows = slice(4 * H * k, 4 * H * (k + 1))
                m = V(lambda e, i, rows=rows, bank=bank: e.scalar_tensor_tensor(
                    L[:, rows, :], bank[:, :].rearrange("p (r n) -> p r n", n=NBLK), scale,
                    bc(blk01[:, :], 1, 4 * H), ALU.mult, ALU.mult), m)
                ring.give(n, m)
                ml.append(V(lambda e, i, rows=rows: e.tensor_tensor(L[:, rows, :], L[:, rows, :],
                                                                    bc(blkneg[:, :], 1, 4 * H), ALU.add), m))
                n, bank, freed = ring.take()
                for j in range(4):
                    m = M(lambda e, i, b=4 * k + j, j=j, bank=bank: e.transpose(bank[:, j * P:(j + 1) * P],
                                                                              vcM[:, b, :], ident[:, :]), freed, mM)
                m = A(lambda e, i, k=k, bank=bank: e.activation(
                    vcBD[:, 4 * k:4 * k + 4, :], bank[:, :].rearrange("p (b f) -> p b f", f=P), ACT.Copy), m)
                ring.give(n, m)
                mbd.append(m)
            n, bank, freed = ring.take()
            for b in range(NB):
                m = M(lambda e, i, b=b, bank=bank: e.matmul(bank[:, 3 * b:3 * b + 3], qT[:, b * P:(b + 1) * P],
                                                            w["WgR"][:, :], start=True, stop=True), freed, mq, lw)
            m = V(lambda e, i, bank=bank: e.scalar_tensor_tensor(
                gl, bank[:, 0:3 * NB].rearrange("p (b c) -> p b c", c=3), 1.0 / H, bc(w["bg"][:, :], 1, NB), ALU.mult,
                ALU.add), m)
            ring.give(n, m)
            m = V(lambda e, i: e.tensor_reduce(gm, gl, AX.X, ALU.max), m)
            m = V(lambda e, i: e.tensor_tensor(gl, gl, bc(gm, 2, 3), ALU.subtract), m)
            mg = A(lambda e, i: e.activation(gl, gl, ACT.Exp), m)
            m = V(lambda e, i: e.tensor_reduce(mx, L, AX.X, ALU.max), ml)
            m = V(lambda e, i: e.tensor_tensor(pc, L, bc(mx, 2, NBLK), ALU.subtract), m)
            me = A(lambda e, i: e.activation(pc, pc, ACT.Exp), m)
            m = V(lambda e, i: e.tensor_reduce(gs, gl, AX.X, ALU.add), mg)
            m = V(lambda e, i: e.reciprocal(gs, gs), m)
            m = V(lambda e, i: e.tensor_tensor(gl, gl, bc(gs, 2, 3), ALU.mult), m)
            mg = V(lambda e, i: e.tensor_scalar(gl[:, :, 0:1], gl[:, :, 0:1], anyblk[:, :], None, ALU.mult), m)
            m = V(lambda e, i: e.tensor_reduce(sm, pc, AX.X, ALU.add), me)
            m = V(lambda e, i: e.reciprocal(sm, sm), m)
            mp = V(lambda e, i: e.tensor_tensor(pc, pc, bc(sm, 2, NBLK), ALU.mult), m)
            pc3 = pc.rearrange("p (b h) n -> p b (h n)", h=H)
            for k in range(2):
                n, bank, freed = ring.take()
                for j in range(4):
                    m = M(lambda e, i, b=4 * k + j, j=j, bank=bank: e.transpose(bank[:, j * P:(j + 1) * P],
                                                                              pc3[:, b, :], ident[:, :]), freed, mp)
                m = A(lambda e, i, k=k, bank=bank: e.activation(
                    pcT[:, 4 * k:4 * k + 4, :], bank[:, :].rearrange("p (b f) -> p b f", f=P), ACT.Copy), m)
                ring.give(n, m)
                n, bank, freed = ring.take()
                for j in range(4):
                    m2 = M(lambda e, i, b=4 * k + j, j=j, bank=bank: e.matmul(
                        bank[:, j * P:(j + 1) * P], pcT[:, b, :], vcBD[:, b, :], start=True, stop=True),
                        freed, m, mbd)
                m = V(lambda e, i, k=k, bank=bank: e.tensor_tensor(
                    oc[:, 4 * k:4 * k + 4, :], bank[:, :].rearrange("p (b f) -> p b f", f=P),
                    gl[:, 4 * k:4 * k + 4, 0:1].broadcast_to([P, 4, P]), ALU.mult), m2, mg)
                ring.give(n, m)
            m = None
            for k in range(2):
                rows = slice(4 * H * k, 4 * H * (k + 1))
                m = ranked(L[:, rows, :], sel[:, rows, :], TOP_BLOCKS, pairs, r1[:, rows, :], r2[:, rows, :], ml, m)
                m = V(lambda e, i, rows=rows: e.tensor_scalar(sel[:, rows, :], sel[:, rows, :], 1.0, BIG,
                                                              ALU.subtract, ALU.mult), m)

            per = 4
            fl.segment("L0_attn: batch", NB // per)
            used[0] = temporary
            every, two = range(per), range(2)
            qb, kM = [carve(P) for _ in every], [carve(4, P) for _ in every]
            o, o2, oT, rs, rl = ([carve(n) for _ in two] for n in (P, P, P, H, H))
            ring_s, ring_t = Ring(banks[0:3]), Ring(banks[3:6])
            ring_a, ring_p = Ring([carve(BANK) for _ in range(10)]), Ring([carve(BANK) for _ in range(4)])
            mxs = [carve(4) for _ in range(16)]
            bat = [lambda i, u=u: i * per + u for u in every]
            done, staged = {}, []
            for u in every:
                m1 = G(lambda e, i, u=u: e.tensor_copy(qb[u], b_(qT)(bat[u](i))))
                m2 = G(lambda e, i, u=u: e.tensor_tensor(kM[u], b_(kT)(bat[u](i)).unsqueeze(1).broadcast_to([P, 4, P]),
                                                         bc(mask4[:, :], 2, P), ALU.mult))
                staged.append([m1, m2])

            def score(k, _):
                u, g = divmod(k, 4)
                q = slice(32 * g, 32 * g + 32)
                n, bank, freed = ring_s.take()
                m = M(lambda e, i: e.matmul(bank[:, :], qb[u][q, :], kM[u][q, :, :].rearrange("p j t -> p (j t)"),
                                            start=True, stop=True), freed, staged[u])
                s3 = bank[:, :].rearrange("p (j t) -> p j t", t=P)
                tiles = []
                for mask in (causal, window):
                    a, tile, freed = ring_a.take()
                    t3 = tile.rearrange("p (j t) -> p j t", t=P)
                    mt = V(lambda e, i, t3=t3, mask=mask: e.tensor_tensor(t3, s3, bc(mask[:, :], 1, 4), ALU.add),
                           m, freed)
                    tiles.append([a, tile, t3, mt])
                ring_s.give(n, mt)
                t4 = tiles[0][1].rearrange("p (r c) -> p r c", c=G0)
                tiles[0][3] = G(lambda e, i: e.tensor_tensor(
                    t4, t4, bc(sel[:, ds(bat[u](i) * H + 4 * g, 4), :].rearrange("p h n -> p (h n)"), 2, G0),
                    ALU.add), tiles[0][3])
                tiles[1][3] = softmax_ready(tiles[1][2], 4, scale, mxs[k % 8], tiles[1][3])
                return tiles

            def select_softmax(k, tiles):
                tiles[0][3] = softmax_ready(tiles[0][2], 4, scale, mxs[8 + k % 8], tiles[0][3])
                return tiles

            def turn(k, tiles):
                got = []
                for a, tile, _, m in (tiles[1], tiles[0]):
                    q, pT, mt, mcp = turned(ring_t, ring_p, tile, 0, m)
                    ring_a.give(a, mt)
                    got.append((q, pT, mcp))
                return got[::-1]

            def values(k, got):
                u, g = divmod(k, 4)
                bank = banks[6 + u % 2]
                for local, (q, pT, m) in enumerate(got):
                    for j in range(4):
                        h = 4 * g + j
                        c = local * 144 + h * 9
                        mv = M(lambda e, i, h=h, j=j, c=c, pT=pT: e.matmul(
                            bank[:, c:c + 9], pT[:, j * P:(j + 1) * P],
                            v[:, ds(bat[u](i) * H + h, 1), :].rearrange("p a c -> p (a c)"), start=True, stop=True),
                            m, done.get(u - 2))
                    ring_p.give(q, mv)
                return mv

            def weigh(k, m):
                u, g = divmod(k, 4)
                if g < 3:
                    return None
                t = u % 2
                parts = []
                for n, r, dst in ((0, rs[t], o[t]), (1, rl[t], o2[t])):
                    src = banks[6 + t][:, 144 * n:144 * n + 144].rearrange("p (h c) -> p h c", c=9)
                    mm = V(lambda e, i, r=r, src=src: e.reciprocal(r.unsqueeze(2), src[:, :, HD:HD + 1]), m)
                    mm = V(lambda e, i, r=r, n=n: e.tensor_tensor(
                        r, r, gl[:, ds(bat[u](i), 1), n + 1:n + 2].rearrange("p a c -> p (a c)").broadcast_to([P, H]),
                        ALU.mult), mm)
                    parts.append(V(lambda e, i, r=r, src=src, dst=dst: e.tensor_tensor(
                        dst.rearrange("p (h c) -> p h c", c=HD), src[:, :, 0:HD], bc(r, 2, HD), ALU.mult), mm,
                        done.get(u - 2)))
                m = V(lambda e, i: e.tensor_tensor(o[t], o[t], o2[t], ALU.add), parts)
                return V(lambda e, i: e.tensor_tensor(
                    o[t], o[t], oc[:, ds(bat[u](i), 1), :].rearrange("p a c -> p (a c)"), ALU.add), m)

            def back(k, m):
                t = k // 4 % 2
                return m and turn_back(o[t], banks[6 + t][:, 0:P], oT[t], m)

            def add(k, m):
                t = k // 4 % 2
                if m:
                    done[k // 4] = add_projected(bat[k // 4], banks[6 + t][:, 3 * P:4 * P], oT[t], w["Wo"][:, :], m)

            staircase(4 * per, (0, score), (1, select_softmax), (2, turn), (3, values), (4, weigh), (5, back), (6, add))

        def layer0_cross():
            normalise("L0_xattn")
            ring = Ring(banks)
            lw = [ready["L0_xattn"], m_ctx]
            qT, kT = carve(T), carve(T)
            project(qT, W["L0_xattn_WqT"][:, :], xnT, ring, None, lw)
            project(kT, W["L0_xattn_WkT"][:, :], ctxT, ring, None, lw)
            v, dst4, _ = heads_with_ones()
            project_tokens(dst4, W["L0_xattn_WvT"][:, :], ctxT, ring, None, lw)
            attention("L0_xattn: batch", qT, kT, v, causal[:, :], W["L0_xattn_WoT"][:, :])

        def mixture(name, gw, gb, top, w1, w2, b1, b2, buf_ready):
            normalise(name)
            lw = ready[name]
            lg, m = token_logits(gw[:, :], NE, None, lw)
            m = V(lambda e, i: e.tensor_tensor(gv, lg, gb, ALU.add), m)
            if top == "logits":
                mk = ranked(gv, gk, 2, gt, gr1, gr2, m)
                m = soft8(gv, gc, gmx, gsm, mk, keep=gk)
            else:
                m = soft8(gv, gc, gmx, gsm, m)
                m = ranked(gc, gk, 2, gt, gr1, gr2, m)
                m = V(lambda e, i: e.tensor_tensor(gc, gc, gk, ALU.mult), m)
                m = V(lambda e, i: e.tensor_reduce(gsm, gc, AX.X, ALU.add), m)
                m = V(lambda e, i: e.reciprocal(gsm, gsm), m)
                m = V(lambda e, i: e.tensor_tensor(gc, gc, bc(gsm, 2, NE), ALU.mult), m)
            add_expert_bias(gc, b2[:, :], m)
            experts(name + ": experts", gc, w1, w2, b1[:, :], buf_ready)

        def layer1_recurrence():
            normalise("L1_attn")
            lw = ready["L1_attn"]
            wi, cw, cb, wg, bg, fb, wo = (W[f"L1_attn_{n}"] for n in (
                "WiT", "conv_w", "conv_b", "WgT", "bg", "forget_base", "WoT"))
            two = range(2)
            C = HC
            gate_, u2, al, be = (carve(2, T, parts=C) for _ in range(4))
            up = carve(2 * NB, P + KC - 1, parts=C)
            sp = [carve(2, parts=C) for _ in range(5)]
            ring = Ring(banks)
            fbv = fb[:, :]
            z, s, s2, acc, num = sp
            m = V(lambda e, i: e.tensor_scalar(z, fbv, -1.0, None, ALU.mult), lw)
            m = V(lambda e, i: e.tensor_tensor(z, z, fbv, ALU.min), m)
            m = A(lambda e, i: e.activation(z, z, ACT.Exp), m)
            m = V(lambda e, i: e.tensor_scalar(s, z, 2.0, None, ALU.add), m)
            m = V(lambda e, i: e.reciprocal(s, s), m)
            m = V(lambda e, i: e.tensor_tensor(s, s, z, ALU.mult), m)
            m = V(lambda e, i: e.tensor_tensor(s2, s, s, ALU.mult), m)
            m = V(lambda e, i: e.tensor_scalar(acc, s2, 1.0 / 17, 1.0 / 15, ALU.mult, ALU.add), m)
            for k in (13, 11, 9, 7, 5, 3, 1):
                m = V(lambda e, i: e.tensor_tensor(acc, acc, s2, ALU.mult), m)
                m = V(lambda e, i, k=k: e.tensor_scalar(acc, acc, 1.0 / k, None, ALU.add), m)
            m = V(lambda e, i: e.tensor_tensor(acc, acc, s, ALU.mult), m)
            m = V(lambda e, i: e.tensor_scalar(num, fbv, 0.0, None, ALU.max), m)
            m = V(lambda e, i: e.scalar_tensor_tensor(acc, acc, 2.0, num, ALU.mult, ALU.add), m)
            m_sp = V(lambda e, i: e.tensor_scalar(acc, acc, -8.0, None, ALU.mult), m)
            m0 = G(lambda e, i: e.memset(up[:, :, 0:KC - 1], 0.0))
            conv = []
            for c in two:
                mu = []
                for k in two:
                    n, bank, freed = ring.take()
                    m = M(lambda e, i, bank=bank, c=c, k=k: e.matmul(
                        bank[0:C, :], wi[:, HID + c * C:HID + (c + 1) * C], xnT[:, k * BANK:(k + 1) * BANK],
                        start=True, stop=True), freed, lw)
                    m = A(lambda e, i, bank=bank, c=c, k=k: e.activation(
                        up[:, c * NB + 4 * k:c * NB + 4 * k + 4, KC - 1:KC - 1 + P],
                        bank[0:C, :].rearrange("p (b t) -> p b t", t=P), ACT.Copy), m)
                    ring.give(n, m)
                    mu.append(m)
                u3 = u2[:, c, :].rearrange("p (b t) -> p b t", t=P)
                uc = up[:, c * NB:(c + 1) * NB, :]
                m = V(lambda e, i, c=c, u3=u3, uc=uc: e.tensor_scalar(
                    u3, uc[:, :, 0:P], cw[:, c * KC:c * KC + 1], cb[:, c:c + 1], ALU.mult, ALU.add), mu, m0)
                for k in range(1, KC):
                    m = V(lambda e, i, c=c, k=k, u3=u3, uc=uc: e.scalar_tensor_tensor(
                        u3, uc[:, :, k:k + P], cw[:, c * KC + k:c * KC + k + 1], u3, ALU.mult, ALU.add), m)
                conv.append(m)
            for c in two:
                for k in two:
                    n, bank, freed = ring.take()
                    m = M(lambda e, i, bank=bank, c=c, k=k: e.matmul(
                        bank[0:C, :], wi[:, c * C:(c + 1) * C], xnT[:, k * BANK:(k + 1) * BANK],
                        start=True, stop=True), freed)
                    m = A(lambda e, i, bank=bank, c=c, k=k: e.activation(
                        gate_[:, c, k * BANK:(k + 1) * BANK], bank[0:C, :], ACT.Gelu), m)
                    ring.give(n, m)
            sig = []
            for g in range(4):
                dst = (al, be)[g // 2][:, g % 2, :]
                for k in two:
                    n, bank, freed = ring.take()
                    for c in two:
                        m = M(lambda e, i, bank=bank, c=c, k=k, g=g: e.matmul(
                            bank[0:C, :], wg[:, c * 2 * HID + g * C:c * 2 * HID + (g + 1) * C],
                            u2[:, c, k * BANK:(k + 1) * BANK], start=c == 0, stop=c == 1), freed, conv)
                    m = A(lambda e, i, bank=bank, k=k, g=g, dst=dst: e.activation(
                        dst[:, k * BANK:(k + 1) * BANK], bank[0:C, :], ACT.Sigmoid, bias=bg[:, g:g + 1]), m)
                    ring.give(n, m)
                    sig.append(m)
            m_in = V(lambda e, i: e.tensor_tensor(be, be, u2, ALU.mult), sig)
            ma = [A(lambda e, i, c=c: e.activation(al[:, c, :], al[:, c, :], ACT.Exp, scale=acc[:, c:c + 1]),
                    sig, m_sp) for c in two]
            beta = carve(2, T, parts=C)
            m = V(lambda e, i: e.tensor_tensor(beta, al, al, ALU.mult), ma)
            m = V(lambda e, i: e.tensor_scalar(beta, beta, -1.0, 1.0, ALU.mult, ALU.add), m)
            m = V(lambda e, i: e.tensor_scalar(beta, beta, 1.0e-6, None, ALU.add), m)
            m = A(lambda e, i: e.activation(beta, beta, ACT.Sqrt), m)
            m_xt = V(lambda e, i: e.tensor_tensor(be, be, beta, ALU.mult), m, m_in)
            m_z = V(lambda e, i: e.memset(al.rearrange("p c (b t) -> p (c b) t", t=P)[:, :, 0:1], 0.0), ma, m_xt)
            hs = u2
            for c in two:
                m = V(lambda e, i, c=c: e.tensor_tensor_scan(hs[:, c, :], al[:, c, :], be[:, c, :], 0.0, ALU.mult,
                                                             ALU.add), m_z, m_xt)
                m_y = V(lambda e, i, c=c: e.tensor_tensor(hs[:, c, :], hs[:, c, :], gate_[:, c, :], ALU.mult), m)
            for k in two:
                n, bank, freed = ring.take()
                for j in range(4):
                    for c in two:
                        t0 = (4 * k + j) * P
                        m = M(lambda e, i, bank=bank, c=c, j=j, t0=t0: e.matmul(
                            bank[:, j * P:(j + 1) * P], hs[:, c, t0:t0 + P], wo[:, c * P:(c + 1) * P],
                            start=c == 0, stop=c == 1), freed, m_y)
                xs = x[:, k * BANK:(k + 1) * BANK]
                V(lambda e, i, xs=xs, bank=bank: e.tensor_tensor(xs, xs, bank[:, :], ALU.add), m)

        def layer1_cross():
            normalise("L1_xattn")
            lw = [ready["L1_xattn"], m_ctx]
            NP_ = 2 * H * P
            tiles = []
            ring = Ring(banks)
            for n, (wn, bn, src) in enumerate((("WqT", "bq8", xnT), ("WkT", "bk8", ctxT), ("WvT", "bv8", ctxT))):
                w, b8 = W[f"L1_xattn_{wn}"], W[f"L1_xattn_{bn}"]
                dst = carve(NP_)
                for f2 in range(H // 2):
                    k, bank, freed = ring.take()
                    for f in (2 * f2, 2 * f2 + 1):
                        f0 = min(8 * f, P - 32)
                        for g in range(4):
                            m = M(lambda e, i, bank=bank, f=f, g=g, w=w, src=src: e.matmul(
                                bank[32 * g:32 * g + 32, (f % 2) * 256:(f % 2) * 256 + 256], w[:, 8 * f:8 * f + 32],
                                src[:, 256 * g:256 * g + 256], start=True, stop=True), freed, lw)
                    view = dst.rearrange("p (t f) -> p f t", f=H)[:, 2 * f2:2 * f2 + 2, :]
                    bias = bc(b8[:, 2 * f2:2 * f2 + 2], 2, 256)
                    m = V(lambda e, i, bank=bank, view=view, bias=bias: e.tensor_tensor(
                        view, bank[:, :].rearrange("p (f t) -> p f t", f=2), bias, ALU.add), m)
                    ring.give(k, m)
                tiles.append(dst)
            fl.segment("L1_xattn: batch", 2)
            S2 = H * P
            scale = float(np.sqrt(HD))
            qs, ks, vs = (bufA[:, n * S2:(n + 1) * S2] for n in range(3))
            st = [G(lambda e, i: e.tensor_copy(qs, tiles[0][:, ds(i * S2, S2)])),
                  A(lambda e, i: e.activation(ks, tiles[1][:, ds(i * S2, S2)], ACT.Copy)),
                  G(lambda e, i: e.tensor_copy(vs, tiles[2][:, ds(i * S2, S2)]))]
            vh = [carve(H, HD + 1) for _ in range(4)]
            ring_s, ring_t = Ring(banks[0:2]), Ring(banks[2:5])
            ring_a = Ring([bufA[:, 3 * S2 + n * BANK:3 * S2 + (n + 1) * BANK] for n in range(3)])
            ring_p, o8 = Ring([carve(BANK) for _ in range(3)]), [carve(S2) for _ in range(2)]
            ring_o = Ring(banks[5:7])
            mask = [sb(f"l1mask{g}", [P, P])[:, :] for g in range(4)]
            rs = [sb(f"l1rs{g}", [P, H])[:, :] for g in range(4)]
            tmp = [sb(f"l1tmp{g}", [P, P])[:, :] for g in range(4)]
            mx = sb("l1mx", [P, 16 * 4])
            bat = [lambda i, g=g: i + 2 * g for g in range(4)]
            m_one = [G(lambda e, i, g=g: e.memset(vh[g][:, :, HD:HD + 1], 1.0)) for g in range(4)]
            mm = []
            for g in range(4):
                m = V(lambda e, i, g=g: e.scalar_tensor_tensor(
                    mask[g], pad_u8[:, ds(bat[g](i) * P, P)], -BIG, causal[:, :], ALU.mult, ALU.add), m_pad)
                mm.append(m)
                n, bank, freed = ring_o.take()
                for h in range(H):
                    m = M(lambda e, i, g=g, h=h, bank=bank: e.matmul(
                        bank[:, h * HD:(h + 1) * HD], vs[32 * g:32 * g + HD, h * P:(h + 1) * P],
                        ident[32 * g:32 * g + HD, 32 * g:32 * g + HD], start=True, stop=True), freed, st[2])
                m = V(lambda e, i, g=g, bank=bank: e.tensor_copy(
                    vh[g][:, :, 0:HD], bank[:, 0:P].rearrange("p (h c) -> p h c", c=HD)), m)
                ring_o.give(n, m)
                m_one[g] = [m_one[g], m]

            def score(k, _):
                g, hg = divmod(k, 4)
                n, bank, freed = ring_s.take()
                r = slice(32 * g, 32 * g + HD)
                for j in range(4):
                    c = slice((4 * hg + j) * P, (4 * hg + j + 1) * P)
                    m = M(lambda e, i, j=j, c=c: e.matmul(bank[:, j * P:(j + 1) * P], qs[r, c], ks[r, c],
                                                          start=True, stop=True), freed, st[0:2])
                a, tile, freed = ring_a.take()
                t3 = tile.rearrange("p (j t) -> p j t", t=P)
                s3 = bank[:, :].rearrange("p (j t) -> p j t", t=P)
                m = V(lambda e, i: e.tensor_tensor(t3, s3, bc(mask[g], 1, 4), ALU.add), m, freed, mm[g])
                ring_s.give(n, m)
                return a, tile, softmax_ready(t3, 4, scale, mx[:, 4 * k:4 * k + 4], m)

            def turn(k, s):
                a, tile, m = s
                q, pT, mt, mc = turned(ring_t, ring_p, tile, 0, m)
                ring_a.give(a, mt)
                return q, pT, mc

            def values(k, s):
                g, hg = divmod(k, 4)
                q, pT, m = s
                n, bank, freed = ring_o.take()
                for j in range(4):
                    h = 4 * hg + j
                    m = M(lambda e, i, j=j, h=h: e.matmul(bank[0:9, j * P:(j + 1) * P], vh[g][:, h, :],
                                                          pT[:, j * P:(j + 1) * P], start=True, stop=True),
                          m, freed, m_one[g])
                ring_p.give(q, m)
                dst = o8[g % 2][0:9, hg * BANK:(hg + 1) * BANK]
                m = A(lambda e, i: e.activation(dst, bank[0:9, :], ACT.Copy), m, o8_free[g % 2])
                ring_o.give(n, m)
                if hg == 3:
                    src = o8[g % 2][0:9, :].rearrange("p (t f) -> p f t", f=H)
                    n, bank = 0, banks[7]
                    for f in range(H):
                        m = M(lambda e, i, f=f: e.matmul(bank[:, f * 9:f * 9 + 9], src[:, f, :], ident[0:9, 0:9],
                                                         start=True, stop=True), m, b7_free)
                    o8_free[g % 2] = m
                    o3 = bank[:, 0:144].rearrange("p (f c) -> p f c", c=9)
                    m = V(lambda e, i: e.reciprocal(rs[g].unsqueeze(2), o3[:, :, HD:HD + 1]), m)
                    m = V(lambda e, i: e.tensor_tensor(tmp[g].rearrange("p (f c) -> p f c", c=HD), o3[:, :, 0:HD],
                                                       bc(rs[g], 2, HD), ALU.mult), m)
                    b7_free[:] = [m]
                    V(lambda e, i: e.tensor_tensor(b_(x)(bat[g](i)), b_(x)(bat[g](i)), tmp[g], ALU.add), m)

            o8_free, b7_free = [None, None], []
            staircase(16, (0, score), (2, turn), (3, values), newest=True)

        def layer2_attention():
            gu, dn = (NE + 1) * 2 * FI, (NE + 1) * 3 * FI
            marks = normalise("L2_attn", loads=[
                ("in_A", bufA[:, 0:4096], "L2_attn_Wqkv"), ("in_A", bufA[:, 4096:6144], "L2_attn_Wout"),
                ("in_B", bufB[:, 0:gu], "L2_ffn_Wgu"), ("in_B", bufB[:, gu:dn], "L2_ffn_Wd")])
            m_late["L2_ffn"] = marks[3]
            lw = [ready["L2_attn"], marks[1]]
            wq, wk, wv = bufA[:, 0:2048], bufA[:, 2048:3072], bufA[:, 3072:4096]
            wo = bufA[:, 4096:6144]
            bias = carve(QH, P)
            rel = carve(P)
            m = G(lambda e, i: e.iota(rel, pattern=[[1, P]], base=0, channel_multiplier=-1,
                                      allow_small_or_imprecise_dtypes=True))
            m = V(lambda e, i: e.tensor_tensor(bias, bc(rel, 1, QH), bc(W["slopes"][:, :], 2, P), ALU.mult), m, lw)
            V(lambda e, i: e.tensor_tensor(bias, bias, bc(causal[:, :], 1, QH), ALU.add), m)
            PER = 2
            QG, KG = 4, 2
            GROUPS = NPAIR // KG
            v = carve(PER * KVH, DH + 1)
            G(lambda e, i: e.memset(v[:, :, DH:DH + 1], 1.0))
            fl.segment("L2_attn: batch", NB // PER)
            xb = carve(PER * P)
            qT, kT = carve(QG * GROUPS, PER * P), carve(KG * GROUPS, PER * P)
            v4 = v.rearrange("p (u h) c -> p u h c", u=PER)
            ring_s, ring_t = Ring(banks[0:2]), Ring(banks[2:4])
            proj, ring_o, backs, sums = banks[4], Ring(banks[5:6]), banks[6], banks[7]
            ring_a, ring_p = Ring([carve(BANK) for _ in range(4)]), Ring([carve(BANK) for _ in range(3)])
            oo, oT = [carve(2 * P) for _ in range(2)], [carve(2 * P) for _ in range(2)]
            rs, mxs = [carve(4) for _ in range(2)], [carve(4) for _ in range(8)]
            m_xb = A(lambda e, i: e.activation(xb, xnT[:, ds(i * PER * P, PER * P)], ACT.Copy))
            projected = {}

            def project_part(gg, part, bank, *freed):
                if part == 3:
                    for u in range(PER):
                        m = M(lambda e, i, u=u: e.matmul(bank[:, u * 256:(u + 1) * 256], xb[:, u * P:(u + 1) * P],
                                                         wv[:, gg * 256:(gg + 1) * 256], start=True, stop=True),
                              m_xb, lw, freed)
                    dst = v4[:, :, 4 * gg:4 * gg + 4, 0:DH]
                    src = bank[:, :].rearrange("p (u h c) -> p u h c", u=PER, c=DH)
                else:
                    w, t0, out_ = (wk, KG * gg, kT) if part == 0 else (wq, QG * gg + 2 * (part - 1), qT)
                    for t in range(2):
                        c = (t0 + t) * P
                        m = M(lambda e, i, t=t, c=c: e.matmul(bank[:, t * 256:(t + 1) * 256], w[:, c:c + P], xb,
                                                              start=True, stop=True), m_xb, lw, freed)
                    dst, src = out_[:, t0:t0 + 2, :], bank[:, :].rearrange("p (t c) -> p t c", t=2)
                projected[gg, part] = evacuate(dst, src, part, m)
                return projected[gg, part]

            early = [project_part(0, part, banks[4 + part]) for part in range(4)]
            last_proj, o_free, b6_free, b7_free = [early[0]], early[1], [early[2]], early[3]
            ring_o.give(0, o_free)
            M(lambda e, i: e.matmul(sums[:, 0:PER * P], ident[:, :], x[:, ds(i * PER * P, PER * P)], start=True,
                                    stop=False), b7_free)

            def unit(k):
                return k // 4, k // 2 % 2, k % 2

            products = {}

            def score(k, _):
                gg, u, r = unit(k)
                if r == 0:
                    slots = [ring_s.take() for _ in range(2)]
                    for jj in range(2):
                        for s in range(2):
                            for rr in range(2):
                                j = KG * gg + jj
                                p, c = slice(64 * rr, 64 * rr + 64), slice(u * P, (u + 1) * P)
                                n, bank, freed = slots[rr]
                                at = (2 * jj + s) * P
                                products[k + rr] = M(lambda e, i, p=p, c=c, j=j, s=s, at=at, bank=bank: e.matmul(
                                    bank[:, at:at + P], qT[p, 2 * j + s, c], kT[p, j, c], start=True, stop=True),
                                    freed, [projected[gg, n] for n in range(3)])
                    products["slots"] = slots
                n, bank, _ = products["slots"][r]
                m = products[k]
                a, tile, freed = ring_a.take()
                h0 = 4 * (2 * gg + r)
                bb = bias[:, h0:h0 + 4, :].rearrange("p h t -> p (h t)")
                m = V(lambda e, i: e.scalar_tensor_tensor(tile, bank[:, :], 1.0 / np.sqrt(DH).item(), bb, ALU.mult,
                                                          ALU.add), m, freed)
                ring_s.give(n, m)
                m = softmax_ready(tile.rearrange("p (j t) -> p j t", t=P), 4, 1.0, mxs[k % 8], m)
                if gg + 1 < GROUPS:
                    last_proj[0] = project_part(gg + 1, k % 4, proj, last_proj[0])
                return a, tile, m

            def turn(k, s):
                a, tile, m = s
                q, pT, mt, mc = turned(ring_t, ring_p, tile, 0, m)
                ring_a.give(a, mt)
                return q, pT, mc

            def values(k, s):
                gg, u, r = unit(k)
                q, pT, m = s
                n, bank, freed = ring_o.take()
                for hh in range(4):
                    h = u * KVH + 4 * gg + 2 * (hh // 2) + r
                    m = M(lambda e, i, hh=hh, h=h: e.matmul(bank[:, hh * 65:hh * 65 + 65], pT[:, hh * P:(hh + 1) * P],
                                                            v[:, h, :], start=True, stop=True),
                          m, freed, projected[gg, 3])
                ring_p.give(q, m)
                o3 = bank[:, 0:260].rearrange("p (h c) -> p h c", c=65)
                w = k % 2
                m = V(lambda e, i: e.reciprocal(rs[w].unsqueeze(2), o3[:, :, DH:DH + 1]), m, rs_free[w])
                m = V(lambda e, i: e.tensor_tensor(oo[w].rearrange("p (h c) -> p h c", c=DH), o3[:, :, 0:DH],
                                                   bc(rs[w], 2, DH), ALU.mult), m, oo_free[w])
                rs_free[w] = m
                ring_o.give(n, m)
                return m

            def back(k, m):
                w = k % 2
                for j in range(2):
                    m = M(lambda e, i, j=j: e.transpose(backs[:, (2 * w + j) * P:(2 * w + j + 1) * P],
                                                        oo[w][:, j * P:(j + 1) * P], ident[:, :]), m, b6_free[0])
                oo_free[w] = m
                m = A(lambda e, i: e.activation(oT[w], backs[:, 2 * w * P:2 * (w + 1) * P], ACT.Copy), m, oT_free[w])
                b6_free[0] = m
                return m

            def outputs(k, m):
                gg, u, r = unit(k)
                w = k % 2
                at = slice(u * P, (u + 1) * P)
                for j in range(2):
                    c = (2 * (2 * gg + j) + r) * P
                    m = M(lambda e, i, j=j, c=c: e.matmul(sums[:, at], oT[w][:, j * P:(j + 1) * P], wo[:, c:c + P],
                                                          start=False, stop=k == 4 * GROUPS - 1 and j == 1), m)
                oT_free[w] = m
                if k == 4 * GROUPS - 1:
                    V(lambda e, i: e.tensor_copy(x[:, ds(i * PER * P, PER * P)], sums[:, 0:PER * P]), m)

            rs_free, oo_free, oT_free = ([None, None] for _ in range(3))
            staircase(4 * GROUPS, (0, score), (2, turn), (3, values), (4, back), (5, outputs))

        def layer2_cross():
            half = NE * FF
            marks = normalise("L2_xattn", loads=[("in_A", bufA[:, 0:half], "L3_ffn_w1"),
                                                 ("in_A", bufA[:, half:2 * half], "L3_ffn_w2")])
            m_late["L3_ffn"] = marks[1]
            w = {n: W[f"L2_xattn_{n}"] for n in ("Wq", "bq", "Wk", "bk", "Wv", "bv", "Wo", "bo")}
            lw = [ready["L2_xattn"], m_ctx]
            ring = Ring(banks)
            qT, kT, low = carve(T), carve(T), carve(T)
            v, dst4, _ = heads_with_ones()
            mv = project_tokens(dst4, w["Wv"][:, :], ctxT, ring,
                                w["bv"][:, :].rearrange("p (a c) -> p a c", c=HD), lw)
            m_low = None
            for dst, wn, bn, src in ((qT, "Wq", "bq", xnT), (kT, "Wk", "bk", ctxT)):
                m = project(dst, w[wn][:, :], src, ring, w[bn][:, 0:1], lw)
                m = V(lambda e, i, dst=dst: e.tensor_scalar(low, dst, 0.0, None, ALU.min), m, m_low)
                me = A(lambda e, i: e.activation(low, low, ACT.Exp), m)
                m_low = V(lambda e, i, dst=dst: e.scalar_tensor_tensor(dst, dst, 0.0, low, ALU.max, ALU.add), me)
            fl.segment("L2_xattn: batch", NB // 2)
            two = range(2)
            kb, qb, qtok, o, oT, zr = ([carve(P) for _ in two] for _ in range(6))
            qM = [carve(4, P) for _ in two]
            ring_s, ring_a = Ring(banks[0:4]), Ring([carve(BANK) for _ in range(4)])
            bat = [lambda i: i * 2, lambda i: i * 2 + 1]
            staged = []
            for u in two:
                m1 = G(lambda e, i, u=u: e.tensor_copy(kb[u], b_(kT)(bat[u](i))))
                m2 = V(lambda e, i, u=u: e.tensor_tensor(qM[u], b_(qT)(bat[u](i)).unsqueeze(1).broadcast_to([P, 4, P]),
                                                         bc(mask4[:, :], 2, P), ALU.mult))
                m3 = G(lambda e, i, u=u: e.tensor_copy(qb[u], b_(qT)(bat[u](i))))
                staged.append([m1, m2, m3])

            def running_sums(u):
                z = banks[6 + u]
                m = M(lambda e, i: e.transpose(z[:, 0:P], qb[u], ident[:, :]), staged[u][2])
                m = A(lambda e, i: e.activation(qtok[u], z[:, 0:P], ACT.Copy), m)
                m = M(lambda e, i: e.matmul(z[:, P:2 * P], tri[:, :], qtok[u], start=True, stop=True), m)
                return V(lambda e, i: e.reciprocal(zr[u], z[:, P:2 * P]), m)

            norms = [running_sums(u) for u in two]

            def score(k, _):
                u, g = divmod(k, 4)
                q = slice(32 * g, 32 * g + 32)
                n, bank, freed = ring_s.take()
                m = M(lambda e, i: e.matmul(bank[:, :], kb[u][q, :], qM[u][q, :, :].rearrange("p j t -> p (j t)"),
                                            start=True, stop=True), freed, staged[u][0:2])
                a, tile, freed = ring_a.take()
                m = V(lambda e, i: e.tensor_tensor(tile.rearrange("p (j t) -> p j t", t=P),
                                                   bank[:, :].rearrange("p (j t) -> p j t", t=P),
                                                   bc(tri[:, :], 1, 4), ALU.mult), m, freed)
                ring_s.give(n, m)
                return a, tile, m

            def values(k, s):
                u, g = divmod(k, 4)
                a, tile, m = s
                bank = banks[4 + u]
                for j in range(4):
                    h = 4 * g + j
                    m = M(lambda e, i, h=h, j=j: e.matmul(
                        bank[:, h * HD:(h + 1) * HD], tile[:, j * P:(j + 1) * P],
                        v[:, ds(bat[u](i) * H + h, 1), 0:HD].rearrange("p a c -> p (a c)"), start=True, stop=True), m)
                ring_a.give(a, m)
                if g == 3:
                    m = V(lambda e, i: e.tensor_tensor(o[u], bank[:, 0:P], zr[u], ALU.mult), m, norms[u])
                    m = turn_back(o[u], bank[:, P:2 * P], oT[u], m)
                    add_projected(bat[u], bank[:, 2 * P:3 * P], oT[u], w["Wo"][:, :], m, w["bo"][:, :])

            staircase(8, (0, score), (1, values), newest=True)

        def layer2_experts():
            normalise("L2_ffn")
            lg, m = token_logits(W["L2_ffn_WrT"][:, :], NE, None, ready["L2_ffn"])
            m = V(lambda e, i: e.tensor_tensor(gv, lg, bc(W["L2_ffn_rb"][:, :], 1, NB), ALU.add), m)
            m = A(lambda e, i: e.activation(gv, gv, ACT.Sigmoid), m)
            m = ranked(gv, gk, 2, gt, gr1, gr2, m)
            comb = carve(NE + 1, NB)
            V(lambda e, i: e.tensor_tensor(comb[:, 0:NE, :].rearrange("p e b -> p b e"), gv, gk, ALU.mult), m)
            G(lambda e, i: e.memset(comb[:, NE, :], 1.0))
            U = 3
            fl.segment("L2_ffn: experts", (NE + 1) // U)
            WU = 2 * FI
            wu, wd = bufB[:, 0:(NE + 1) * WU], bufB[:, (NE + 1) * WU:(NE + 1) * (WU + FI)]
            wus, wds, cs = [carve(WU) for _ in range(U)], [carve(FI) for _ in range(U)], [carve(NB) for _ in range(U)]
            ring_h, ring_y = Ring(banks[0:6]), Ring(banks[6:8])
            ring_a = Ring([carve(2, BANK) for _ in range(2)])
            ring_g = Ring([carve(BANK) for _ in range(2)])
            staged = []
            for u in range(U):
                staged.append([
                    G(lambda e, i, u=u: e.tensor_copy(wus[u], wu[:, ds((i * U + u) * WU, WU)]), m_late["L2_ffn"]),
                    G(lambda e, i, u=u: e.tensor_copy(wds[u], wd[:, ds((i * U + u) * FI, FI)])),
                    G(lambda e, i, u=u: e.tensor_copy(cs[u], comb[:, ds(i * U + u, 1), :].rearrange(
                        "p a b -> p (a b)")))])

            def up(k, _):
                u, t = divmod(k, 2)
                a, h, freed_h = ring_a.take()
                for f in range(2):
                    n1, bg_, freed1 = ring_h.take()
                    n2, bu_, freed2 = ring_h.take()
                    ms = []
                    for bank, c, fr in ((bg_, f * P, freed1), (bu_, FI + f * P, freed2)):
                        ms.append(M(lambda e, i, bank=bank, c=c: e.matmul(
                            bank[:, :], wus[u][:, c:c + P], xnT[:, t * BANK:(t + 1) * BANK], start=True, stop=True),
                            fr, staged[u][0]))
                    g, sg, freed = ring_g.take()
                    m = A(lambda e, i, sg=sg, bg_=bg_: e.activation(sg, bg_[:, :], ACT.Silu), ms[0], freed)
                    ring_h.give(n1, m)
                    m = V(lambda e, i, sg=sg, bu_=bu_, f=f: e.tensor_tensor(h[:, f, :], sg, bu_[:, :], ALU.mult),
                          m, ms[1], freed_h)
                    ring_h.give(n2, m)
                    ring_g.give(g, m)
                return a, h, m

            def down(k, s):
                u, t = divmod(k, 2)
                a, h, m = s
                n, bank, freed = ring_y.take()
                for j in range(4):
                    for f in range(2):
                        my = M(lambda e, i, j=j, f=f: e.matmul(bank[:, j * P:(j + 1) * P], h[:, f, j * P:(j + 1) * P],
                                                               wds[u][:, f * P:(f + 1) * P], start=f == 0, stop=f == 1),
                               freed, m, staged[u][1], signal=f == 1)
                for j in range(4):
                    xs = x[:, (4 * t + j) * P:(4 * t + j + 1) * P]
                    c = cs[u][:, 4 * t + j:4 * t + j + 1]
                    last_x[(t, j)] = mv = V(lambda e, i, j=j, xs=xs, c=c: e.scalar_tensor_tensor(
                        xs, bank[:, j * P:(j + 1) * P], c, xs, ALU.mult, ALU.add), my, staged[u][2],
                        last_x.get((t, j)))
                ring_a.give(a, my)
                ring_y.give(n, mv)

            last_x = {}
            staircase(2 * U, (0, up), (1, down), newest=True)

        def layer3_attention():
            normalise("L3_attn")
            w = {n: W[f"L3_attn_{n}"] for n in ("wqT", "bq", "bqrow", "wkT", "bk", "wvT", "bv", "woT", "bo")}
            lw = ready["L3_attn"]
            ring = Ring(banks[0:7])
            qT, kT = carve(T), carve(T)
            project(qT, w["wqT"][:, :], xnT, ring, w["bq"][:, 0:1], lw)
            project(kT, w["wkT"][:, :], xnT, ring, w["bk"][:, 0:1], lw)
            v, dst4, _ = heads_with_ones()
            project_tokens(dst4, w["wvT"][:, :], xnT, ring, w["bv"][:, :].rearrange("p (a c) -> p a c", c=HD), lw)
            BH = NB * H
            keepT = carve(BH)
            q, t1, t2 = (carve(BH, HD) for _ in range(3))
            l2, mx, sm, en, mean, var = (carve(BH) for _ in range(6))

            def q4(k, bank):
                return q[:, 4 * H * k:4 * H * (k + 1), :], bank[:, :].rearrange("p (a c) -> p a c", c=HD)
            mq = project_tokens(q4, w["wqT"][:, :], xnT, ring, w["bqrow"][:, :].rearrange("p (a c) -> p a c", c=HD), lw)
            m = V(lambda e, i: e.tensor_tensor(t1, q, q, ALU.mult), mq)
            m = V(lambda e, i: e.tensor_reduce(l2, t1, AX.X, ALU.add), m)
            ml = A(lambda e, i: e.activation(l2, l2, ACT.Sqrt), m)
            m = V(lambda e, i: e.tensor_reduce(mean, q, AX.X, ALU.add), mq)
            m = V(lambda e, i: e.tensor_scalar(mean, mean, 1.0 / HD, None, ALU.mult), m)
            m = V(lambda e, i: e.tensor_tensor(t1, q, bc(mean, 2, HD), ALU.subtract), m)
            m = V(lambda e, i: e.tensor_tensor(t1, t1, t1, ALU.mult), m)
            m = V(lambda e, i: e.tensor_reduce(var, t1, AX.X, ALU.add), m)
            mvar = V(lambda e, i: e.tensor_scalar(var, var, 1.0 / (HD - 1), 0.2, ALU.mult, ALU.mult), m)
            m = V(lambda e, i: e.tensor_reduce(mx, q, AX.X, ALU.max), mq)
            mq2 = V(lambda e, i: e.tensor_tensor(q, q, bc(mx, 2, HD), ALU.subtract), m)
            m = A(lambda e, i: e.activation(t2, q, ACT.Exp), mq2)
            m = V(lambda e, i: e.tensor_reduce(sm, t2, AX.X, ALU.add), m)
            m = A(lambda e, i: e.activation(sm, sm, ACT.Ln), m)
            m = V(lambda e, i: e.tensor_tensor(q, q, bc(sm, 2, HD), ALU.subtract), m)
            me = A(lambda e, i: e.activation(t2, q, ACT.Exp), m)
            m = V(lambda e, i: e.tensor_scalar(t1, t2, 1.0e-9, None, ALU.add), me, mvar)
            m = A(lambda e, i: e.activation(t1, t1, ACT.Ln), m)
            m = V(lambda e, i: e.tensor_tensor(t1, t1, t2, ALU.mult), m)
            m = V(lambda e, i: e.tensor_reduce(en, t1, AX.X, ALU.add), m)
            m = V(lambda e, i: e.scalar_tensor_tensor(var, en, -0.3, var, ALU.mult, ALU.add), m, mvar)
            m = V(lambda e, i: e.scalar_tensor_tensor(var, l2, 0.5, var, ALU.mult, ALU.add), m, ml)
            m = M(lambda e, i: e.transpose(banks[7][:, 0:P], var, ident[:, :]), m)
            sc, sc2, iota, kp = (carve(P) for _ in range(4))
            c1 = [carve(1) for _ in range(4)]
            top, idf = carve(16), carve(16)
            idx = sb("top_index", [P, 16], U32)
            ms = V(lambda e, i: e.tensor_copy(sc, banks[7][:, 0:P]), m)
            mu, sd, fac, tmp = c1
            m = V(lambda e, i: e.tensor_reduce(mu, sc, AX.X, ALU.add), ms)
            m = V(lambda e, i: e.tensor_scalar(mu, mu, 1.0 / P, None, ALU.mult), m)
            m = V(lambda e, i: e.tensor_scalar(sc2, sc, mu, None, ALU.subtract), m)
            m = V(lambda e, i: e.tensor_tensor(sc2, sc2, sc2, ALU.mult), m)
            m = V(lambda e, i: e.tensor_reduce(sd, sc2, AX.X, ALU.add), m)
            m = V(lambda e, i: e.tensor_scalar(sd, sd, 1.0 / (P - 1), None, ALU.mult), m)
            m = A(lambda e, i: e.activation(sd, sd, ACT.Sqrt), m)
            m = V(lambda e, i: e.tensor_scalar(tmp, mu, 1.0e-6, None, ALU.add), m)
            m = V(lambda e, i: e.reciprocal(tmp, tmp), m)
            m = V(lambda e, i: e.scalar_tensor_tensor(fac, sd, tmp, sd, ALU.mult, ALU.bypass), m)
            m = V(lambda e, i: e.tensor_scalar(fac, fac, float(MAX_F), None, ALU.mult), m)
            m = V(lambda e, i: e.tensor_scalar(fac, fac, -100.0, 100.0, ALU.max, ALU.min), m)
            m = V(lambda e, i: e.tensor_scalar(fac, fac, 12582912.0, None, ALU.add), m)
            m = V(lambda e, i: e.tensor_scalar(fac, fac, 12582912.0, None, ALU.subtract), m)
            m = V(lambda e, i: e.tensor_scalar(fac, fac, float(MIN_F), float(MAX_F), ALU.max, ALU.min), m)
            pick, blk = carve(P), carve(P)
            mp = G(lambda e, i: e.memset(pick, 1.0))
            p3 = pick.rearrange("p (b h) -> p b h", h=H)
            mp = select(p3, [[-H, NB], [0, H]], 0, 1, ALU.is_equal, 0.0, mp)
            m = M(lambda e, i: e.matmul(banks[7][:, P:P + 1], pick, fac, start=True, stop=True), m, mp)
            mcount = V(lambda e, i: e.tensor_copy(fac, banks[7][:, P:P + 1]), m)
            m = V(lambda e, i: e.max(top[:, 0:8], sc), ms)
            m1 = V(lambda e, i: e.max_index(idx[:, 0:8], top[:, 0:8], sc), m)
            m = V(lambda e, i: e.match_replace(sc2, top[:, 0:8], sc, -3.0e38), m, m1)
            m2 = V(lambda e, i: e.max(top[:, 8:16], sc2), m)
            m2 = V(lambda e, i: e.max_index(idx[:, 8:16], top[:, 8:16], sc2), m2)
            m = V(lambda e, i: e.tensor_copy(idf, idx[:, :]), m1, m2)
            mi = G(lambda e, i: e.iota(iota, pattern=[[1, P]], base=0, channel_multiplier=0,
                                       allow_small_or_imprecise_dtypes=True))
            act = carve(16)
            for j in range(MAX_F):
                m = V(lambda e, i, j=j: e.tensor_scalar(act[:, j:j + 1], fac, float(j) + 0.5, 1000.0, ALU.is_lt,
                                                        ALU.mult), m, mcount)
            m = V(lambda e, i: e.tensor_tensor(idf[:, 0:MAX_F], idf[:, 0:MAX_F], act[:, 0:MAX_F], ALU.add), m)
            m = V(lambda e, i: e.tensor_scalar(kp, iota, idf[:, 0:1], None, ALU.is_equal), m, mi)
            for j in range(1, MAX_F):
                m = V(lambda e, i, j=j: e.scalar_tensor_tensor(kp, iota, idf[:, j:j + 1], kp, ALU.is_equal, ALU.add), m)
            m = M(lambda e, i: e.transpose(banks[7][:, 2 * P:3 * P], kp, ident[:, :]), m)
            V(lambda e, i: e.tensor_copy(keepT, banks[7][:, 2 * P:3 * P]), m)
            used[0] = 2 * T + NB * H * 9 + BH
            attention("L3_attn: batch", qT, kT, v, None, w["woT"][:, :], bias=w["bo"][:, :],
                      keep=lambda b: keepT[:, ds(b * H, H)])

        def layer3_cross():
            normalise("L3_xattn")
            lw = [ready["L3_xattn"], m_ctx]
            cs, cb = carve(NB), carve(NB, P)
            m = V(lambda e, i: e.tensor_reduce(cs, ctxT[:, :].rearrange("p (b t) -> p b t", t=P), AX.X, ALU.add), lw)
            m = V(lambda e, i: e.tensor_scalar(cs, cs, 1.0 / P, None, ALU.mult), m)
            mc = V(lambda e, i: e.tensor_copy(cb, bc(cs, 2, P)), m)
            for k in range(2):
                bank = banks[k]
                for j in range(4):
                    b = 4 * k + j
                    M(lambda e, i, b=b, j=j, bank=bank: e.matmul(bank[:, j * P:(j + 1) * P], xnT[:, b * P:(b + 1) * P],
                                                                 W["L3_xattn_W1T"][:, :], start=True, stop=False),
                      mc, lw, signal=False)
                    m = M(lambda e, i, b=b, j=j, bank=bank: e.matmul(bank[:, j * P:(j + 1) * P], cb[:, b, :],
                                                                     W["L3_xattn_W2T"][:, :], start=False, stop=True))
                xs = x[:, k * BANK:(k + 1) * BANK]
                m = V(lambda e, i, xs=xs, bank=bank: e.tensor_tensor(xs, xs, bank[:, :], ALU.add), m)
                V(lambda e, i, k=k: e.tensor_tensor(x3[:, 4 * k:4 * k + 4, :], x3[:, 4 * k:4 * k + 4, :],
                                                    bc(W["L3_xattn_b"][:, :], 1, 4), ALU.add), m)

        def layer3_experts():
            normalise("L3_ffn")
            lw = ready["L3_ffn"]
            GD = 16
            wg, wgT = W["L3_ffn_wg"], carve(NE, parts=GD)
            sq, nr = carve(GD, parts=NE), carve(1, parts=NE)
            m = V(lambda e, i: e.tensor_tensor(sq, wg[:, :], wg[:, :], ALU.mult), lw)
            m = V(lambda e, i: e.tensor_reduce(nr, sq, AX.X, ALU.add), m)
            m = A(lambda e, i: e.activation(nr, nr, ACT.Sqrt), m)
            m = V(lambda e, i: e.tensor_scalar(nr, nr, 1.0e-4, None, ALU.max), m)
            m = V(lambda e, i: e.reciprocal(nr, nr), m)
            m = V(lambda e, i: e.tensor_scalar(sq, wg[:, :], nr, None, ALU.mult), m)
            m = M(lambda e, i: e.transpose(banks[6][0:GD, 0:NE], sq, ident[0:NE, 0:NE]), m)
            mw = V(lambda e, i: e.tensor_copy(wgT, banks[6][0:GD, 0:NE]), m)
            xr = carve(T, parts=GD)
            mr = []
            for k in range(2):
                c = slice(k * BANK, (k + 1) * BANK)
                m = M(lambda e, i, k=k, c=c: e.matmul(banks[4 + k][0:GD, :], W["L3_ffn_wg_redT"][:, :], xnT[:, c],
                                                      start=True, stop=True), lw)
                mr.append(evacuate(xr[:, c], banks[4 + k][0:GD, :], k, m))
            lg, m = token_logits(wgT, NE, xr, mw, mr)
            m = V(lambda e, i: e.tensor_copy(gv, lg), m)
            m = soft8(gv, gc, gmx, gsm, m)
            m = ranked(gc, gk, 1, gt, gr1, gr2, m)
            m = V(lambda e, i: e.tensor_tensor(gc, gc, gk, ALU.mult), m)
            add_expert_bias(gc, W["L3_ffn_b2"][:, :], m)
            half = NE * FF
            experts("L3_ffn: experts", gc, bufA[:, 0:half], bufA[:, half:2 * half], W["L3_ffn_b1T"][:, :], m_late["L3_ffn"])

        half = NE * FF
        m_late = {}
        layer0_attention()
        layer0_cross() if last_layer > 1 else None
        if last_layer > 2:
            gb0 = bc(W["L0_ffn_gate_b"][:, :], 1, NB)
            mixture("L0_ffn", W["L0_ffn_gate_w"], gb0, "logits", bufA[:, 0:half], bufA[:, half:2 * half],
                    W["L0_ffn_b1T"], W["L0_ffn_b2"], m_A)
        if last_layer > 3:
            layer1_recurrence()
        if last_layer > 4:
            layer1_cross()
        if last_layer > 5:
            mixture("L1_ffn", W["L1_ffn_Wg"], bc(W["L1_ffn_bg"][:, :], 1, NB), "probabilities", bufB[:, 0:half],
                    bufB[:, half:2 * half], W["L1_ffn_b1T"], W["L1_ffn_b2"], m_B)
        if last_layer > 6:
            layer2_attention()
        if last_layer > 7:
            layer2_cross()
        if last_layer > 8:
            layer2_experts()
        if last_layer > 9:
            layer3_attention()
        if last_layer > 10:
            layer3_cross()
        if last_layer > 11:
            layer3_experts()

        fl.segment("out")
        fl.semaphore("stored")
        stored = D("stored", out, x[:, :].rearrange("p (b f) -> p b f", f=P), end_marks(fl, -2))
        fl.put("sync", lambda e, i: e.nop(), [stored, list(ready.values()), m_ctx, m_pad, m_A, m_B, list(m_late.values())],
               sem=False)

        block = ctx.enter_context(nc.Block())

        @block.sync
        def _(eng):
            fl.run("sync", eng)

        @block.gpsimd
        def _(eng):
            fl.run("gpsimd", eng)

        @block.scalar
        def _(eng):
            fl.run("scalar", eng)

        @block.tensor
        def _(eng):
            fl.run("tensor", eng)

        @block.vector
        def _(eng):
            fl.run("vector", eng)


def end_marks(fl, at=-1):
    n = len(fl.segments) + at
    return [(n, e, k) for e, k in fl.segments[n]["count"].items() if e in ENGINES[1:]]


def lay_out(inputs):
    a = {k: np.asarray(v) for k, v in inputs.items()}
    out = {}

    def rep(v, n=P):
        return np.broadcast_to(v.reshape(1, -1), (n, v.size))

    out["x"] = a["x"].transpose(1, 0, 2).reshape(P, T)
    out["ctxT"] = a["ctx_1024"].transpose(2, 0, 1).reshape(P, T)
    out["mask"] = a["mask_BxS2_bf0"].reshape(T)
    for n in ("Wq", "Wk", "Wv", "Wo"):
        out[f"L0_attn_{n}"] = a[f"L0_attn_{n}"]
        out[f"L0_xattn_{n}T"] = a[f"L0_xattn_{n}"].T
    for n in ("Wck", "Wcv"):
        out[f"L0_attn_{n}R"] = np.tile(a[f"L0_attn_{n}"].reshape(G0, HD, HD).transpose(1, 0, 2).reshape(HD, -1), (H, 1))
    out["L0_attn_WgR"] = np.tile(a["L0_attn_Wg"], (H, 1))
    out["L0_attn_bg"] = rep(a["L0_attn_bg"])
    out["L0_ffn_gate_w"] = a["L0_ffn_gate_w"]
    out["L0_ffn_gate_b"] = rep(a["L0_ffn_gate_b"])
    out["L1_ffn_Wg"] = a["L1_ffn_Wg"]
    out["L1_ffn_bg"] = rep(a["L1_ffn_bg"])
    for layer, w1, w2 in (("L0", "w1", "w2"), ("L1", "W1", "W2"), ("L3", "w1", "w2")):
        out[f"{layer}_ffn_{w1}"] = a[f"{layer}_ffn_{w1}"].transpose(1, 0, 2).reshape(P, NE * FF)
        w = a[f"{layer}_ffn_{w2}"].reshape(NE, FF // P, P, P)
        out[f"{layer}_ffn_{w2}"] = w.transpose(2, 0, 1, 3).reshape(P, NE * FF)
        out[f"{layer}_ffn_b1T"] = a[f"{layer}_ffn_b1"].reshape(NE * FF // P, P).T
        out[f"{layer}_ffn_b2"] = a[f"{layer}_ffn_b2"]
    out["L1_attn_WiT"] = a["L1_attn_Wi"].T
    out["L1_attn_conv_w"] = a["L1_attn_conv_w"].reshape(2, HC, KC).transpose(1, 0, 2).reshape(HC, 2 * KC)
    out["L1_attn_conv_b"] = a["L1_attn_conv_b"].reshape(2, HC).T
    out["L1_attn_WgT"] = a["L1_attn_Wg"].T.reshape(2, HC, 2 * HID).transpose(1, 0, 2).reshape(HC, 4 * HID)
    out["L1_attn_bg"] = a["L1_attn_bg"].reshape(4, HC).T
    out["L1_attn_forget_base"] = a["L1_attn_forget_base"].reshape(2, HC).T
    out["L1_attn_WoT"] = a["L1_attn_Wo"].T.reshape(2, HC, P).transpose(1, 0, 2).reshape(HC, 2 * P)
    for n in "qkv":
        wt = a[f"L1_xattn_W{n}"].T
        out[f"L1_xattn_W{n}T"] = np.concatenate([wt, wt[:, 0:24]], axis=1)
        b8 = a[f"L1_xattn_b{n}"].reshape(H, HD).T
        out[f"L1_xattn_b{n}8"] = np.tile(b8, (P // HD, 1))
    out["slopes"] = rep(alibi_slopes().reshape(NPAIR // 2, 2, 2, 2).transpose(0, 2, 1, 3))
    w = a["L2_attn_W_qkv"]
    wq = w[:, 0:QH * DH].reshape(P, NPAIR, 2, 2, DH).transpose(0, 1, 3, 2, 4).reshape(P, QH * DH)
    out["L2_attn_Wqkv"] = np.concatenate([wq, w[:, QH * DH:]], axis=1)
    out["L2_attn_Wout"] = a["L2_attn_W_out"].reshape(QH * DH // P, P, P).transpose(1, 0, 2).reshape(P, QH * DH)
    for n in ("Wq", "Wk", "Wv", "Wo"):
        out[f"L2_xattn_{n}"] = a[f"L2_xattn_{n}"]
    for n in ("bq", "bk"):
        out[f"L2_xattn_{n}"] = a[f"L2_xattn_{n}"].reshape(P, 1)
        out[f"L3_attn_{n}"] = a[f"L3_attn_{n}"].reshape(P, 1)
    out["L2_xattn_bv"] = rep(np.tile(a["L2_xattn_bv"], 4))
    out["L2_xattn_bo"] = rep(a["L2_xattn_bo"])
    gu = np.concatenate([np.concatenate([a["L2_ffn_Wg"], a["L2_ffn_Wu"]], axis=1),
                         np.concatenate([a["L2_ffn_Wg_s"], a["L2_ffn_Wu_s"]], axis=0)[None]], axis=0)
    out["L2_ffn_Wgu"] = gu.transpose(2, 0, 1).reshape(P, (NE + 1) * 2 * FI)
    wd = np.concatenate([a["L2_ffn_Wd"], a["L2_ffn_Wd_s"][None]], axis=0).transpose(0, 2, 1)
    out["L2_ffn_Wd"] = wd.reshape(NE + 1, FI // P, P, P).transpose(2, 0, 1, 3).reshape(P, (NE + 1) * FI)
    out["L2_ffn_WrT"] = a["L2_ffn_Wr"].T
    out["L2_ffn_rb"] = rep(a["L2_ffn_rb"])
    for n in ("wq", "wk", "wv", "wo"):
        out[f"L3_attn_{n}T"] = a[f"L3_attn_{n}"].T
    out["L3_attn_bqrow"] = rep(np.tile(a["L3_attn_bq"], 4))
    out["L3_attn_bv"] = rep(np.tile(a["L3_attn_bv"], 4))
    out["L3_attn_bo"] = rep(a["L3_attn_bo"])
    out["L3_xattn_W1T"] = a["L3_xattn_W"][:, 0:P].T
    out["L3_xattn_W2T"] = a["L3_xattn_W"][:, P:].T
    out["L3_xattn_b"] = rep(a["L3_xattn_b"])
    out["L3_ffn_wg_redT"] = a["L3_ffn_wg_red"].T
    out["L3_ffn_wg"] = a["L3_ffn_wg"]
    return {k: np.ascontiguousarray(v) for k, v in out.items()}


def alibi_slopes():
    base = 2.0 ** (-(2.0 ** (-(np.log2(QH) - 3))))
    return (base ** np.arange(1, QH + 1, dtype=np.float32)).astype(np.float32)


def kernel(**inputs):
    import concourse.bacc as bacc
    from concourse.bass_utils import run_bass_kernel_spmd

    arrays = lay_out(inputs)
    nc = bacc.Bacc("TRN2", target_bir_lowering=False, num_devices=1)
    d = {n: nc.dram_tensor(f"in_{n}", list(v.shape), mybir.dt.from_np(v.dtype), kind="ExternalInput").ap()
         for n, v in arrays.items()}
    out = nc.dram_tensor("out_0", [NB, P, P], F32, kind="ExternalOutput").ap()
    build_program(nc, d, out.rearrange("b t f -> t b f"))
    r = run_bass_kernel_spmd(nc, [{f"in_{n}": v for n, v in arrays.items()}], core_ids=[0])
    return r.results[0]["out_0"]
```

```python
from contextlib import ExitStack

import numpy as np

import concourse.bass as bass
from concourse import mybir

F32 = mybir.dt.float32
F32R = mybir.dt.float32r
U8 = mybir.dt.uint8
U32 = mybir.dt.uint32
ALU = mybir.AluOpType
ACT = mybir.ActivationFunctionType
AX = mybir.AxisListType
ds = bass.ds

P = 128
NB = 8
T = NB * P
H = 16
HD = 8
NE = 8
BANK = 512
BIG = 1.0e30
NEG = -1.0e9
EPS = 1.0e-5
G0 = 16
NBLK = P // G0
TOP_BLOCKS = 4
WIN = 32
HID = 192
HC = HID // 2
KC = 4
QH, KVH, DH = 32, 16, 64
NPAIR = KVH // 2
FF = 512
FI = 256
MIN_F, MAX_F = 3, 10
ARENA = 19500
ENGINES = ("sync", "gpsimd", "scalar", "tensor", "vector")


class Flow:

    def __init__(self, nc, ctx):
        self.nc, self.ctx = nc, ctx
        self.sems = {e: ctx.enter_context(nc.semaphore(f"done_{e}")) for e in ENGINES}
        self.segments = []
        self.base = {}

    def semaphore(self, name):
        self.sems[name] = self.ctx.enter_context(self.nc.semaphore(name))
        return name

    def segment(self, name, trips=1):
        if self.segments:
            last = self.segments[-1]
            for s, k in last["count"].items():
                self.base[s] = self.base.get(s, 0) + k * last["trips"]
        self.segments.append(dict(name=name, trips=trips, base=dict(self.base), count={},
                                  queue={e: [] for e in ENGINES}))

    def put(self, engine, make, after, sem=None, step=1):
        seg = self.segments[-1]
        waits = []

        def add(a):
            if a is None:
                return
            if isinstance(a, list):
                for x in a:
                    add(x)
            else:
                waits.append(a)
        add(list(after))
        mark = None
        if sem is not False:
            name = sem or engine
            seg["count"][name] = seg["count"].get(name, 0) + step
            mark = (len(self.segments) - 1, name, seg["count"][name])
            signal = (name, step)
        else:
            signal = None
        seg["queue"][engine].append((make, waits, signal))
        return mark

    def run(self, engine, eng):
        for at, seg in enumerate(self.segments):
            queue = seg["queue"][engine]
            if not queue:
                continue
            if seg["trips"] == 1:
                self.issue(engine, eng, at, seg, queue, 0)
            else:
                with eng.Fori(0, seg["trips"]) as i:
                    self.issue(engine, eng, at, seg, queue, i)

    def issue(self, engine, eng, at, seg, queue, i):
        looped = seg["trips"] > 1
        seen = {}

        def wait(name, value, per_trip):
            eng.wait_ge(self.sems[name], i * per_trip + value if looped and per_trip else value)

        if engine != "sync":
            for other in ENGINES[1:]:
                start, per_trip = seg["base"].get(other, 0), seg["count"].get(other, 0)
                if start or (looped and per_trip):
                    wait(other, start, per_trip)
        for make, waits, signal in queue:
            need = {}
            for where, name, k in waits:
                if where == at:
                    need[(name, True)] = max(need.get((name, True), 0), k)
                elif name not in ENGINES[1:] or engine == "sync":
                    s = self.segments[where]
                    total = s["base"].get(name, 0) + (s["trips"] - 1) * s["count"][name] + k
                    need[(name, False)] = max(need.get((name, False), 0), total)
            for (name, here), k in need.items():
                if seen.get((name, here), 0) >= k:
                    continue
                seen[(name, here)] = k
                if here:
                    wait(name, seg["base"].get(name, 0) + k, seg["count"][name])
                else:
                    eng.wait_ge(self.sems[name], k)
            ins = make(eng, i)
            if signal:
                ins.then_inc(self.sems[signal[0]], signal[1])


class Ring:

    def __init__(self, buffers):
        self.buffers, self.at, self.busy = buffers, 0, [[] for _ in buffers]

    def take(self):
        n = self.at % len(self.buffers)
        self.at += 1
        freed, self.busy[n] = self.busy[n], []
        return n, self.buffers[n], freed

    def give(self, n, *marks):
        self.busy[n] += list(marks)


def build_program(nc, d, out):
    ctx = ExitStack()
    with ctx:
        fl = Flow(nc, ctx)

        def sb(name, shape, dt=F32):
            return ctx.enter_context(nc.sbuf_tensor(name, shape, dt))

        def V(make, *after):
            return fl.put("vector", make, after)

        def A(make, *after):
            return fl.put("scalar", make, after)

        def G(make, *after):
            return fl.put("gpsimd", make, after)

        def M(make, *after, signal=True):
            return fl.put("tensor", make, others(after), sem=None if signal else False)

        def others(after):
            return [others(a) if isinstance(a, (list, tuple)) and not is_mark(a) else a for a in after
                    if not (is_mark(a) and a[1] == "tensor")]

        def is_mark(a):
            return isinstance(a, tuple) and len(a) == 3 and isinstance(a[1], str)

        def D(sem, dst, src, *after):
            return fl.put("sync", lambda e, i: e.dma_start(dst, src), after, sem=sem, step=16)

        def bc(ap, axis, n):
            ap = ap.unsqueeze(axis)
            shape = list(ap.shape)
            shape[axis] = n
            return ap.broadcast_to(shape)

        x = sb("x", [P, T])
        xnT = sb("xnT", [P, T])
        ctxT = sb("ctxT", [P, T])
        bufA = sb("bufA", [P, 2 * NE * FF])
        bufB = sb("bufB", [P, 2 * NE * FF])
        arena = sb("arena", [P, ARENA])
        banks = [ctx.enter_context(nc.psum_tensor(f"bank{n}", [P, BANK], F32)) for n in range(8)]
        used = [0]

        def fresh():
            used[0] = 0

        def carve(*shape, parts=P):
            n = int(np.prod(shape))
            v = arena[0:parts, used[0]:used[0] + n]
            used[0] += n
            assert used[0] <= ARENA, used[0]
            if len(shape) == 2:
                v = v.rearrange("p (a b) -> p a b", b=shape[1])
            elif len(shape) == 3:
                v = v.rearrange("p (a b c) -> p a b c", b=shape[1], c=shape[2])
            return v

        def loaded(names, sem):
            fl.semaphore(sem)
            tiles, mark = {}, None
            for n in names:
                shape = list(d[n].shape)
                tiles[n] = sb(f"w_{n}", shape)
                mark = D(sem, tiles[n][tuple(slice(None) for _ in shape)], d[n])
            return tiles, mark

        fl.segment("constants")
        fl.semaphore("in_x")
        m_x = D("in_x", x[:, :], d["x"])
        fl.semaphore("in_ctx")
        W = {}
        ready = {}
        for group, names in (
            ("L0_attn", ("L0_attn_Wq", "L0_attn_Wk", "L0_attn_Wv", "L0_attn_Wo", "L0_attn_WckR", "L0_attn_WcvR",
                         "L0_attn_WgR", "L0_attn_bg")),
            ("L0_xattn", ("L0_xattn_WqT", "L0_xattn_WkT", "L0_xattn_WvT", "L0_xattn_WoT")),
            ("L0_ffn", ("L0_ffn_gate_w", "L0_ffn_gate_b", "L0_ffn_b1T", "L0_ffn_b2")),
            ("L1_attn", ("L1_attn_WiT", "L1_attn_conv_w", "L1_attn_conv_b", "L1_attn_WgT", "L1_attn_bg",
                         "L1_attn_forget_base", "L1_attn_WoT")),
            ("L1_xattn", ("L1_xattn_WqT", "L1_xattn_WkT", "L1_xattn_WvT", "L1_xattn_bq8", "L1_xattn_bk8",
                          "L1_xattn_bv8")),
            ("L1_ffn", ("L1_ffn_Wg", "L1_ffn_bg", "L1_ffn_b1T", "L1_ffn_b2")),
            ("L2_attn", ("slopes",)),
            ("L2_xattn", ("L2_xattn_Wq", "L2_xattn_bq", "L2_xattn_Wk", "L2_xattn_bk", "L2_xattn_Wv",
                          "L2_xattn_bv", "L2_xattn_Wo", "L2_xattn_bo")),
            ("L2_ffn", ("L2_ffn_WrT", "L2_ffn_rb")),
            ("L3_attn", ("L3_attn_wqT", "L3_attn_bq", "L3_attn_bqrow", "L3_attn_wkT", "L3_attn_bk",
                         "L3_attn_wvT", "L3_attn_bv", "L3_attn_woT", "L3_attn_bo")),
            ("L3_xattn", ("L3_xattn_W1T", "L3_xattn_W2T", "L3_xattn_b")),
            ("L3_ffn", ("L3_ffn_wg_redT", "L3_ffn_wg", "L3_ffn_b1T", "L3_ffn_b2")),
        ):
            tiles, ready[group] = loaded(names, f"in_{group}")
            W.update(tiles)
            if group == "L0_attn":
                m_ctx = D("in_ctx", ctxT[:, :], d["ctxT"])
            if group == "L0_ffn":
                fl.semaphore("in_A")
                fl.semaphore("in_B")
                half = NE * FF
                D("in_A", bufA[:, 0:half], d["L0_ffn_w1"])
                m_A = D("in_A", bufA[:, half:2 * half], d["L0_ffn_w2"])
                D("in_B", bufB[:, 0:half], d["L1_ffn_W1"])
                m_B = D("in_B", bufB[:, half:2 * half], d["L1_ffn_W2"])
        pad_u8 = sb("pad_u8", [P, T], U8)
        fl.semaphore("in_pad")
        m_pad = D("in_pad", pad_u8[:, :], d["mask"].partition_broadcast(P))

        ident = sb("ident", [P, P])
        mask16 = sb("mask16", [P, H])
        mask4 = sb("mask4", [P, 4])
        causal = sb("causal", [P, P])
        window = sb("window", [P, P])
        tri = sb("tri", [P, P])
        blk01 = sb("blk01", [P, NBLK])
        blkneg = sb("blkneg", [P, NBLK])
        anyblk = sb("anyblk", [P, 1])
        below = sb("below", [P, 8, 8])
        nm7 = sb("nm7", [P, 8])

        def select(t, pattern, base, mult, op, fill, *after):
            return G(lambda e, i: e.affine_select(out=t, in_=t, compare_op=op, fill=fill, base=base,
                                                  pattern=pattern, channel_multiplier=mult), *after)

        def filled(t, v):
            return G(lambda e, i: e.memset(t, v))

        select(ident[:, :], [[-1, P]], 0, 1, ALU.not_equal, 1.0, filled(ident[:, :], 0.0))
        m = filled(mask16[:, :], 1.0)
        m = select(mask16[:, :], [[-HD, H]], 0, 1, ALU.is_ge, 0.0, m)
        m16 = select(mask16[:, :], [[HD, H]], HD - 1, -1, ALU.is_ge, 0.0, m)
        V(lambda e, i: e.tensor_reduce(mask4[:, :], mask16[:, :].rearrange("p (g j) -> p j g", j=4),
                                       AX.X, ALU.add), m16)
        select(causal[:, :], [[-1, P]], 0, 1, ALU.is_ge, -BIG, filled(causal[:, :], 0.0))
        m = select(window[:, :], [[-1, P]], 0, 1, ALU.is_ge, -BIG, filled(window[:, :], 0.0))
        select(window[:, :], [[1, P]], WIN, -1, ALU.is_ge, -BIG, m)
        select(tri[:, :], [[1, P]], 0, -1, ALU.is_ge, 0.0, filled(tri[:, :], 1.0))
        select(blk01[:, :], [[-G0, NBLK]], -G0, 1, ALU.is_ge, 0.0, filled(blk01[:, :], 1.0))
        select(blkneg[:, :], [[-G0, NBLK]], -G0, 1, ALU.is_ge, NEG, filled(blkneg[:, :], 0.0))
        select(anyblk[:, :], [[0, 1]], -G0, 1, ALU.is_ge, 0.0, filled(anyblk[:, :], 1.0))
        select(below[:, :, :], [[1, 8], [-1, 8]], 0, 0, ALU.is_gt, 0.0, filled(below[:, :, :], 1.0))
        G(lambda e, i: e.iota(nm7[:, :], pattern=[[1, 8]], base=-7, channel_multiplier=0,
                              allow_small_or_imprecise_dtypes=True))

        def b_(ap):
            return lambda b: ap[:, ds(b * P, P)]

        stat = {n: sb(f"norm_{n}", shape) for n, shape in (("parts", [P, NB, 6]), ("mean_var", [P, NB, 2]),
                                                           ("std", [P, NB]), ("rstd", [P, NB]))}

        def normalise(name, *after, loads=()):
            last = end_marks(fl)
            fl.segment(name)
            marks = [D(sem, dst, d[src], last) for sem, dst, src in loads]
            fresh()
            x3 = x[:, :].rearrange("p (b f) -> p b f", f=P)
            xc = carve(NB, P)
            A(lambda e, i: e.activation(stat["rstd"][:, 0:1], blk01[:, 0:1], ACT.Sqrt))
            ms = []
            for b in range(NB):
                m = V(lambda e, i, b=b: e.bn_stats(stat["parts"][:, b, :], x3[:, b, :]), *after)
                ms.append(m)
            for b in range(NB):
                m = V(lambda e, i, b=b: e.bn_aggr(stat["mean_var"][:, b, :], stat["parts"][:, b, :]), ms[b])
            std, rstd = stat["std"][:, :], stat["rstd"][:, :]
            m = V(lambda e, i: e.tensor_scalar(std, stat["mean_var"][:, :, 1], EPS, None, ALU.add), m)
            m = A(lambda e, i: e.activation(std, std, ACT.Sqrt), m)
            mr = V(lambda e, i: e.reciprocal(rstd, std), m)
            for k in range(2):
                for b in range(4 * k, 4 * k + 4):
                    mn = V(lambda e, i, b=b: e.tensor_scalar(xc[:, b, :], x3[:, b, :], stat["mean_var"][:, b, 0:1],
                                                             rstd[:, b:b + 1], ALU.subtract, ALU.mult), mr)
                    mt = M(lambda e, i, b=b: e.transpose(banks[b // 4][:, (b % 4) * P:(b % 4 + 1) * P],
                                                         xc[:, b, :], ident[:, :]), mn)
                evacuate(xnT[:, k * BANK:(k + 1) * BANK], banks[k][:, :], k, mt)
            fl.segment(name + ": work")
            fresh()
            return marks

        def evacuate(dst, src, turn, *after):
            if turn % 2:
                return V(lambda e, i: e.tensor_copy(dst, src), *after)
            return A(lambda e, i: e.activation(dst, src, ACT.Copy), *after)

        def project(dst, w, src, ring, bias=None, *after):
            marks = []
            for k in range(2):
                n, bank, freed = ring.take()
                c = slice(k * BANK, (k + 1) * BANK)
                m = M(lambda e, i, bank=bank, c=c: e.matmul(bank[:, :], w, src[:, c], start=True, stop=True),
                      freed, *after)
                if bias is None:
                    m = evacuate(dst[:, c], bank[:, :], k, m)
                else:
                    m = V(lambda e, i, bank=bank, c=c: e.tensor_scalar(dst[:, c], bank[:, :], bias, None, ALU.add), m)
                ring.give(n, m)
                marks.append(m)
            return marks

        def project_tokens(dst4, w, src, ring, bias=None, *after):
            marks = []
            for k in range(2):
                n, bank, freed = ring.take()
                for j in range(4):
                    c = (4 * k + j) * P
                    m = M(lambda e, i, bank=bank, j=j, c=c: e.matmul(bank[:, j * P:(j + 1) * P], src[:, c:c + P], w,
                                                                      start=True, stop=True), freed, *after)
                dst, view = dst4(k, bank)
                if bias is None:
                    m = evacuate(dst, view, k, m)
                else:
                    m = V(lambda e, i, dst=dst, view=view: e.tensor_tensor(dst, view, bias, ALU.add), m)
                ring.give(n, m)
                marks.append(m)
            return marks

        def tokens(dst):
            return lambda k, bank: (dst[:, k * BANK:(k + 1) * BANK], bank[:, :])

        def padded_values(count):
            tiles = [carve(H, 32) for _ in range(count)]
            for t in tiles:
                m = G(lambda e, i, t=t: e.memset(t, 0.0))
                G(lambda e, i, t=t: e.memset(t[:, :, HD:HD + 1], 1.0), m)
            return tiles

        def ranked(v, keep, ge, before, r1, r2, *after):
            rows = v.shape[1]
            m1 = V(lambda e, i: e.memset(r1[:, :, 0:1], 0.0), *after)
            m2 = G(lambda e, i: e.memset(r2, 0.0), *after)
            for n in range(7, 0, -1):
                c = before[:, rows * n * (n - 1) // 2:rows * n * (n + 1) // 2].rearrange("p (r m) -> p r m", m=n)
                m = V(lambda e, i, n=n, c=c: e.tensor_tensor(c, v[:, :, 0:n], v[:, :, n:n + 1].broadcast_to(
                    [P, rows, n]), ALU.is_ge), *after)
                m2 = G(lambda e, i, n=n, c=c: e.tensor_tensor(r2[:, :, 0:n], r2[:, :, 0:n], c, ALU.add), m, m2)
                m1 = V(lambda e, i, n=n, c=c: e.tensor_reduce(r1[:, :, n:n + 1], c, AX.X, ALU.add), m, m1)
            m = V(lambda e, i: e.tensor_tensor(r1, r1, bc(nm7[:, :], 1, rows), ALU.subtract), m1)
            m = V(lambda e, i: e.tensor_tensor(r1, r1, r2, ALU.subtract), m, m2)
            return V(lambda e, i: e.tensor_scalar(keep, r1, ge - 0.5, None, ALU.is_lt), m)

        def staircase(n, *stages, newest=False):
            state = [None] * n
            for step in range(n + max(lag for lag, _ in stages)):
                for lag, stage in (stages if newest else reversed(stages)):
                    if 0 <= step - lag < n:
                        state[step - lag] = stage(step - lag, state[step - lag])

        def softmax_ready(tile, heads, scale, mx, *after):
            m = V(lambda e, i: e.tensor_reduce(mx, tile, AX.X, ALU.max), *after)
            m = V(lambda e, i: e.tensor_tensor(tile, tile, bc(mx, 2, P), ALU.subtract), m)
            return A(lambda e, i: e.activation(tile, tile, ACT.Exp, scale=scale), m)

        def softmax_biased(tile, heads, scale, mx, *after):
            m = V(lambda e, i: e.tensor_reduce(mx, tile, AX.X, ALU.max), *after)
            m = V(lambda e, i: e.tensor_scalar(mx, mx, -scale, None, ALU.mult), m)
            for j in range(heads):
                me = A(lambda e, i, j=j: e.activation(tile[:, j, :], tile[:, j, :], ACT.Exp, bias=mx[:, j:j + 1],
                                                      scale=scale), m)
            return me

        def turned(ring_t, ring_p, tile, turn, *after):
            n, bank, freed = ring_t.take()
            for j in range(4):
                m = M(lambda e, i, j=j: e.transpose(bank[:, j * P:(j + 1) * P], tile[:, j * P:(j + 1) * P], ident[:, :]),
                      freed, *after)
            q, dst, freed = ring_p.take()
            c = evacuate(dst, bank[:, :], turn, m, freed)
            ring_t.give(n, c)
            return q, dst, m, c

        def turn_back(o, area, oT, *after):
            m = M(lambda e, i: e.transpose(area, o, ident[:, :]), *after)
            return A(lambda e, i: e.activation(oT, area, ACT.Copy), m)

        def add_projected(b, area, oT, w, m, bias=None):
            m = M(lambda e, i: e.matmul(area, oT, w, start=True, stop=True), m)
            m = V(lambda e, i: e.tensor_tensor(b_(x)(b(i)), b_(x)(b(i)), area, ALU.add), m)
            if bias is not None:
                m = V(lambda e, i: e.tensor_tensor(b_(x)(b(i)), b_(x)(b(i)), bias, ALU.add), m)
            return m

        def staged_heads(per, qT, kT, v, vp):
            bat = [lambda i, u=u: i * per + u for u in range(per)]
            qb, kM = [carve(P) for _ in bat], [carve(4, P) for _ in bat]
            marks = []
            for u, b in enumerate(bat):
                copy = (lambda o, s: A(lambda e, i: e.activation(o, s(i), ACT.Copy))) if u == 0 else \
                       (lambda o, s: G(lambda e, i: e.tensor_copy(o, s(i))))
                m1 = copy(qb[u], lambda i, b=b: b_(qT)(b(i)))
                m2 = (V if u == 0 else G)(lambda e, i, u=u, b=b: e.tensor_tensor(
                    kM[u], b_(kT)(b(i)).unsqueeze(1).broadcast_to([P, 4, P]), bc(mask4[:, :], 2, P), ALU.mult))
                m3 = G(lambda e, i, u=u, b=b: e.tensor_copy(vp[u][:, :, 0:HD],
                                                            b_(v)(b(i)).rearrange("p (h c) -> p h c", c=HD)))
                marks.append([[m1, m2], m3])
            return bat, qb, kM, marks

        def head_values(bank, g, pT, vp, *after):
            for j in range(4):
                m = M(lambda e, i, j=j: e.matmul(bank[32 * j:32 * j + 32, g * P:(g + 1) * P], vp[:, 4 * g + j, :],
                                                 pT[:, j * P:(j + 1) * P], start=True, stop=True), *after)
            return m

        def heads_back(bank, src, *after):
            for g in range(4):
                m = M(lambda e, i, g=g: e.transpose(bank[:, g * P:(g + 1) * P], src[:, g * P:(g + 1) * P],
                                                    ident[:, :]), *after)
            return bank[:, :].rearrange("p (h c) -> p h c", c=32), m

        def attention(name, qT, kT, v, vp, mask, wo, bias=None, keep=None):
            per = len(vp)
            fl.segment(name, NB // per)
            scale = 1.0 / float(np.sqrt(HD))
            bat, qb, kM, staged = staged_heads(per, qT, kT, v, vp)
            o, oT, rs, res = ([carve(n) for _ in range(2)] for n in (P, P, H, BANK))
            ring_s, ring_t = Ring(banks[0:2]), Ring(banks[2:4])
            ring_a, ring_p = Ring([carve(BANK) for _ in range(4)]), Ring([carve(BANK) for _ in range(3)])
            mxs = [carve(4) for _ in range(8)]
            done, copied = {}, {}

            def score(k, _):
                u, g = divmod(k, 4)
                q = slice(32 * g, 32 * g + 32)
                n, bank, freed = ring_s.take()
                m = M(lambda e, i: e.matmul(bank[:, :], qb[u][q, :], kM[u][q, :, :].rearrange("p j t -> p (j t)"),
                                            start=True, stop=True), freed, staged[u][0])
                a, tile, freed = ring_a.take()
                t3 = tile.rearrange("p (j t) -> p j t", t=P)
                s3 = bank[:, :].rearrange("p (j t) -> p j t", t=P)
                mx = mxs[k % 8]
                if mask is not None:
                    m = V(lambda e, i: e.tensor_tensor(t3, s3, bc(mask, 1, 4), ALU.add), m, freed)
                    ring_s.give(n, m)
                    return a, tile, softmax_biased(t3, 4, scale, mx, m)
                m = V(lambda e, i: e.tensor_reduce(mx, s3, AX.X, ALU.max), m, freed)
                m = V(lambda e, i: e.tensor_tensor(t3, s3, bc(mx, 2, P), ALU.subtract), m)
                ring_s.give(n, m)
                return a, tile, A(lambda e, i: e.activation(t3, t3, ACT.Exp, scale=scale), m)

            def turn(k, s):
                a, tile, m = s
                q, pT, mt, mc = turned(ring_t, ring_p, tile, 0, m)
                ring_a.give(a, mt)
                return q, pT, mc

            def values(k, s):
                u, g = divmod(k, 4)
                q, pT, m = s
                bank, w = banks[4 + u % 2], u % 2
                m = head_values(bank, g, pT, vp[u], m, staged[u][1], copied.get(u - 2))
                ring_p.give(q, m)
                if g == 3:
                    copied[u] = A(lambda e, i: e.activation(res[w], bank[:, :], ACT.Copy), m, done.get(u - 2))
                    return copied[u]

            def weigh(k, m):
                if m is None:
                    return None
                u, w = k // 4, k // 4 % 2
                o3, m = heads_back(banks[6], res[w], m, done.get(u - 1))
                m = V(lambda e, i: e.reciprocal(rs[w].unsqueeze(2), o3[:, :, HD:HD + 1]), m)
                if keep is not None:
                    m = V(lambda e, i: e.tensor_tensor(rs[w], rs[w], keep(bat[u](i)), ALU.mult), m)
                return V(lambda e, i: e.tensor_tensor(o[w].rearrange("p (h c) -> p h c", c=HD), o3[:, :, 0:HD],
                                                      bc(rs[w], 2, HD), ALU.mult), m, done.get(u - 2))

            def back(k, m):
                return m and turn_back(o[k // 4 % 2], banks[7][:, 0:P], oT[k // 4 % 2], m)

            def add(k, m):
                if m:
                    done[k // 4] = add_projected(bat[k // 4], banks[7][:, P:2 * P], oT[k // 4 % 2], wo, m, bias)

            staircase(4 * per, (0, score), (3, turn), (5, values), (6, weigh), (7, back), (8, add))

        def add_expert_bias(comb, b2, *after):
            cT = carve(T, parts=NE)
            mc = []
            for k in range(2):
                for j in range(4):
                    m = M(lambda e, i, k=k, j=j: e.transpose(banks[k][0:NE, j * P:(j + 1) * P], comb[:, 4 * k + j, :],
                                                             ident[:, :]), *after)
                mc.append(evacuate(cT[:, k * BANK:(k + 1) * BANK], banks[k][0:NE, :], k, m))
            for k in range(2):
                for j in range(4):
                    c = (4 * k + j) * P
                    m = M(lambda e, i, k=k, j=j, c=c: e.matmul(banks[2 + k][:, j * P:(j + 1) * P], cT[:, c:c + P], b2,
                                                               start=True, stop=True), mc[k])
                xs = x[:, k * BANK:(k + 1) * BANK]
                V(lambda e, i, k=k, xs=xs: e.tensor_tensor(xs, xs, banks[2 + k][:, :], ALU.add), m)

        x_high, x_low = sb("x_high", [P, T], F32R), sb("x_low", [P, T], F32R)
        w_high, w_low = ([sb(f"w_{n}{k}", [P, FF], F32R) for k in range(2)] for n in ("high", "low"))

        def split(high, low, src, *after):
            m = V(lambda e, i: e.tensor_copy(high, src(i)), *after)
            return V(lambda e, i: e.tensor_tensor(low, src(i), high, ALU.subtract), m)

        def split_tokens():
            for k in range(2):
                c = slice(k * BANK, (k + 1) * BANK)
                split(x_high[:, c], x_low[:, c], lambda i, c=c: xnT[:, c])

        def up_product(bank, part, t, f, *after):
            ws, c = slice(f * P, (f + 1) * P), slice(t * BANK, (t + 1) * BANK)
            for n, (a, b) in enumerate(((w_low[part], x_high), (w_high[part], x_low), (w_high[part], x_high))):
                m = M(lambda e, i, n=n, a=a, b=b: e.matmul(bank[:, :], a[:, ws], b[:, c], start=n == 0, stop=n == 2),
                      *after, signal=n == 2)
            return m

        def experts(name, comb, w1, w2, b1, buf_ready):
            U = 4
            fl.segment(name, NE // U)
            NF = FF // P
            w2s = [carve(FF) for _ in range(2)]
            b1s, cs = [carve(NF) for _ in range(U)], [carve(NB) for _ in range(U)]
            ring_h, ring_y = Ring(banks[0:4]), Ring(banks[4:8])
            ring_a = Ring([carve(NF, BANK) for _ in range(2)])
            staged = [[G(lambda e, i, u=u: e.tensor_copy(b1s[u], b1[:, ds((i * U + u) * NF, NF)])),
                       G(lambda e, i, u=u: e.tensor_copy(cs[u].unsqueeze(2), comb[:, :, ds(i * U + u, 1)]))]
                      for u in range(U)]
            last_x, w1_used, w2_used = {}, {}, {}

            def weights(k, _):
                u, t = divmod(k, 2)
                if t == 0:
                    p = u % 2
                    m1 = split(w_high[p][:, :], w_low[p][:, :], lambda i: w1[:, ds((i * U + u) * FF, FF)], buf_ready,
                               w1_used.get(u - 2))
                    m2 = V(lambda e, i: e.tensor_copy(w2s[p], w2[:, ds((i * U + u) * FF, FF)]), w2_used.get(u - 2))
                    placed[u] = m1, m2

            def up(k, _):
                u, t = divmod(k, 2)
                a, h, freed_h = ring_a.take()
                for f in range(NF):
                    n, bank, freed = ring_h.take()
                    mm = up_product(bank, u % 2, t, f, freed, placed[u][0])
                    m = A(lambda e, i, bank=bank, f=f: e.activation(h[:, f, :], bank[:, :], ACT.Gelu,
                                                                   bias=b1s[u][:, f:f + 1]), mm, staged[u][0], freed_h)
                    ring_h.give(n, m)
                w1_used[u] = mm
                return a, h, m

            def down(k, s):
                u, t = divmod(k, 2)
                a, h, m = s
                n, bank, freed = ring_y.take()
                for j in range(4):
                    for f in range(NF):
                        my = M(lambda e, i, j=j, f=f: e.matmul(bank[:, j * P:(j + 1) * P], h[:, f, j * P:(j + 1) * P],
                                                               w2s[u % 2][:, f * P:(f + 1) * P], start=f == 0,
                                                               stop=f == NF - 1), freed, m, placed[u][1],
                               signal=f == NF - 1)
                w2_used[u] = my
                for j in range(4):
                    xs = x[:, (4 * t + j) * P:(4 * t + j + 1) * P]
                    c = cs[u][:, 4 * t + j:4 * t + j + 1]
                    mv = V(lambda e, i, j=j, xs=xs, c=c: e.scalar_tensor_tensor(
                        xs, bank[:, j * P:(j + 1) * P], c, xs, ALU.mult, ALU.add), my, staged[u][1],
                        last_x.get((t, j)))
                    last_x[(t, j)] = mv
                ring_a.give(a, my)
                ring_y.give(n, mv)

            placed = {}
            staircase(2 * U, (0, weights), (1, up), (2, down), newest=True)

        def token_logits(w, width, src=None, *after):
            src = xnT if src is None else src
            for b in range(NB):
                m = M(lambda e, i, b=b: e.matmul(banks[7][:, b * width:(b + 1) * width], src[:, b * P:(b + 1) * P], w,
                                                 start=True, stop=True), *after)
            return banks[7][:, 0:NB * width].rearrange("p (b c) -> p b c", c=width), m

        def soft8(v, out, mx, sm, m, keep=None):
            m = V(lambda e, i: e.tensor_reduce(mx, v, AX.X, ALU.max), m)
            m = V(lambda e, i: e.tensor_tensor(out, v, bc(mx, 2, NE), ALU.subtract), m)
            m = A(lambda e, i: e.activation(out, out, ACT.Exp), m)
            if keep is not None:
                m = V(lambda e, i: e.tensor_tensor(out, out, keep, ALU.mult), m)
            m = V(lambda e, i: e.tensor_reduce(sm, out, AX.X, ALU.add), m)
            m = V(lambda e, i: e.reciprocal(sm, sm), m)
            return V(lambda e, i: e.tensor_tensor(out, out, bc(sm, 2, NE), ALU.mult), m)

        gate = dict(v=sb("gate_v", [P, NB, NE]), c=sb("gate_comb", [P, NB, NE]), r1=sb("gate_r1", [P, NB, NE]),
                    r2=sb("gate_r2", [P, NB, NE]), k=sb("gate_keep", [P, NB, NE]), mx=sb("gate_mx", [P, NB]),
                    sm=sb("gate_sm", [P, NB]), t=sb("gate_before", [P, NB * 28]))
        gv, gc, gr1, gr2, gk = (gate[n][:, :, :] for n in ("v", "c", "r1", "r2", "k"))
        gmx, gsm, gt = (gate[n][:, :] for n in ("mx", "sm", "t"))
        x3 = x[:, :].rearrange("p (b f) -> p b f", f=P)

        ckT, cvT = sb("ckT", [P, NB * NBLK]), sb("cvT", [P, NB * NBLK])

        def layer0_attention():
            normalise("L0_attn", m_x)
            ring = Ring(banks)
            w = {n: W[f"L0_attn_{n}"] for n in ("Wq", "Wk", "Wv", "Wo", "WckR", "WcvR", "WgR", "bg")}
            lw = ready["L0_attn"]
            qT, kT, vT = carve(T), carve(T), carve(T)
            mq = project(qT, w["Wq"][:, :], xnT, ring, None, lw)
            mk = project(kT, w["Wk"][:, :], xnT, ring, None, lw)
            mv = project(vT, w["Wv"][:, :], xnT, ring, None, lw)
            v = carve(T)
            project_tokens(tokens(v), w["Wv"][:, :], xnT, ring, None, lw)
            oc, sel, gl = carve(NB, P), carve(NB * H, NBLK), carve(NB, 3)
            vp = padded_values(4)
            temporary = used[0]
            diag = [carve(G0 * P) for _ in range(2)]
            mc, blocks = [], [carve(P, parts=NB * NBLK) for _ in range(2)]
            for n, src, ms, dg, dst in ((0, kT, mk, diag[0], ckT), (1, vT, mv, diag[1], cvT)):
                wr = w[("WckR", "WcvR")[n]][:, :].rearrange("p (g c) -> p g c", c=HD)
                shape = [P, G0, H, HD]
                md = V(lambda e, i, dg=dg, wr=wr: e.tensor_tensor(
                    dg.rearrange("p (g h c) -> p g h c", h=H, c=HD), wr.unsqueeze(2).broadcast_to(shape),
                    bc(mask16[:, :], 1, G0).unsqueeze(3).broadcast_to(shape), ALU.mult), lw)
                k, bank, freed = ring.take()
                NG = NB * NBLK
                for g in range(G0):
                    m = M(lambda e, i, dg=dg, src=src, bank=bank, g=g: e.matmul(
                        bank[0:NG, 0:P], src.rearrange("p (n g) -> p g n", g=G0)[:, g, :], dg[:, g * P:(g + 1) * P],
                        start=g == 0, stop=g == G0 - 1), freed, md, ms, signal=g == G0 - 1)
                m = A(lambda e, i, bank=bank, n=n: e.activation(blocks[n], bank[0:NG, 0:P], ACT.Copy), m)
                m = M(lambda e, i, bank=bank, n=n: e.transpose(bank[:, P:P + NG], blocks[n], ident[0:NG, 0:NG]), m)
                m = V(lambda e, i, dst=dst, bank=bank: e.tensor_copy(dst[:, :], bank[:, P:P + NG]), m)
                ring.give(k, m)
                mc.append(m)
            used[0] = temporary
            kcM, vcM = carve(NB, P), carve(NB, P)
            by_head = [P, NB, H, NBLK]
            mM = [V(lambda e, i, s=s, t=t: e.tensor_tensor(
                t.rearrange("p b (h n) -> p b h n", n=NBLK),
                s[:, :].rearrange("p (b n) -> p b n", n=NBLK).unsqueeze(2).broadcast_to(by_head),
                bc(mask16[:, :], 1, NB).unsqueeze(3).broadcast_to(by_head), ALU.mult), mc)
                for s, t in ((ckT, kcM), (cvT, vcM))]
            vcBD = carve(NB, P)
            pc, pcT = carve(NB * H, NBLK), kcM
            L, r1, r2 = (carve(NB * H, NBLK) for _ in range(3))
            before = carve(NB * H * 28)
            mx, sm = carve(NB * H), carve(NB * H)
            gm, gs = carve(NB), carve(NB)
            scale = 1.0 / float(np.sqrt(HD))
            ml, mbd = [], []
            for k in range(2):
                n, bank, freed = ring.take()
                for j in range(4):
                    b = 4 * k + j
                    m = M(lambda e, i, b=b, j=j, bank=bank: e.matmul(
                        bank[:, j * P:(j + 1) * P], qT[:, b * P:(b + 1) * P], kcM[:, b, :], start=True, stop=True),
                        freed, mM, mq)
                rows = slice(4 * H * k, 4 * H * (k + 1))
                m = V(lambda e, i, rows=rows, bank=bank: e.scalar_tensor_tensor(
                    L[:, rows, :], bank[:, :].rearrange("p (r n) -> p r n", n=NBLK), scale,
                    bc(blk01[:, :], 1, 4 * H), ALU.mult, ALU.mult), m)
                ring.give(n, m)
                ml.append(V(lambda e, i, rows=rows: e.tensor_tensor(L[:, rows, :], L[:, rows, :],
                                                                    bc(blkneg[:, :], 1, 4 * H), ALU.add), m))
                n, bank, freed = ring.take()
                for j in range(4):
                    m = M(lambda e, i, b=4 * k + j, j=j, bank=bank: e.transpose(bank[:, j * P:(j + 1) * P],
                                                                              vcM[:, b, :], ident[:, :]), freed, mM)
                m = A(lambda e, i, k=k, bank=bank: e.activation(
                    vcBD[:, 4 * k:4 * k + 4, :], bank[:, :].rearrange("p (b f) -> p b f", f=P), ACT.Copy), m)
                ring.give(n, m)
                mbd.append(m)
            n, bank, freed = ring.take()
            for b in range(NB):
                m = M(lambda e, i, b=b, bank=bank: e.matmul(bank[:, 3 * b:3 * b + 3], qT[:, b * P:(b + 1) * P],
                                                            w["WgR"][:, :], start=True, stop=True), freed, mq, lw)
            m = V(lambda e, i, bank=bank: e.scalar_tensor_tensor(
                gl, bank[:, 0:3 * NB].rearrange("p (b c) -> p b c", c=3), 1.0 / H, bc(w["bg"][:, :], 1, NB), ALU.mult,
                ALU.add), m)
            ring.give(n, m)
            m = V(lambda e, i: e.tensor_reduce(gm, gl, AX.X, ALU.max), m)
            m = V(lambda e, i: e.tensor_tensor(gl, gl, bc(gm, 2, 3), ALU.subtract), m)
            mg = A(lambda e, i: e.activation(gl, gl, ACT.Exp), m)
            m = V(lambda e, i: e.tensor_reduce(mx, L, AX.X, ALU.max), ml)
            m = V(lambda e, i: e.tensor_tensor(pc, L, bc(mx, 2, NBLK), ALU.subtract), m)
            me = A(lambda e, i: e.activation(pc, pc, ACT.Exp), m)
            m = V(lambda e, i: e.tensor_reduce(gs, gl, AX.X, ALU.add), mg)
            m = V(lambda e, i: e.reciprocal(gs, gs), m)
            m = V(lambda e, i: e.tensor_tensor(gl, gl, bc(gs, 2, 3), ALU.mult), m)
            mg = V(lambda e, i: e.tensor_scalar(gl[:, :, 0:1], gl[:, :, 0:1], anyblk[:, :], None, ALU.mult), m)
            m = V(lambda e, i: e.tensor_reduce(sm, pc, AX.X, ALU.add), me)
            m = V(lambda e, i: e.reciprocal(sm, sm), m)
            mp = V(lambda e, i: e.tensor_tensor(pc, pc, bc(sm, 2, NBLK), ALU.mult), m)
            pc3 = pc.rearrange("p (b h) n -> p b (h n)", h=H)
            for k in range(2):
                n, bank, freed = ring.take()
                for j in range(4):
                    m = M(lambda e, i, b=4 * k + j, j=j, bank=bank: e.transpose(bank[:, j * P:(j + 1) * P],
                                                                              pc3[:, b, :], ident[:, :]), freed, mp)
                m = A(lambda e, i, k=k, bank=bank: e.activation(
                    pcT[:, 4 * k:4 * k + 4, :], bank[:, :].rearrange("p (b f) -> p b f", f=P), ACT.Copy), m)
                ring.give(n, m)
                n, bank, freed = ring.take()
                for j in range(4):
                    m2 = M(lambda e, i, b=4 * k + j, j=j, bank=bank: e.matmul(
                        bank[:, j * P:(j + 1) * P], pcT[:, b, :], vcBD[:, b, :], start=True, stop=True),
                        freed, m, mbd)
                m = V(lambda e, i, k=k, bank=bank: e.tensor_tensor(
                    oc[:, 4 * k:4 * k + 4, :], bank[:, :].rearrange("p (b f) -> p b f", f=P),
                    gl[:, 4 * k:4 * k + 4, 0:1].broadcast_to([P, 4, P]), ALU.mult), m2, mg)
                ring.give(n, m)
            m = ranked(L, sel, TOP_BLOCKS, before, r1, r2, ml)
            V(lambda e, i: e.tensor_scalar(sel, sel, 1.0, BIG, ALU.subtract, ALU.mult), m)

            per, two = 4, range(2)
            used[0] = temporary
            fl.segment("L0_attn: batch", NB // per)
            bat, qb, kM, staged = staged_heads(per, qT, kT, v, vp)
            o, o2, oT, rs, rl = ([carve(n) for _ in two] for n in (P, P, P, H, H))
            res = [carve(BANK) for _ in two]
            ring_s, ring_t = Ring(banks[0:2]), Ring(banks[2:4])
            ring_a, ring_p = Ring([carve(BANK) for _ in range(8)]), Ring([carve(BANK) for _ in range(4)])
            mxs = [carve(4) for _ in range(16)]
            done, unpacked, copied = {}, {}, {}

            def score(k, _):
                u, g = divmod(k, 4)
                q = slice(32 * g, 32 * g + 32)
                n, bank, freed = ring_s.take()
                m = M(lambda e, i: e.matmul(bank[:, :], qb[u][q, :], kM[u][q, :, :].rearrange("p j t -> p (j t)"),
                                            start=True, stop=True), freed, staged[u][0])
                s3 = bank[:, :].rearrange("p (j t) -> p j t", t=P)
                tiles = []
                for mask in (causal, window):
                    a, tile, freed = ring_a.take()
                    t3 = tile.rearrange("p (j t) -> p j t", t=P)
                    mt = V(lambda e, i, t3=t3, mask=mask: e.tensor_tensor(t3, s3, bc(mask[:, :], 1, 4), ALU.add),
                           m, freed)
                    tiles.append([a, tile, t3, mt])
                ring_s.give(n, mt)
                t4 = tiles[0][1].rearrange("p (r c) -> p r c", c=G0)
                tiles[0][3] = G(lambda e, i: e.tensor_tensor(
                    t4, t4, bc(sel[:, ds(bat[u](i) * H + 4 * g, 4), :].rearrange("p h n -> p (h n)"), 2, G0),
                    ALU.add), tiles[0][3])
                tiles[1][3] = softmax_biased(tiles[1][2], 4, scale, mxs[k % 8], tiles[1][3])
                return tiles

            def select_softmax(k, tiles):
                tiles[0][3] = softmax_biased(tiles[0][2], 4, scale, mxs[8 + k % 8], tiles[0][3])
                return tiles

            def turn(k, tiles):
                got = []
                for a, tile, _, m in (tiles[1], tiles[0]):
                    q, pT, mt, mcp = turned(ring_t, ring_p, tile, 0, m)
                    ring_a.give(a, mt)
                    got.append((q, pT, mcp))
                return got[::-1]

            def values(k, got):
                u, g = divmod(k, 4)
                marks = []
                for n, (q, pT, m) in enumerate(got):
                    m = head_values(banks[4 + n], g, pT, vp[u], m, staged[u][1], copied.get((u - 1, n)))
                    ring_p.give(q, m)
                    if g == 3:
                        m = A(lambda e, i, n=n: e.activation(res[n], banks[4 + n][:, :], ACT.Copy), m,
                              unpacked.get((u - 1, n)))
                        copied[u, n] = m
                    marks.append(m)
                return marks if g == 3 else None

            def unpack(n, k, marks):
                u, w = k // 4, k // 4 % 2
                o3, m = heads_back(banks[6], res[n], marks[n], unpacked.get((u - 1 + n, 1 - n)))
                unpacked[u, n] = m
                r, dst = ((rs, o), (rl, o2))[n]
                m = V(lambda e, i: e.reciprocal(r[w].unsqueeze(2), o3[:, :, HD:HD + 1]), m)
                m = V(lambda e, i: e.tensor_tensor(
                    r[w], r[w], gl[:, ds(bat[u](i), 1), n + 1:n + 2].rearrange("p a c -> p (a c)").broadcast_to([P, H]),
                    ALU.mult), m)
                m = V(lambda e, i: e.tensor_tensor(dst[w].rearrange("p (h c) -> p h c", c=HD), o3[:, :, 0:HD],
                                                   bc(r[w], 2, HD), ALU.mult), m, done.get(u - 2))
                unpacked[u, n] = m
                return m

            def selected(k, marks):
                return marks and [unpack(0, k, marks)] + marks

            def local(k, marks):
                if marks is None:
                    return None
                u, w = k // 4, k // 4 % 2
                m = unpack(1, k, marks[1:])
                m = V(lambda e, i: e.tensor_tensor(o[w], o[w], o2[w], ALU.add), m, marks[0])
                return V(lambda e, i: e.tensor_tensor(
                    o[w], o[w], oc[:, ds(bat[u](i), 1), :].rearrange("p a c -> p (a c)"), ALU.add), m)

            def back(k, m):
                return m and turn_back(o[k // 4 % 2], banks[7][:, 0:P], oT[k // 4 % 2], m)

            def add(k, m):
                if m:
                    done[k // 4] = add_projected(bat[k // 4], banks[7][:, P:2 * P], oT[k // 4 % 2], w["Wo"][:, :], m)

            staircase(4 * per, (0, score), (1, select_softmax), (3, turn), (5, values), (6, selected), (7, local),
                      (8, back), (9, add))

        def layer0_cross():
            normalise("L0_xattn")
            ring = Ring(banks)
            lw = [ready["L0_xattn"], m_ctx]
            qT, kT = carve(T), carve(T)
            project(qT, W["L0_xattn_WqT"][:, :], xnT, ring, None, lw)
            project(kT, W["L0_xattn_WkT"][:, :], ctxT, ring, None, lw)
            v = carve(T)
            project_tokens(tokens(v), W["L0_xattn_WvT"][:, :], ctxT, ring, None, lw)
            attention("L0_xattn: batch", qT, kT, v, padded_values(4), causal[:, :], W["L0_xattn_WoT"][:, :])

        def mixture(name, gw, gb, top, w1, w2, b1, b2, buf_ready):
            normalise(name)
            lw = ready[name]
            lg, m = token_logits(gw[:, :], NE, None, lw)
            m = V(lambda e, i: e.tensor_tensor(gv, lg, gb, ALU.add), m)
            if top == "logits":
                mk = ranked(gv, gk, 2, gt, gr1, gr2, m)
                m = soft8(gv, gc, gmx, gsm, mk, keep=gk)
            else:
                m = soft8(gv, gc, gmx, gsm, m)
                m = ranked(gc, gk, 2, gt, gr1, gr2, m)
                m = V(lambda e, i: e.tensor_tensor(gc, gc, gk, ALU.mult), m)
                m = V(lambda e, i: e.tensor_reduce(gsm, gc, AX.X, ALU.add), m)
                m = V(lambda e, i: e.reciprocal(gsm, gsm), m)
                m = V(lambda e, i: e.tensor_tensor(gc, gc, bc(gsm, 2, NE), ALU.mult), m)
            split_tokens()
            add_expert_bias(gc, b2[:, :], m)
            if name == "L1_ffn":
                linear_biases()
            experts(name + ": experts", gc, w1, w2, b1[:, :], buf_ready)

        def layer1_recurrence():
            normalise("L1_attn")
            lw = ready["L1_attn"]
            wi, cw, cb, wg, bg, fb, wo = (W[f"L1_attn_{n}"] for n in (
                "WiT", "conv_w", "conv_b", "WgT", "bg", "forget_base", "WoT"))
            two = range(2)
            C = HC
            gate_, u2, al, be = (carve(2, T, parts=C) for _ in range(4))
            up = carve(2 * NB, P + KC - 1, parts=C)
            sp = [carve(2, parts=C) for _ in range(5)]
            ring = Ring(banks)
            fbv = fb[:, :]
            z, s, s2, acc, num = sp
            m = V(lambda e, i: e.tensor_scalar(z, fbv, -1.0, None, ALU.mult), lw)
            m = V(lambda e, i: e.tensor_tensor(z, z, fbv, ALU.min), m)
            m = A(lambda e, i: e.activation(z, z, ACT.Exp), m)
            m = V(lambda e, i: e.tensor_scalar(s, z, 2.0, None, ALU.add), m)
            m = V(lambda e, i: e.reciprocal(s, s), m)
            m = V(lambda e, i: e.tensor_tensor(s, s, z, ALU.mult), m)
            m = V(lambda e, i: e.tensor_tensor(s2, s, s, ALU.mult), m)
            m = V(lambda e, i: e.tensor_scalar(acc, s2, 1.0 / 17, 1.0 / 15, ALU.mult, ALU.add), m)
            for k in (13, 11, 9, 7, 5, 3, 1):
                m = V(lambda e, i: e.tensor_tensor(acc, acc, s2, ALU.mult), m)
                m = V(lambda e, i, k=k: e.tensor_scalar(acc, acc, 1.0 / k, None, ALU.add), m)
            m = V(lambda e, i: e.tensor_tensor(acc, acc, s, ALU.mult), m)
            m = V(lambda e, i: e.tensor_scalar(num, fbv, 0.0, None, ALU.max), m)
            m = V(lambda e, i: e.scalar_tensor_tensor(acc, acc, 2.0, num, ALU.mult, ALU.add), m)
            m_sp = V(lambda e, i: e.tensor_scalar(acc, acc, -8.0, None, ALU.mult), m)
            m0 = G(lambda e, i: e.memset(up[:, :, 0:KC - 1], 0.0))
            conv = []
            for c in two:
                mu = []
                for k in two:
                    n, bank, freed = ring.take()
                    m = M(lambda e, i, bank=bank, c=c, k=k: e.matmul(
                        bank[0:C, :], wi[:, HID + c * C:HID + (c + 1) * C], xnT[:, k * BANK:(k + 1) * BANK],
                        start=True, stop=True), freed, lw)
                    m = A(lambda e, i, bank=bank, c=c, k=k: e.activation(
                        up[:, c * NB + 4 * k:c * NB + 4 * k + 4, KC - 1:KC - 1 + P],
                        bank[0:C, :].rearrange("p (b t) -> p b t", t=P), ACT.Copy), m)
                    ring.give(n, m)
                    mu.append(m)
                u3 = u2[:, c, :].rearrange("p (b t) -> p b t", t=P)
                uc = up[:, c * NB:(c + 1) * NB, :]
                m = V(lambda e, i, c=c, u3=u3, uc=uc: e.tensor_scalar(
                    u3, uc[:, :, 0:P], cw[:, c * KC:c * KC + 1], cb[:, c:c + 1], ALU.mult, ALU.add), mu, m0)
                for k in range(1, KC):
                    m = V(lambda e, i, c=c, k=k, u3=u3, uc=uc: e.scalar_tensor_tensor(
                        u3, uc[:, :, k:k + P], cw[:, c * KC + k:c * KC + k + 1], u3, ALU.mult, ALU.add), m)
                conv.append(m)
            for c in two:
                for k in two:
                    n, bank, freed = ring.take()
                    m = M(lambda e, i, bank=bank, c=c, k=k: e.matmul(
                        bank[0:C, :], wi[:, c * C:(c + 1) * C], xnT[:, k * BANK:(k + 1) * BANK],
                        start=True, stop=True), freed)
                    m = A(lambda e, i, bank=bank, c=c, k=k: e.activation(
                        gate_[:, c, k * BANK:(k + 1) * BANK], bank[0:C, :], ACT.Gelu), m)
                    ring.give(n, m)
            sig = []
            for g in range(4):
                dst = (al, be)[g // 2][:, g % 2, :]
                for k in two:
                    n, bank, freed = ring.take()
                    for c in two:
                        m = M(lambda e, i, bank=bank, c=c, k=k, g=g: e.matmul(
                            bank[0:C, :], wg[:, c * 2 * HID + g * C:c * 2 * HID + (g + 1) * C],
                            u2[:, c, k * BANK:(k + 1) * BANK], start=c == 0, stop=c == 1), freed, conv)
                    m = A(lambda e, i, bank=bank, k=k, g=g, dst=dst: e.activation(
                        dst[:, k * BANK:(k + 1) * BANK], bank[0:C, :], ACT.Sigmoid, bias=bg[:, g:g + 1]), m)
                    ring.give(n, m)
                    sig.append(m)
            m_in = V(lambda e, i: e.tensor_tensor(be, be, u2, ALU.mult), sig)
            ma = [A(lambda e, i, c=c: e.activation(al[:, c, :], al[:, c, :], ACT.Exp, scale=acc[:, c:c + 1]),
                    sig, m_sp) for c in two]
            beta = carve(2, T, parts=C)
            m = V(lambda e, i: e.tensor_tensor(beta, al, al, ALU.mult), ma)
            m = V(lambda e, i: e.tensor_scalar(beta, beta, -1.0, 1.0, ALU.mult, ALU.add), m)
            m = V(lambda e, i: e.tensor_scalar(beta, beta, 1.0e-6, None, ALU.add), m)
            m = A(lambda e, i: e.activation(beta, beta, ACT.Sqrt), m)
            m_xt = V(lambda e, i: e.tensor_tensor(be, be, beta, ALU.mult), m, m_in)
            m_z = V(lambda e, i: e.memset(al.rearrange("p c (b t) -> p (c b) t", t=P)[:, :, 0:1], 0.0), ma, m_xt)
            hs = u2
            for c in two:
                m = V(lambda e, i, c=c: e.tensor_tensor_scan(hs[:, c, :], al[:, c, :], be[:, c, :], 0.0, ALU.mult,
                                                             ALU.add), m_z, m_xt)
                m_y = V(lambda e, i, c=c: e.tensor_tensor(hs[:, c, :], hs[:, c, :], gate_[:, c, :], ALU.mult), m)
            for k in two:
                n, bank, freed = ring.take()
                for j in range(4):
                    for c in two:
                        t0 = (4 * k + j) * P
                        m = M(lambda e, i, bank=bank, c=c, j=j, t0=t0: e.matmul(
                            bank[:, j * P:(j + 1) * P], hs[:, c, t0:t0 + P], wo[:, c * P:(c + 1) * P],
                            start=c == 0, stop=c == 1), freed, m_y)
                xs = x[:, k * BANK:(k + 1) * BANK]
                V(lambda e, i, xs=xs, bank=bank: e.tensor_tensor(xs, xs, bank[:, :], ALU.add), m)

        def layer1_cross():
            normalise("L1_xattn")
            lw = [ready["L1_xattn"], m_ctx]
            pair_columns = 2 * H * P
            tiles = []
            ring = Ring(banks)
            for n, (wn, bn, src) in enumerate((("WqT", "bq8", xnT), ("WkT", "bk8", ctxT), ("WvT", "bv8", ctxT))):
                w, b8 = W[f"L1_xattn_{wn}"], W[f"L1_xattn_{bn}"]
                dst = carve(pair_columns)
                for f2 in range(H // 2):
                    k, bank, freed = ring.take()
                    for f in (2 * f2, 2 * f2 + 1):
                        for g in range(4):
                            m = M(lambda e, i, bank=bank, f=f, g=g, w=w, src=src: e.matmul(
                                bank[32 * g:32 * g + 32, (f % 2) * 256:(f % 2) * 256 + 256], w[:, 8 * f:8 * f + 32],
                                src[:, 256 * g:256 * g + 256], start=True, stop=True), freed, lw)
                    view = dst.rearrange("p (t f) -> p f t", f=H)[:, 2 * f2:2 * f2 + 2, :]
                    bias = bc(b8[:, 2 * f2:2 * f2 + 2], 2, 256)
                    m = V(lambda e, i, bank=bank, view=view, bias=bias: e.tensor_tensor(
                        view, bank[:, :].rearrange("p (f t) -> p f t", f=2), bias, ALU.add), m)
                    ring.give(k, m)
                tiles.append(dst)
            vh = carve(4 * H, 32)
            m = G(lambda e, i: e.memset(vh[:, :, HD:32], 0.0))
            G(lambda e, i: e.memset(vh[:, :, HD:HD + 1], 1.0), m)
            fl.segment("L1_xattn: batch", 2)
            S2 = H * P
            scale = float(np.sqrt(HD))
            four = range(4)
            vs, qs, ks, halves = bufA[:, 6144:6144 + S2], bufA[:, 4096:4096 + S2], carve(S2), {}
            o8 = vs
            for dst, n in ((vs, 2), (qs, 0), (ks, 1)):
                for half, copy in enumerate((lambda o, s: V(lambda e, i: e.tensor_copy(o, s(i))),
                                             lambda o, s: A(lambda e, i: e.activation(o, s(i), ACT.Copy)))):
                    c = half * S2 // 2
                    halves[n, half] = copy(dst[:, c:c + S2 // 2], lambda i, n=n, c=c: tiles[n][:, ds(i * S2 + c, S2 // 2)])
            ring_s, ring_t, ring_o = Ring(banks[0:2]), Ring(banks[2:5]), Ring(banks[5:7])
            ring_a, ring_p = (Ring([bufA[:, n * BANK:(n + 1) * BANK] for n in ns]) for ns in (range(4), range(4, 7)))
            mask, tmp, rs = carve(4, P), carve(4, H, HD), carve(H, 4)
            mxs = [carve(4) for _ in range(8)]
            pad = pad_u8[:, :].rearrange("p (g b t) -> p g b t", g=4, b=2)
            m_mask = V(lambda e, i: e.scalar_tensor_tensor(
                mask.unsqueeze(2), pad[:, :, ds(i, 1), :], -BIG, bc(causal[:, :], 1, 4).unsqueeze(2), ALU.mult,
                ALU.add), m_pad)
            mv = []
            for hg in four:
                n, bank, freed = ring_t.take()
                for j in four:
                    m = M(lambda e, i, h=4 * hg + j, j=j, bank=bank: e.transpose(
                        bank[:, j * P:(j + 1) * P], vs[:, h * P:(h + 1) * P], ident[:, :]), freed,
                          halves[2, hg // 2])
                m = V(lambda e, i, hg=hg, bank=bank: e.tensor_copy(
                    vh[:, 16 * hg:16 * hg + 16, 0:HD], bank[:, :].rearrange("p (a c) -> p a c", c=32)[:, :, 0:HD]), m)
                ring_t.give(n, m)
                mv.append(m)

            def score(k, _):
                hg, g = divmod(k, 4)
                n, bank, freed = ring_s.take()
                r = slice(32 * g, 32 * g + HD)
                for j in four:
                    c = (4 * hg + j) * P
                    m = M(lambda e, i, j=j, c=c: e.matmul(bank[:, j * P:(j + 1) * P], qs[r, c:c + P],
                                                          ks[r, c:c + P], start=True, stop=True),
                          freed, halves[0, hg // 2], halves[1, hg // 2])
                a, tile, freed = ring_a.take()
                t3 = tile.rearrange("p (j t) -> p j t", t=P)
                s3 = bank[:, :].rearrange("p (j t) -> p j t", t=P)
                m = V(lambda e, i: e.tensor_tensor(t3, s3, bc(mask[:, g, :], 1, 4), ALU.add), m, freed, m_mask)
                ring_s.give(n, m)
                return a, tile, softmax_ready(t3, 4, scale, mxs[k % 8], m)

            def turn(k, s):
                a, tile, m = s
                q, pT, mt, mc = turned(ring_t, ring_p, tile, 0, m)
                ring_a.give(a, mt)
                return q, pT, mc

            def values(k, s):
                hg, g = divmod(k, 4)
                q, pT, m = s
                if g == 0:
                    o_bank[:] = ring_o.take()
                n, bank, freed = o_bank
                for j in four:
                    h = 4 * hg + j
                    m = M(lambda e, i, j=j, h=h: e.matmul(
                        bank[32 * g:32 * g + 32, j * P:(j + 1) * P], vh[:, 4 * h + g, :],
                        pT[:, j * P:(j + 1) * P], start=True, stop=True), m, freed, mv[hg])
                ring_p.give(q, m)
                if g == 3:
                    m = A(lambda e, i: e.activation(o8[:, hg * BANK:(hg + 1) * BANK], bank[:, :], ACT.Copy), m, mv)
                    ring_o.give(n, m)
                    results.append(m)

            o_bank, results = [], []
            staircase(16, (0, score), (3, turn), (5, values))
            src = o8.rearrange("p (t f) -> p f t", f=H)
            for fg in four:
                n, bank, freed = ring_t.take()
                for j in four:
                    m = M(lambda e, i, f=4 * fg + j, j=j, bank=bank: e.transpose(
                        bank[:, j * P:(j + 1) * P], src[:, f, :], ident[:, :]), freed, results)
                o4 = bank[:, :].rearrange("p (f g c) -> p f g c", f=4, g=4)
                fs = slice(4 * fg, 4 * fg + 4)
                m = V(lambda e, i, o4=o4, fs=fs: e.reciprocal(rs[:, fs, :].unsqueeze(3), o4[:, :, :, HD:HD + 1]), m)
                m = V(lambda e, i, o4=o4, fs=fs: e.tensor_tensor(
                    tmp[:, :, fs, :].rearrange("p g f c -> p f g c"), o4[:, :, :, 0:HD], bc(rs[:, fs, :], 3, HD),
                    ALU.mult), m)
                ring_t.give(n, m)
            x4 = lambda i: x[:, :].rearrange("p (g b f) -> p g b f", g=4, b=2)[:, :, ds(i, 1), :]
            V(lambda e, i: e.tensor_tensor(x4(i), x4(i), tmp.rearrange("p g f c -> p g (f c)").unsqueeze(2), ALU.add),
              m)

        bias = bufA[:, 4096:8192].rearrange("p (h t) -> p h t", t=P)

        def linear_biases():
            rel = carve(P)
            m = G(lambda e, i: e.iota(rel, pattern=[[1, P]], base=0, channel_multiplier=-1,
                                      allow_small_or_imprecise_dtypes=True))
            m = G(lambda e, i: e.tensor_tensor(rel, rel, causal[:, :], ALU.add), m)
            G(lambda e, i: e.tensor_tensor(bias, bc(rel, 1, QH), bc(W["slopes"][:, :], 2, P), ALU.mult), m,
              ready["L2_attn"])

        def layer2_attention():
            gu, dn = (NE + 1) * 2 * FI, (NE + 1) * 3 * FI
            wo = arena[:, ARENA - 2048:ARENA]
            marks = normalise("L2_attn", loads=[
                ("in_A", bufA[:, 0:4096], "L2_attn_Wqkv"), ("in_A", wo, "L2_attn_Wout"),
                ("in_B", bufB[:, 0:gu], "L2_ffn_Wgu"), ("in_B", bufB[:, gu:dn], "L2_ffn_Wd")])
            m_late["L2_ffn"] = marks[3]
            lw = [ready["L2_attn"], marks[1]]
            wq, wk, wv = bufA[:, 0:2048], bufA[:, 2048:3072], bufA[:, 3072:4096]
            PER = 4
            QG, KG = 4, 2
            GROUPS, GU = NPAIR // KG, 2 * PER
            kT, qT, vs = [carve(KG, BANK) for _ in range(2)], [carve(QG, BANK) for _ in range(2)], []
            for _ in range(2):
                vs.append(carve(PER * 4, DH + 1))
                G(lambda e, i, v=vs[-1]: e.memset(v[:, :, DH:DH + 1], 1.0))
            fl.segment("L2_attn: batch", NB // PER)
            xb = carve(BANK)
            ring_s, ring_t = Ring(banks[0:2]), Ring(banks[2:4])
            proj, ring_o, backs, sums = Ring(banks[4:5]), Ring(banks[5:6]), Ring(banks[6:7]), banks[7]
            ring_a, ring_p = Ring([carve(BANK) for _ in range(4)]), Ring([carve(BANK) for _ in range(3)])
            oo, oT = [carve(2 * P) for _ in range(2)], [carve(2 * P) for _ in range(2)]
            rs, mxs = [carve(4) for _ in range(2)], [carve(4) for _ in range(8)]
            m_xb = A(lambda e, i: e.activation(xb, xnT[:, ds(i * BANK, BANK)], ACT.Copy))
            projected, last_score, last_values = {}, {}, {}

            def project_part(gg, part, ring):
                n, bank, freed = ring.take()
                if part < KG + QG:
                    w, tile, out_ = (wk, part, kT) if part < KG else (wq, part - KG, qT)
                    c = ((KG if part < KG else QG) * gg + tile) * P
                    m = M(lambda e, i: e.matmul(bank[:, :], w[:, c:c + P], xb, start=True, stop=True), m_xb, lw, freed)
                    m = evacuate(out_[gg % 2][:, tile, :], bank[:, :], part, m, last_score.get(gg - 2))
                else:
                    u0 = 2 * (part - KG - QG)
                    for u in range(2):
                        m = M(lambda e, i, u=u: e.matmul(bank[:, u * 256:(u + 1) * 256],
                                                         xb[:, (u0 + u) * P:(u0 + u + 1) * P],
                                                         wv[:, gg * 256:(gg + 1) * 256], start=True, stop=True),
                              m_xb, lw, freed)
                    m = evacuate(vs[gg % 2][:, 4 * u0:4 * u0 + 8, 0:DH],
                                 bank[:, :].rearrange("p (a c) -> p a c", c=DH), part, m, last_values.get(gg - 2))
                ring.give(n, m)
                projected[gg, part] = m

            M(lambda e, i: e.matmul(sums[:, :], ident[:, :], x[:, ds(i * BANK, BANK)], start=True, stop=False))
            for part, ring in enumerate((proj, backs, ring_o, ring_t, ring_t, proj, backs, ring_o)):
                project_part(0, part, ring)

            def unit(k):
                return k // GU, k // 2 % PER, k % 2

            products = {}

            def score(k, _):
                gg, u, r = unit(k)
                if r == 0:
                    slots = [ring_s.take() for _ in range(2)]
                    for jj in range(2):
                        for s in range(2):
                            for rr in range(2):
                                p, c = slice(64 * rr, 64 * rr + 64), slice(u * P, (u + 1) * P)
                                n, bank, freed = slots[rr]
                                at = (2 * jj + s) * P
                                products[k + rr] = M(lambda e, i, p=p, c=c, jj=jj, s=s, at=at, bank=bank: e.matmul(
                                    bank[:, at:at + P], qT[gg % 2][p, 2 * jj + s, c], kT[gg % 2][p, jj, c], start=True,
                                    stop=True), freed, [projected[gg, n] for n in range(KG + QG)])
                    last_score[gg] = products[k + 1]
                    products["slots"] = slots
                n, bank, _ = products["slots"][r]
                m = products[k]
                a, tile, freed = ring_a.take()
                h0 = 4 * (2 * gg + r)
                bb = bias[:, h0:h0 + 4, :].rearrange("p h t -> p (h t)")
                m = V(lambda e, i: e.scalar_tensor_tensor(tile, bank[:, :], 1.0 / np.sqrt(DH).item(), bb, ALU.mult,
                                                          ALU.add), m, freed)
                ring_s.give(n, m)
                m = softmax_ready(tile.rearrange("p (j t) -> p j t", t=P), 4, 1.0, mxs[k % 8], m)
                if gg + 1 < GROUPS:
                    project_part(gg + 1, k % GU, proj)
                return a, tile, m

            def turn(k, s):
                a, tile, m = s
                q, pT, mt, mc = turned(ring_t, ring_p, tile, 0, m)
                ring_a.give(a, mt)
                return q, pT, mc

            def values(k, s):
                gg, u, r = unit(k)
                q, pT, m = s
                n, bank, freed = ring_o.take()
                for hh in range(4):
                    h = 4 * u + 2 * (hh // 2) + r
                    m = M(lambda e, i, hh=hh, h=h: e.matmul(bank[:, hh * 65:hh * 65 + 65], pT[:, hh * P:(hh + 1) * P],
                                                            vs[gg % 2][:, h, :], start=True, stop=True),
                          m, freed, projected[gg, KG + QG], projected[gg, KG + QG + 1])
                last_values[gg] = m
                ring_p.give(q, m)
                o3 = bank[:, 0:260].rearrange("p (h c) -> p h c", c=65)
                w = k % 2
                m = V(lambda e, i: e.reciprocal(rs[w].unsqueeze(2), o3[:, :, DH:DH + 1]), m, rs_free[w])
                m = V(lambda e, i: e.tensor_tensor(oo[w].rearrange("p (h c) -> p h c", c=DH), o3[:, :, 0:DH],
                                                   bc(rs[w], 2, DH), ALU.mult), m, oo_free[w])
                rs_free[w] = m
                ring_o.give(n, m)
                return m

            def back(k, m):
                w = k % 2
                n, bank, freed = backs.take()
                for j in range(2):
                    m = M(lambda e, i, j=j: e.transpose(bank[:, j * P:(j + 1) * P], oo[w][:, j * P:(j + 1) * P],
                                                        ident[:, :]), m, freed)
                oo_free[w] = m
                m = A(lambda e, i: e.activation(oT[w], bank[:, 0:2 * P], ACT.Copy), m, oT_free[w])
                backs.give(n, m)
                return m

            def outputs(k, m):
                gg, u, r = unit(k)
                w = k % 2
                at = slice(u * P, (u + 1) * P)
                for j in range(2):
                    c = (2 * (2 * gg + j) + r) * P
                    m = M(lambda e, i, j=j, c=c: e.matmul(sums[:, at], oT[w][:, j * P:(j + 1) * P], wo[:, c:c + P],
                                                          start=False, stop=k == GU * GROUPS - 1 and j == 1), m)
                oT_free[w] = m
                if k == GU * GROUPS - 1:
                    V(lambda e, i: e.tensor_copy(x[:, ds(i * BANK, BANK)], sums[:, :]), m)

            rs_free, oo_free, oT_free = ([None, None] for _ in range(3))
            staircase(GU * GROUPS, (0, score), (2, turn), (3, values), (4, back), (5, outputs))

        def layer2_cross():
            half = NE * FF
            marks = normalise("L2_xattn", loads=[("in_A", bufA[:, 0:half], "L3_ffn_w1"),
                                                 ("in_A", bufA[:, half:2 * half], "L3_ffn_w2")])
            m_late["L3_ffn"] = marks[1]
            w = {n: W[f"L2_xattn_{n}"] for n in ("Wq", "bq", "Wk", "bk", "Wv", "bv", "Wo", "bo")}
            lw = [ready["L2_xattn"], m_ctx]
            ring = Ring(banks)
            qT, kT, low = carve(T), carve(T), carve(T)
            v = carve(T)
            mv = project_tokens(tokens(v), w["Wv"][:, :], ctxT, ring, w["bv"][:, :], lw)
            m_low = None
            for dst, wn, bn, src in ((qT, "Wq", "bq", xnT), (kT, "Wk", "bk", ctxT)):
                m = project(dst, w[wn][:, :], src, ring, w[bn][:, 0:1], lw)
                m = V(lambda e, i, dst=dst: e.tensor_scalar(low, dst, 0.0, None, ALU.min), m, m_low)
                me = A(lambda e, i: e.activation(low, low, ACT.Exp), m)
                m_low = V(lambda e, i, dst=dst: e.scalar_tensor_tensor(dst, dst, 0.0, low, ALU.max, ALU.add), me)
            per = 4
            vp = [carve(H, 32) for _ in range(per)]
            for t in vp:
                G(lambda e, i, t=t: e.memset(t, 0.0))
            fl.segment("L2_xattn: batch", NB // per)
            kb, qb, qtok, oT, zr = ([carve(P) for _ in range(per)] for _ in range(5))
            qM = [carve(4, P) for _ in range(per)]
            ring_s, ring_a = Ring(banks[0:4]), Ring([carve(BANK) for _ in range(4)])
            bat = [lambda i, u=u: i * per + u for u in range(per)]
            staged = []
            for u in range(per):
                m1 = (G(lambda e, i, u=u: e.tensor_copy(kb[u], b_(kT)(bat[u](i)))) if u else
                      A(lambda e, i, u=u: e.activation(kb[u], b_(kT)(bat[u](i)), ACT.Copy)))
                m2 = V(lambda e, i, u=u: e.tensor_tensor(qM[u], b_(qT)(bat[u](i)).unsqueeze(1).broadcast_to([P, 4, P]),
                                                         bc(mask4[:, :], 2, P), ALU.mult))
                for j in range(4):
                    m3 = G(lambda e, i, u=u, j=j: e.tensor_copy(
                        vp[u].rearrange("p (g j) c -> p g j c", j=4)[:, :, j, 8 * j:8 * j + 8],
                        b_(v)(bat[u](i)).rearrange("p (g j c) -> p g j c", j=4, c=HD)[:, :, j, :]))
                m4 = G(lambda e, i, u=u: e.tensor_copy(qb[u], b_(qT)(bat[u](i))))
                staged.append([[m1, m2], m3, m4])

            def score(k, _):
                u, g = divmod(k, 4)
                q = slice(32 * g, 32 * g + 32)
                n, bank, freed = ring_s.take()
                m = M(lambda e, i: e.matmul(bank[:, :], kb[u][q, :], qM[u][q, :, :].rearrange("p j t -> p (j t)"),
                                            start=True, stop=True), freed, staged[u][0])
                a, tile, freed = ring_a.take()
                m = V(lambda e, i: e.tensor_tensor(tile.rearrange("p (j t) -> p j t", t=P),
                                                   bank[:, :].rearrange("p (j t) -> p j t", t=P),
                                                   bc(tri[:, :], 1, 4), ALU.mult), m, freed)
                ring_s.give(n, m)
                return a, tile, m

            def values(k, s):
                u, g = divmod(k, 4)
                a, tile, m = s
                bank = banks[4 + u % 2]
                for j in range(4):
                    m = M(lambda e, i, j=j: e.matmul(bank[32 * g:32 * g + 32, 0:P], vp[u][:, 4 * g + j, :],
                                                     tile[:, j * P:(j + 1) * P], start=j == 0, stop=j == 3),
                          m, staged[u][1], scaled.get(u - 2))
                ring_a.give(a, m)
                return m

            def sums_1(k, m):
                u, g = divmod(k, 4)
                if g == 0:
                    z = banks[6 + u % 2]
                    n = M(lambda e, i: e.transpose(z[:, 0:P], qb[u], ident[:, :]), staged[u][2], added.get(u - 2))
                    turned_q[u] = A(lambda e, i: e.activation(qtok[u], z[:, 0:P], ACT.Copy), n)
                return m

            def sums_2(k, m):
                u, g = divmod(k, 4)
                if g == 0:
                    z = banks[6 + u % 2]
                    n = M(lambda e, i: e.matmul(z[:, P:2 * P], qtok[u], tri[:, :], start=True, stop=True), turned_q[u])
                    norms[u] = V(lambda e, i: e.reciprocal(zr[u], z[:, P:2 * P]), n)
                return m

            def scale_results(k, m):
                u, g = divmod(k, 4)
                if g == 3:
                    scaled[u] = V(lambda e, i: e.tensor_tensor(oT[u], banks[4 + u % 2][:, 0:P], zr[u], ALU.mult), m,
                                  norms[u])
                    return scaled[u]

            def add(k, m):
                if m:
                    u = k // 4
                    added[u] = add_projected(bat[u], banks[6 + u % 2][:, 2 * P:3 * P], oT[u], w["Wo"][:, :], m,
                                             w["bo"][:, :])

            scaled, turned_q, norms, added = {}, {}, {}, {}
            staircase(4 * per, (0, score), (1, sums_1), (2, values), (2, sums_2), (3, scale_results), (4, add))

        def layer2_experts():
            normalise("L2_ffn")
            lg, m = token_logits(W["L2_ffn_WrT"][:, :], NE, None, ready["L2_ffn"])
            m = V(lambda e, i: e.tensor_tensor(gv, lg, bc(W["L2_ffn_rb"][:, :], 1, NB), ALU.add), m)
            m = A(lambda e, i: e.activation(gv, gv, ACT.Sigmoid), m)
            m = ranked(gv, gk, 2, gt, gr1, gr2, m)
            comb = carve(NE + 1, NB)
            V(lambda e, i: e.tensor_tensor(comb[:, 0:NE, :].rearrange("p e b -> p b e"), gv, gk, ALU.mult), m)
            G(lambda e, i: e.memset(comb[:, NE, :], 1.0))
            split_tokens()
            U = 3
            fl.segment("L2_ffn: experts", (NE + 1) // U)
            WU = 2 * FI
            wu, wd = bufB[:, 0:(NE + 1) * WU], bufB[:, (NE + 1) * WU:(NE + 1) * (WU + FI)]
            wds, cs = [carve(FI) for _ in range(2)], [carve(NB) for _ in range(U)]
            ring_h, ring_y = Ring(banks[0:6]), Ring(banks[6:8])
            ring_a = Ring([carve(2, BANK) for _ in range(2)])
            ring_g = Ring([carve(BANK) for _ in range(2)])
            staged = [G(lambda e, i, u=u: e.tensor_copy(cs[u], comb[:, ds(i * U + u, 1), :].rearrange(
                "p a b -> p (a b)"))) for u in range(U)]
            placed, last_x, w1_used, w2_used = {}, {}, {}, {}

            def weights(k, _):
                u, t = divmod(k, 2)
                if t == 0:
                    p = u % 2
                    m1 = split(w_high[p][:, :], w_low[p][:, :], lambda i: wu[:, ds((i * U + u) * WU, WU)],
                               m_late["L2_ffn"], w1_used.get(u - 2))
                    m2 = V(lambda e, i: e.tensor_copy(wds[p], wd[:, ds((i * U + u) * FI, FI)]), w2_used.get(u - 2))
                    placed[u] = m1, m2

            def up(k, _):
                u, t = divmod(k, 2)
                a, h, freed_h = ring_a.take()
                for f in range(2):
                    n1, bg_, freed1 = ring_h.take()
                    n2, bu_, freed2 = ring_h.take()
                    ms = []
                    for bank, chunk, fr in ((bg_, f, freed1), (bu_, FI // P + f, freed2)):
                        ms.append(up_product(bank, u % 2, t, chunk, fr, placed[u][0]))
                    g, sg, freed = ring_g.take()
                    m = A(lambda e, i, sg=sg, bg_=bg_: e.activation(sg, bg_[:, :], ACT.Silu), ms[0], freed)
                    ring_h.give(n1, m)
                    m = V(lambda e, i, sg=sg, bu_=bu_, f=f: e.tensor_tensor(h[:, f, :], sg, bu_[:, :], ALU.mult),
                          m, ms[1], freed_h)
                    ring_h.give(n2, m)
                    ring_g.give(g, m)
                w1_used[u] = ms[1]
                return a, h, m

            def down(k, s):
                u, t = divmod(k, 2)
                a, h, m = s
                n, bank, freed = ring_y.take()
                for j in range(4):
                    for f in range(2):
                        my = M(lambda e, i, j=j, f=f: e.matmul(bank[:, j * P:(j + 1) * P], h[:, f, j * P:(j + 1) * P],
                                                               wds[u % 2][:, f * P:(f + 1) * P], start=f == 0,
                                                               stop=f == 1),
                               freed, m, placed[u][1], signal=f == 1)
                w2_used[u] = my
                for j in range(4):
                    xs = x[:, (4 * t + j) * P:(4 * t + j + 1) * P]
                    c = cs[u][:, 4 * t + j:4 * t + j + 1]
                    last_x[(t, j)] = mv = V(lambda e, i, j=j, xs=xs, c=c: e.scalar_tensor_tensor(
                        xs, bank[:, j * P:(j + 1) * P], c, xs, ALU.mult, ALU.add), my, staged[u],
                        last_x.get((t, j)))
                ring_a.give(a, my)
                ring_y.give(n, mv)

            staircase(2 * U, (0, weights), (1, up), (2, down), newest=True)

        def layer3_attention():
            normalise("L3_attn")
            w = {n: W[f"L3_attn_{n}"] for n in ("wqT", "bq", "bqrow", "wkT", "bk", "wvT", "bv", "woT", "bo")}
            lw = ready["L3_attn"]
            ring = Ring(banks[0:7])
            qT, kT = carve(T), carve(T)
            project(qT, w["wqT"][:, :], xnT, ring, w["bq"][:, 0:1], lw)
            project(kT, w["wkT"][:, :], xnT, ring, w["bk"][:, 0:1], lw)
            v = carve(T)
            project_tokens(tokens(v), w["wvT"][:, :], xnT, ring, w["bv"][:, :], lw)
            vp = padded_values(4)
            BH = NB * H
            keepT = carve(BH)
            free = used[0]
            q, t1, t2, t3 = (carve(BH, HD) for _ in range(4))
            l2, mx, sm, en, mean, var = (carve(BH) for _ in range(6))

            def q4(k, bank):
                return q[:, 4 * H * k:4 * H * (k + 1), :], bank[:, :].rearrange("p (a c) -> p a c", c=HD)
            mq = project_tokens(q4, w["wqT"][:, :], xnT, ring, w["bqrow"][:, :].rearrange("p (a c) -> p a c", c=HD), lw)
            m = V(lambda e, i: e.tensor_tensor(t1, q, q, ALU.mult), mq)
            m = V(lambda e, i: e.tensor_reduce(l2, t1, AX.X, ALU.add), m)
            ml = A(lambda e, i: e.activation(l2, l2, ACT.Sqrt), m)
            m = V(lambda e, i: e.tensor_reduce(mean, q, AX.X, ALU.add), mq)
            m = V(lambda e, i: e.tensor_scalar(mean, mean, 1.0 / HD, None, ALU.mult), m)
            mt3 = G(lambda e, i: e.tensor_tensor(t3, q, bc(mean, 2, HD), ALU.subtract), m)
            mt4 = G(lambda e, i: e.tensor_tensor(t3, t3, t3, ALU.mult), mt3)
            m = V(lambda e, i: e.tensor_reduce(mx, q, AX.X, ALU.max), mq)
            mq2 = V(lambda e, i: e.tensor_tensor(q, q, bc(mx, 2, HD), ALU.subtract), m, mt3)
            m = A(lambda e, i: e.activation(t2, q, ACT.Exp), mq2)
            m = V(lambda e, i: e.tensor_reduce(sm, t2, AX.X, ALU.add), m)
            mln = A(lambda e, i: e.activation(sm, sm, ACT.Ln), m)
            m = V(lambda e, i: e.tensor_reduce(var, t3, AX.X, ALU.add), mt4)
            mvar = V(lambda e, i: e.tensor_scalar(var, var, 1.0 / (HD - 1), 0.2, ALU.mult, ALU.mult), m)
            m = V(lambda e, i: e.tensor_tensor(q, q, bc(sm, 2, HD), ALU.subtract), mln)
            me = A(lambda e, i: e.activation(t2, q, ACT.Exp), m)
            m = V(lambda e, i: e.tensor_scalar(t1, t2, 1.0e-9, None, ALU.add), me, mvar)
            m = A(lambda e, i: e.activation(t1, t1, ACT.Ln), m)
            m = V(lambda e, i: e.tensor_tensor(t1, t1, t2, ALU.mult), m)
            m = V(lambda e, i: e.tensor_reduce(en, t1, AX.X, ALU.add), m)
            m = V(lambda e, i: e.scalar_tensor_tensor(var, en, -0.3, var, ALU.mult, ALU.add), m, mvar)
            m = V(lambda e, i: e.scalar_tensor_tensor(var, l2, 0.5, var, ALU.mult, ALU.add), m, ml)
            m = M(lambda e, i: e.transpose(banks[7][:, 0:P], var, ident[:, :]), m)
            sc, sc2, iota, kp = (carve(P) for _ in range(4))
            c1 = [carve(1) for _ in range(4)]
            top, idf = carve(16), carve(16)
            idx = sb("top_index", [P, 16], U32)
            ms = V(lambda e, i: e.tensor_copy(sc, banks[7][:, 0:P]), m)
            mu, sd, fac, tmp = c1
            m = V(lambda e, i: e.tensor_reduce(mu, sc, AX.X, ALU.add), ms)
            m = V(lambda e, i: e.tensor_scalar(mu, mu, 1.0 / P, None, ALU.mult), m)
            m = V(lambda e, i: e.tensor_scalar(sc2, sc, mu, None, ALU.subtract), m)
            m = V(lambda e, i: e.tensor_tensor(sc2, sc2, sc2, ALU.mult), m)
            m = V(lambda e, i: e.tensor_reduce(sd, sc2, AX.X, ALU.add), m)
            m = V(lambda e, i: e.tensor_scalar(sd, sd, 1.0 / (P - 1), None, ALU.mult), m)
            m = A(lambda e, i: e.activation(sd, sd, ACT.Sqrt), m)
            m = V(lambda e, i: e.tensor_scalar(tmp, mu, 1.0e-6, None, ALU.add), m)
            m = V(lambda e, i: e.reciprocal(tmp, tmp), m)
            m = V(lambda e, i: e.scalar_tensor_tensor(fac, sd, tmp, sd, ALU.mult, ALU.bypass), m)
            m = V(lambda e, i: e.tensor_scalar(fac, fac, float(MAX_F), None, ALU.mult), m)
            m = V(lambda e, i: e.tensor_scalar(fac, fac, -100.0, 100.0, ALU.max, ALU.min), m)
            m = V(lambda e, i: e.tensor_scalar(fac, fac, 12582912.0, None, ALU.add), m)
            m = V(lambda e, i: e.tensor_scalar(fac, fac, 12582912.0, None, ALU.subtract), m)
            m = V(lambda e, i: e.tensor_scalar(fac, fac, float(MIN_F), float(MAX_F), ALU.max, ALU.min), m)
            pick, blk = carve(P), carve(P)
            mp = G(lambda e, i: e.memset(pick, 1.0))
            p3 = pick.rearrange("p (b h) -> p b h", h=H)
            mp = select(p3, [[-H, NB], [0, H]], 0, 1, ALU.is_equal, 0.0, mp)
            m = M(lambda e, i: e.matmul(banks[7][:, P:P + 1], pick, fac, start=True, stop=True), m, mp)
            mcount = V(lambda e, i: e.tensor_copy(fac, banks[7][:, P:P + 1]), m)
            m = V(lambda e, i: e.max(top[:, 0:8], sc), ms)
            m1 = V(lambda e, i: e.max_index(idx[:, 0:8], top[:, 0:8], sc), m)
            m = V(lambda e, i: e.match_replace(sc2, top[:, 0:8], sc, -3.0e38), m, m1)
            m2 = V(lambda e, i: e.max(top[:, 8:16], sc2), m)
            m2 = V(lambda e, i: e.max_index(idx[:, 8:16], top[:, 8:16], sc2), m2)
            m = V(lambda e, i: e.tensor_copy(idf, idx[:, :]), m1, m2)
            mi = G(lambda e, i: e.iota(iota, pattern=[[1, P]], base=0, channel_multiplier=0,
                                       allow_small_or_imprecise_dtypes=True))
            act = carve(16)
            mf = V(lambda e, i: e.tensor_scalar(fac, fac, 0.5, None, ALU.subtract), mcount)
            m = V(lambda e, i: e.tensor_scalar(act[:, 0:MAX_F], iota[:, 0:MAX_F], fac, 1000.0, ALU.is_gt, ALU.mult),
                  m, mf, mi)
            m = V(lambda e, i: e.tensor_tensor(idf[:, 0:MAX_F], idf[:, 0:MAX_F], act[:, 0:MAX_F], ALU.add), m)
            m = V(lambda e, i: e.tensor_scalar(kp, iota, idf[:, 0:1], None, ALU.is_equal), m, mi)
            for j in range(1, MAX_F):
                m = V(lambda e, i, j=j: e.scalar_tensor_tensor(kp, iota, idf[:, j:j + 1], kp, ALU.is_equal, ALU.add), m)
            m = M(lambda e, i: e.transpose(banks[7][:, 2 * P:3 * P], kp, ident[:, :]), m)
            V(lambda e, i: e.tensor_copy(keepT, banks[7][:, 2 * P:3 * P]), m)
            used[0] = free
            attention("L3_attn: batch", qT, kT, v, vp, None, w["woT"][:, :], bias=w["bo"][:, :],
                      keep=lambda b: keepT[:, ds(b * H, H)])

        def layer3_cross():
            normalise("L3_xattn")
            lw = [ready["L3_xattn"], m_ctx]
            cs, cb = carve(NB), carve(NB, P)
            m = V(lambda e, i: e.tensor_reduce(cs, ctxT[:, :].rearrange("p (b t) -> p b t", t=P), AX.X, ALU.add), lw)
            m = V(lambda e, i: e.tensor_scalar(cs, cs, 1.0 / P, None, ALU.mult), m)
            mc = V(lambda e, i: e.tensor_copy(cb, bc(cs, 2, P)), m)
            for k in range(2):
                bank = banks[k]
                for j in range(4):
                    b = 4 * k + j
                    M(lambda e, i, b=b, j=j, bank=bank: e.matmul(bank[:, j * P:(j + 1) * P], xnT[:, b * P:(b + 1) * P],
                                                                 W["L3_xattn_W1T"][:, :], start=True, stop=False),
                      mc, lw, signal=False)
                    m = M(lambda e, i, b=b, j=j, bank=bank: e.matmul(bank[:, j * P:(j + 1) * P], cb[:, b, :],
                                                                     W["L3_xattn_W2T"][:, :], start=False, stop=True))
                xs = x[:, k * BANK:(k + 1) * BANK]
                m = V(lambda e, i, xs=xs, bank=bank: e.tensor_tensor(xs, xs, bank[:, :], ALU.add), m)
                V(lambda e, i, k=k: e.tensor_tensor(x3[:, 4 * k:4 * k + 4, :], x3[:, 4 * k:4 * k + 4, :],
                                                    bc(W["L3_xattn_b"][:, :], 1, 4), ALU.add), m)

        def layer3_experts():
            normalise("L3_ffn")
            lw = ready["L3_ffn"]
            GD = 16
            wg, wgT = W["L3_ffn_wg"], carve(NE, parts=GD)
            sq, nr = carve(GD, parts=NE), carve(1, parts=NE)
            m = V(lambda e, i: e.tensor_tensor(sq, wg[:, :], wg[:, :], ALU.mult), lw)
            m = V(lambda e, i: e.tensor_reduce(nr, sq, AX.X, ALU.add), m)
            m = A(lambda e, i: e.activation(nr, nr, ACT.Sqrt), m)
            m = V(lambda e, i: e.tensor_scalar(nr, nr, 1.0e-4, None, ALU.max), m)
            m = V(lambda e, i: e.reciprocal(nr, nr), m)
            m = V(lambda e, i: e.tensor_scalar(sq, wg[:, :], nr, None, ALU.mult), m)
            m = M(lambda e, i: e.transpose(banks[6][0:GD, 0:NE], sq, ident[0:NE, 0:NE]), m)
            mw = V(lambda e, i: e.tensor_copy(wgT, banks[6][0:GD, 0:NE]), m)
            xr = carve(T, parts=GD)
            mr = []
            for k in range(2):
                c = slice(k * BANK, (k + 1) * BANK)
                m = M(lambda e, i, k=k, c=c: e.matmul(banks[4 + k][0:GD, :], W["L3_ffn_wg_redT"][:, :], xnT[:, c],
                                                      start=True, stop=True), lw)
                mr.append(evacuate(xr[:, c], banks[4 + k][0:GD, :], k, m))
            lg, m = token_logits(wgT, NE, xr, mw, mr)
            m = V(lambda e, i: e.tensor_copy(gv, lg), m)
            m = soft8(gv, gc, gmx, gsm, m)
            m = ranked(gc, gk, 1, gt, gr1, gr2, m)
            m = V(lambda e, i: e.tensor_tensor(gc, gc, gk, ALU.mult), m)
            split_tokens()
            add_expert_bias(gc, W["L3_ffn_b2"][:, :], m)
            half = NE * FF
            experts("L3_ffn: experts", gc, bufA[:, 0:half], bufA[:, half:2 * half], W["L3_ffn_b1T"][:, :], m_late["L3_ffn"])

        half = NE * FF
        m_late = {}
        layer0_attention()
        layer0_cross()
        mixture("L0_ffn", W["L0_ffn_gate_w"], bc(W["L0_ffn_gate_b"][:, :], 1, NB), "logits", bufA[:, 0:half],
                bufA[:, half:2 * half], W["L0_ffn_b1T"], W["L0_ffn_b2"], m_A)
        layer1_recurrence()
        layer1_cross()
        mixture("L1_ffn", W["L1_ffn_Wg"], bc(W["L1_ffn_bg"][:, :], 1, NB), "probabilities", bufB[:, 0:half],
                bufB[:, half:2 * half], W["L1_ffn_b1T"], W["L1_ffn_b2"], m_B)
        layer2_attention()
        layer2_cross()
        layer2_experts()
        layer3_attention()
        layer3_cross()
        layer3_experts()

        fl.segment("out")
        fl.semaphore("stored")
        stored = D("stored", out, x[:, :].rearrange("p (b f) -> p b f", f=P), end_marks(fl, -2))
        fl.put("sync", lambda e, i: e.nop(), [stored, list(ready.values()), m_ctx, m_pad, m_A, m_B, list(m_late.values())],
               sem=False)

        block = ctx.enter_context(nc.Block())

        @block.sync
        def _(eng):
            fl.run("sync", eng)

        @block.gpsimd
        def _(eng):
            fl.run("gpsimd", eng)

        @block.scalar
        def _(eng):
            fl.run("scalar", eng)

        @block.tensor
        def _(eng):
            fl.run("tensor", eng)

        @block.vector
        def _(eng):
            fl.run("vector", eng)


def end_marks(fl, at=-1):
    n = len(fl.segments) + at
    return [(n, e, k) for e, k in fl.segments[n]["count"].items() if e in ENGINES[1:]]


def lay_out(inputs):
    a = {k: np.asarray(v) for k, v in inputs.items()}
    out = {}

    def rep(v, n=P):
        return np.broadcast_to(v.reshape(1, -1), (n, v.size))

    out["x"] = a["x"].transpose(1, 0, 2).reshape(P, T)
    out["ctxT"] = a["ctx_1024"].transpose(2, 0, 1).reshape(P, T)
    out["mask"] = a["mask_BxS2_bf0"].reshape(T)
    for n in ("Wq", "Wk", "Wv", "Wo"):
        out[f"L0_attn_{n}"] = a[f"L0_attn_{n}"]
        out[f"L0_xattn_{n}T"] = a[f"L0_xattn_{n}"].T
    for n in ("Wck", "Wcv"):
        out[f"L0_attn_{n}R"] = np.tile(a[f"L0_attn_{n}"].reshape(G0, HD, HD).transpose(1, 0, 2).reshape(HD, -1), (H, 1))
    out["L0_attn_WgR"] = np.tile(a["L0_attn_Wg"], (H, 1))
    out["L0_attn_bg"] = rep(a["L0_attn_bg"])
    out["L0_ffn_gate_w"] = a["L0_ffn_gate_w"]
    out["L0_ffn_gate_b"] = rep(a["L0_ffn_gate_b"])
    out["L1_ffn_Wg"] = a["L1_ffn_Wg"]
    out["L1_ffn_bg"] = rep(a["L1_ffn_bg"])
    for layer, w1, w2 in (("L0", "w1", "w2"), ("L1", "W1", "W2"), ("L3", "w1", "w2")):
        out[f"{layer}_ffn_{w1}"] = a[f"{layer}_ffn_{w1}"].transpose(1, 0, 2).reshape(P, NE * FF)
        w = a[f"{layer}_ffn_{w2}"].reshape(NE, FF // P, P, P)
        out[f"{layer}_ffn_{w2}"] = w.transpose(2, 0, 1, 3).reshape(P, NE * FF)
        out[f"{layer}_ffn_b1T"] = a[f"{layer}_ffn_b1"].reshape(NE * FF // P, P).T
        out[f"{layer}_ffn_b2"] = a[f"{layer}_ffn_b2"]
    out["L1_attn_WiT"] = a["L1_attn_Wi"].T
    out["L1_attn_conv_w"] = a["L1_attn_conv_w"].reshape(2, HC, KC).transpose(1, 0, 2).reshape(HC, 2 * KC)
    out["L1_attn_conv_b"] = a["L1_attn_conv_b"].reshape(2, HC).T
    out["L1_attn_WgT"] = a["L1_attn_Wg"].T.reshape(2, HC, 2 * HID).transpose(1, 0, 2).reshape(HC, 4 * HID)
    out["L1_attn_bg"] = a["L1_attn_bg"].reshape(4, HC).T
    out["L1_attn_forget_base"] = a["L1_attn_forget_base"].reshape(2, HC).T
    out["L1_attn_WoT"] = a["L1_attn_Wo"].T.reshape(2, HC, P).transpose(1, 0, 2).reshape(HC, 2 * P)
    for n in "qkv":
        wt = a[f"L1_xattn_W{n}"].T
        out[f"L1_xattn_W{n}T"] = np.concatenate([wt, wt[:, 0:24]], axis=1)
        b8 = a[f"L1_xattn_b{n}"].reshape(H, HD).T
        out[f"L1_xattn_b{n}8"] = np.tile(b8, (P // HD, 1))
    out["slopes"] = rep(alibi_slopes().reshape(NPAIR // 2, 2, 2, 2).transpose(0, 2, 1, 3))
    w = a["L2_attn_W_qkv"]
    wq = w[:, 0:QH * DH].reshape(P, NPAIR, 2, 2, DH).transpose(0, 1, 3, 2, 4).reshape(P, QH * DH)
    out["L2_attn_Wqkv"] = np.concatenate([wq, w[:, QH * DH:]], axis=1)
    out["L2_attn_Wout"] = a["L2_attn_W_out"].reshape(QH * DH // P, P, P).transpose(1, 0, 2).reshape(P, QH * DH)
    for n in ("Wq", "Wk", "Wv", "Wo"):
        out[f"L2_xattn_{n}"] = a[f"L2_xattn_{n}"]
    for n in ("bq", "bk"):
        out[f"L2_xattn_{n}"] = a[f"L2_xattn_{n}"].reshape(P, 1)
        out[f"L3_attn_{n}"] = a[f"L3_attn_{n}"].reshape(P, 1)
    out["L2_xattn_bv"] = rep(np.tile(a["L2_xattn_bv"], 4))
    out["L2_xattn_bo"] = rep(a["L2_xattn_bo"])
    gu = np.concatenate([np.concatenate([a["L2_ffn_Wg"], a["L2_ffn_Wu"]], axis=1),
                         np.concatenate([a["L2_ffn_Wg_s"], a["L2_ffn_Wu_s"]], axis=0)[None]], axis=0)
    out["L2_ffn_Wgu"] = gu.transpose(2, 0, 1).reshape(P, (NE + 1) * 2 * FI)
    wd = np.concatenate([a["L2_ffn_Wd"], a["L2_ffn_Wd_s"][None]], axis=0).transpose(0, 2, 1)
    out["L2_ffn_Wd"] = wd.reshape(NE + 1, FI // P, P, P).transpose(2, 0, 1, 3).reshape(P, (NE + 1) * FI)
    out["L2_ffn_WrT"] = a["L2_ffn_Wr"].T
    out["L2_ffn_rb"] = rep(a["L2_ffn_rb"])
    for n in ("wq", "wk", "wv", "wo"):
        out[f"L3_attn_{n}T"] = a[f"L3_attn_{n}"].T
    out["L3_attn_bqrow"] = rep(np.tile(a["L3_attn_bq"], 4))
    out["L3_attn_bv"] = rep(np.tile(a["L3_attn_bv"], 4))
    out["L3_attn_bo"] = rep(a["L3_attn_bo"])
    out["L3_xattn_W1T"] = a["L3_xattn_W"][:, 0:P].T
    out["L3_xattn_W2T"] = a["L3_xattn_W"][:, P:].T
    out["L3_xattn_b"] = rep(a["L3_xattn_b"])
    out["L3_ffn_wg_redT"] = a["L3_ffn_wg_red"].T
    out["L3_ffn_wg"] = a["L3_ffn_wg"]
    return {k: np.ascontiguousarray(v) for k, v in out.items()}


def alibi_slopes():
    base = 2.0 ** (-(2.0 ** (-(np.log2(QH) - 3))))
    return (base ** np.arange(1, QH + 1, dtype=np.float32)).astype(np.float32)


def kernel(**inputs):
    import concourse.bacc as bacc
    from concourse.bass_utils import run_bass_kernel_spmd

    arrays = lay_out(inputs)
    nc = bacc.Bacc("TRN2", target_bir_lowering=False, num_devices=1)
    d = {n: nc.dram_tensor(f"in_{n}", list(v.shape), mybir.dt.from_np(v.dtype), kind="ExternalInput").ap()
         for n, v in arrays.items()}
    out = nc.dram_tensor("out_0", [NB, P, P], F32, kind="ExternalOutput").ap()
    build_program(nc, d, out.rearrange("b t f -> t b f"))
    r = run_bass_kernel_spmd(nc, [{f"in_{n}": v for n, v in arrays.items()}], core_ids=[0])
    return r.results[0]["out_0"]
```
